# Optimizing a Trainium2 kernel written in Bass

```python
import numpy as np
import jax
import jax.numpy as jnp

def _softmax(x, axis=-1):
    return jax.nn.softmax(x, axis=axis)

def _gelu(x):
    return jax.nn.gelu(x, approximate=True)

def _silu(x):
    return jax.nn.silu(x)

def _sigmoid(x):
    return jax.nn.sigmoid(x)

def _layernorm(x, axis=-1, eps=1e-05):
    m = jnp.mean(x, axis=axis, keepdims=True)
    v = jnp.var(x, axis=axis, keepdims=True)
    return (x - m) / jnp.sqrt(v + eps)

def _scatter_add(tgt, idx, src, axis=0):
    return tgt.at[idx].add(src)

def _segment_sum(src, seg, n):
    return jax.ops.segment_sum(src, seg, n)
kernel_name = 'mk_hybrid_d1_jaxref_r8_bf7461'

def setup_inputs(seed: int=0):
    np.random.seed(seed)
    _w = jnp.asarray

    def _L0_attn_a_setup():
        import jax, jax.numpy as jnp
        import numpy as np
        EPS = 1e-06

        def _rmsnorm(x, w):
            return x * jax.lax.rsqrt(jnp.mean(x * x, axis=-1, keepdims=True) + EPS) * w

        def _short_conv_silu(x, w):
            K = w.shape[1]
            T = x.shape[1]
            xp = jnp.pad(x, ((0, 0), (K - 1, 0), (0, 0)))
            y = sum((xp[:, i:i + T, :] * w[:, i] for i in range(K)))
            return jax.nn.silu(y)

        def _l2norm(x):
            return x * jax.lax.rsqrt(jnp.sum(x * x, axis=-1, keepdims=True) + EPS)
        key = jax.random.key(seed)
        ks = jax.random.split(key, 20)
        B, T, D = (4, 256, 128)
        H, dk, dv = (8, 96, 192)
        KD, VD, I = (H * dk, H * dv, 512)
        s = 0.02
        r = lambda k, shp: jax.random.normal(k, shp, jnp.float32) * s
        return {'x': jax.random.normal(ks[0], (B, T, D), jnp.float32), 'Wq': r(ks[1], (D, KD)), 'Wk': r(ks[2], (D, KD)), 'Wv': r(ks[3], (D, VD)), 'Wb': r(ks[4], (D, H)), 'Wa': r(ks[5], (D, H)), 'A_log': jnp.log(jax.random.uniform(ks[6], (H,), jnp.float32, 1.0, 16.0)), 'dt_bias': jax.random.normal(ks[7], (H,), jnp.float32) * 0.1, 'conv_q_w': jax.random.normal(ks[8], (KD, 4), jnp.float32) * 0.2, 'conv_k_w': jax.random.normal(ks[9], (KD, 4), jnp.float32) * 0.2, 'conv_v_w': jax.random.normal(ks[10], (VD, 4), jnp.float32) * 0.2, 'Wg': r(ks[11], (D, VD)), 'onorm_w': jnp.ones((dv,), jnp.float32), 'Wo': r(ks[12], (VD, D)), 'norm1_w': jnp.ones((D,), jnp.float32), 'norm2_w': jnp.ones((D,), jnp.float32), 'Wgate': r(ks[13], (D, I)), 'Wup': r(ks[14], (D, I)), 'Wdown': r(ks[15], (I, D))}
    _L0_attn_a_in = _L0_attn_a_setup()

    def _L0_attn_b_setup():
        import jax, jax.numpy as jnp
        import numpy as np
        DIM = 128
        HEADS = 16
        HEAD_DIM = DIM // HEADS
        WINDOW = 64
        NEG = -1000000000.0

        def _sliding_window_attn(x, Wq, bq, Wk, bk, Wv, bv, Wo, bo):
            B, S, D = x.shape
            H, hd, W = (HEADS, HEAD_DIM, WINDOW)
            nb = S // W

            def proj(Wp, bp):
                y = x @ Wp.T + bp
                return y.reshape(B, S, H, hd).transpose(0, 2, 1, 3)
            q = proj(Wq, bq)
            k = proj(Wk, bk)
            v = proj(Wv, bv)
            scale = hd ** (-0.5)
            qb = q.reshape(B, H, nb, W, hd)

            def window_kv(t):
                pad = jnp.concatenate([jnp.zeros((B, H, W, hd), t.dtype), t], axis=2)
                prev = pad[:, :, :S].reshape(B, H, nb, W, hd)
                cur = t.reshape(B, H, nb, W, hd)
                return jnp.concatenate([prev, cur], axis=3)
            kw = window_kv(k)
            vw = window_kv(v)
            scores = jnp.einsum('bhnqd,bhnkd->bhnqk', qb, kw) * scale
            t = jnp.arange(2 * W)
            s_ = jnp.arange(W)[:, None]
            n = jnp.arange(nb)[:, None, None]
            valid = (t <= s_ + W) & (t >= s_ + 1) & (n * W - W + t >= 0)
            scores = jnp.where(valid, scores, NEG)
            attn = jax.nn.softmax(scores, axis=-1)
            out = jnp.einsum('bhnqk,bhnkd->bhnqd', attn, vw)
            out = out.reshape(B, H, S, hd).transpose(0, 2, 1, 3).reshape(B, S, D)
            return out @ Wo.T + bo
        key = jax.random.key(seed)
        ks = jax.random.split(key, 9)
        s = 1.0 / np.sqrt(DIM)
        inp = {'x': jax.random.normal(ks[0], (2, 512, DIM), dtype=jnp.float32)}
        for i, name in enumerate(['q', 'k', 'v', 'o']):
            inp[f'W{name}'] = jax.random.uniform(ks[1 + 2 * i], (DIM, DIM), jnp.float32, -s, s)
            inp[f'b{name}'] = jax.random.uniform(ks[2 + 2 * i], (DIM,), jnp.float32, -s, s)
        return inp
    _L0_attn_b_in = _L0_attn_b_setup()

    def _L0_ffn_setup():
        import jax, jax.numpy as jnp
        import numpy as np
        DIM = 128
        DEPTH = 2
        HEADS = 8
        DIM_HEAD = 64
        WINDOW = 64
        INNER = HEADS * DIM_HEAD
        HID = int(DIM * 4 * 2 / 3)
        B, N = (2, 1024)
        QK_SCALE = 8.0

        def shift_token(t):
            t1, t2 = jnp.split(t, 2, axis=-1)
            t2 = jnp.pad(t2, ((0, 0), (1, 0), (0, 0)))[:, :-1]
            return jnp.concatenate([t1, t2], axis=-1)

        def l2norm(t):
            return t / jnp.clip(jnp.linalg.norm(t, axis=-1, keepdims=True), 1e-12)

        def rotate_half(x):
            x1, x2 = jnp.split(x, 2, axis=-1)
            return jnp.concatenate([-x2, x1], axis=-1)

        def rotary_xpos(q, k):
            n = q.shape[-2]
            half_idx = jnp.arange(0, DIM_HEAD, 2, dtype=jnp.float32)
            inv_freq = 1.0 / 10000.0 ** (half_idx / DIM_HEAD)
            t = jnp.arange(n, dtype=jnp.float32)
            freqs = t[:, None] * inv_freq[None, :]
            freqs = jnp.concatenate([freqs, freqs], axis=-1)
            base = (half_idx + 0.4 * DIM_HEAD) / (1.4 * DIM_HEAD)
            power = (t - n // 2) / float(WINDOW // 2)
            scale = base[None, :] ** power[:, None]
            scale = jnp.concatenate([scale, scale], axis=-1)
            cos, sin = (jnp.cos(freqs), jnp.sin(freqs))
            q = q * cos * scale + rotate_half(q) * sin * scale
            k = k * cos / scale + rotate_half(k) * sin / scale
            return (q, k)

        def local_attention(q, k, v):
            b, h, n, d = q.shape
            w = n // WINDOW
            bq = q.reshape(b, h, w, WINDOW, d) * QK_SCALE
            bk = k.reshape(b, h, w, WINDOW, d)
            bv = v.reshape(b, h, w, WINDOW, d)

            def look_around(t):
                p = jnp.pad(t, ((0, 0), (0, 0), (1, 0), (0, 0), (0, 0)))
                return jnp.concatenate([p[:, :, :w], p[:, :, 1:]], axis=3)
            bk, bv = (look_around(bk), look_around(bv))
            bt = jnp.arange(n).reshape(w, WINDOW)
            btp = jnp.pad(bt, ((1, 0), (0, 0)), constant_values=-1)
            btk = jnp.concatenate([btp[:w], btp[1:]], axis=1)
            sim = jnp.einsum('bhwid,bhwjd->bhwij', bq, bk)
            i = bt[:, :, None]
            j = btk[:, None, :]
            mask = (i < j) | (i > j + WINDOW) | (j == -1)
            sim = jnp.where(mask, -jnp.finfo(sim.dtype).max, sim)
            attn = jax.nn.softmax(sim, axis=-1)
            out = jnp.einsum('bhwij,bhwjd->bhwid', attn, bv)
            return out.reshape(b, h, n, d)

        def _layer(x, wqkv, qs, ksc, wo, lg, lb, w1, b1, w2, b2):
            b, n, _ = x.shape
            h = shift_token(x)
            qkv = h @ wqkv
            q, k, v = jnp.split(qkv, 3, axis=-1)
            to_heads = lambda t: t.reshape(b, n, HEADS, DIM_HEAD).transpose(0, 2, 1, 3)
            q, k, v = (to_heads(q), to_heads(k), to_heads(v))
            q = l2norm(q) * qs
            k = l2norm(k) * ksc
            q, k = rotary_xpos(q, k)
            o = local_attention(q, k, v)
            o = o.transpose(0, 2, 1, 3).reshape(b, n, INNER)
            x = x + o @ wo
            h = shift_token(x)
            mu = h.mean(-1, keepdims=True)
            var = h.var(-1, keepdims=True)
            h = (h - mu) / jnp.sqrt(var + 1e-05) * lg + lb
            h = h @ w1 + b1
            a, g = jnp.split(h, 2, axis=-1)
            h = a * jax.nn.gelu(g, approximate=False)
            x = x + h @ w2 + b2
            return x
        key = jax.random.key(seed)
        ks = jax.random.split(key, 6)
        return {'x': jax.random.normal(ks[0], (B, N, DIM), jnp.float32), 'wqkv': jax.random.normal(ks[1], (DEPTH, DIM, 3 * INNER), jnp.float32) * 0.02, 'q_scale': jnp.ones((DEPTH, DIM_HEAD), jnp.float32), 'k_scale': jnp.ones((DEPTH, DIM_HEAD), jnp.float32), 'wo': jax.random.normal(ks[2], (DEPTH, INNER, DIM), jnp.float32) * 0.02, 'ln_g': jnp.ones((DEPTH, DIM), jnp.float32), 'ln_b': jnp.zeros((DEPTH, DIM), jnp.float32), 'w1': jax.random.normal(ks[3], (DEPTH, DIM, 2 * HID), jnp.float32) * 0.02, 'b1': jnp.zeros((DEPTH, 2 * HID), jnp.float32), 'w2': jax.random.normal(ks[4], (DEPTH, HID, DIM), jnp.float32) * 0.02, 'b2': jnp.zeros((DEPTH, DIM), jnp.float32)}
    _L0_ffn_in = _L0_ffn_setup()
    _d = {'L0_attn_a_x': _L0_attn_a_in['x'], 'L0_attn_a_Wq': _L0_attn_a_in['Wq'], 'L0_attn_a_Wk': _L0_attn_a_in['Wk'], 'L0_attn_a_Wv': _L0_attn_a_in['Wv'], 'L0_attn_a_Wb': _L0_attn_a_in['Wb'], 'L0_attn_a_Wa': _L0_attn_a_in['Wa'], 'L0_attn_a_A_log': _L0_attn_a_in['A_log'], 'L0_attn_a_dt_bias': _L0_attn_a_in['dt_bias'], 'L0_attn_a_conv_q_w': _L0_attn_a_in['conv_q_w'], 'L0_attn_a_conv_k_w': _L0_attn_a_in['conv_k_w'], 'L0_attn_a_conv_v_w': _L0_attn_a_in['conv_v_w'], 'L0_attn_a_Wg': _L0_attn_a_in['Wg'], 'L0_attn_a_onorm_w': _L0_attn_a_in['onorm_w'], 'L0_attn_a_Wo': _L0_attn_a_in['Wo'], 'L0_attn_a_norm1_w': _L0_attn_a_in['norm1_w'], 'L0_attn_a_norm2_w': _L0_attn_a_in['norm2_w'], 'L0_attn_a_Wgate': _L0_attn_a_in['Wgate'], 'L0_attn_a_Wup': _L0_attn_a_in['Wup'], 'L0_attn_a_Wdown': _L0_attn_a_in['Wdown'], 'L0_attn_b_Wq': _L0_attn_b_in['Wq'], 'L0_attn_b_bq': _L0_attn_b_in['bq'], 'L0_attn_b_Wk': _L0_attn_b_in['Wk'], 'L0_attn_b_bk': _L0_attn_b_in['bk'], 'L0_attn_b_Wv': _L0_attn_b_in['Wv'], 'L0_attn_b_bv': _L0_attn_b_in['bv'], 'L0_attn_b_Wo': _L0_attn_b_in['Wo'], 'L0_attn_b_bo': _L0_attn_b_in['bo'], 'L0_ffn_wqkv': _L0_ffn_in['wqkv'], 'L0_ffn_q_scale': _L0_ffn_in['q_scale'], 'L0_ffn_k_scale': _L0_ffn_in['k_scale'], 'L0_ffn_wo': _L0_ffn_in['wo'], 'L0_ffn_ln_g': _L0_ffn_in['ln_g'], 'L0_ffn_ln_b': _L0_ffn_in['ln_b'], 'L0_ffn_w1': _L0_ffn_in['w1'], 'L0_ffn_b1': _L0_ffn_in['b1'], 'L0_ffn_w2': _L0_ffn_in['w2'], 'L0_ffn_b2': _L0_ffn_in['b2']}
    _x0 = _d['L0_attn_a_x']
    _d['L0_attn_a_x'] = jax.random.normal(jax.random.fold_in(jax.random.key(seed), 1), (4, 1024, 128), dtype=_x0.dtype)
    del _x0
    return _d

def reference(L0_attn_a_x, L0_attn_a_Wq, L0_attn_a_Wk, L0_attn_a_Wv, L0_attn_a_Wb, L0_attn_a_Wa, L0_attn_a_A_log, L0_attn_a_dt_bias, L0_attn_a_conv_q_w, L0_attn_a_conv_k_w, L0_attn_a_conv_v_w, L0_attn_a_Wg, L0_attn_a_onorm_w, L0_attn_a_Wo, L0_attn_a_norm1_w, L0_attn_a_norm2_w, L0_attn_a_Wgate, L0_attn_a_Wup, L0_attn_a_Wdown, L0_attn_b_Wq, L0_attn_b_bq, L0_attn_b_Wk, L0_attn_b_bk, L0_attn_b_Wv, L0_attn_b_bv, L0_attn_b_Wo, L0_attn_b_bo, L0_ffn_wqkv, L0_ffn_q_scale, L0_ffn_k_scale, L0_ffn_wo, L0_ffn_ln_g, L0_ffn_ln_b, L0_ffn_w1, L0_ffn_b1, L0_ffn_w2, L0_ffn_b2):

    def _L0_attn_a_ref(x, Wq, Wk, Wv, Wb, Wa, A_log, dt_bias, conv_q_w, conv_k_w, conv_v_w, Wg, onorm_w, Wo, norm1_w, norm2_w, Wgate, Wup, Wdown):
        import jax, jax.numpy as jnp
        import numpy as np
        EPS = 1e-06

        def _rmsnorm(x, w):
            return x * jax.lax.rsqrt(jnp.mean(x * x, axis=-1, keepdims=True) + EPS) * w

        def _short_conv_silu(x, w):
            K = w.shape[1]
            T = x.shape[1]
            xp = jnp.pad(x, ((0, 0), (K - 1, 0), (0, 0)))
            y = sum((xp[:, i:i + T, :] * w[:, i] for i in range(K)))
            return jax.nn.silu(y)

        def _l2norm(x):
            return x * jax.lax.rsqrt(jnp.sum(x * x, axis=-1, keepdims=True) + EPS)
        B, T, D = x.shape
        H = A_log.shape[0]
        dk = Wq.shape[1] // H
        dv = Wv.shape[1] // H
        scale = dk ** (-0.5)
        h = _rmsnorm(x, norm1_w)
        q = _short_conv_silu(h @ Wq, conv_q_w).reshape(B, T, H, dk)
        k = _short_conv_silu(h @ Wk, conv_k_w).reshape(B, T, H, dk)
        v = _short_conv_silu(h @ Wv, conv_v_w).reshape(B, T, H, dv)
        q = _l2norm(q) * scale
        k = _l2norm(k)
        beta = jax.nn.sigmoid(h @ Wb)
        g = -jnp.exp(A_log) * jax.nn.softplus(h @ Wa + dt_bias)

        def step(S, inp):
            q_t, k_t, v_t, g_t, b_t = inp
            S = S * jnp.exp(g_t)[..., None, None]
            v_old = jnp.einsum('bhk,bhkv->bhv', k_t, S)
            delta = (v_t - v_old) * b_t[..., None]
            S = S + jnp.einsum('bhk,bhv->bhkv', k_t, delta)
            o_t = jnp.einsum('bhk,bhkv->bhv', q_t, S)
            return (S, o_t)
        S0 = jnp.zeros((B, H, dk, dv), x.dtype)
        xs = (jnp.moveaxis(q, 1, 0), jnp.moveaxis(k, 1, 0), jnp.moveaxis(v, 1, 0), jnp.moveaxis(g, 1, 0), jnp.moveaxis(beta, 1, 0))
        _, o = jax.lax.scan(step, S0, xs)
        o = jnp.moveaxis(o, 0, 1)
        g_out = (h @ Wg).reshape(B, T, H, dv)
        o = _rmsnorm(o, onorm_w) * jax.nn.silu(g_out)
        x = x + o.reshape(B, T, H * dv) @ Wo
        h2 = _rmsnorm(x, norm2_w)
        mlp = jax.nn.silu(h2 @ Wgate) * (h2 @ Wup) @ Wdown
        return x + mlp

    def _L0_attn_b_ref(x, Wq, bq, Wk, bk, Wv, bv, Wo, bo):
        import jax, jax.numpy as jnp
        import numpy as np
        DIM = 128
        HEADS = 16
        HEAD_DIM = DIM // HEADS
        WINDOW = 64
        NEG = -1000000000.0

        def _sliding_window_attn(x, Wq, bq, Wk, bk, Wv, bv, Wo, bo):
            B, S, D = x.shape
            H, hd, W = (HEADS, HEAD_DIM, WINDOW)
            nb = S // W

            def proj(Wp, bp):
                y = x @ Wp.T + bp
                return y.reshape(B, S, H, hd).transpose(0, 2, 1, 3)
            q = proj(Wq, bq)
            k = proj(Wk, bk)
            v = proj(Wv, bv)
            scale = hd ** (-0.5)
            qb = q.reshape(B, H, nb, W, hd)

            def window_kv(t):
                pad = jnp.concatenate([jnp.zeros((B, H, W, hd), t.dtype), t], axis=2)
                prev = pad[:, :, :S].reshape(B, H, nb, W, hd)
                cur = t.reshape(B, H, nb, W, hd)
                return jnp.concatenate([prev, cur], axis=3)
            kw = window_kv(k)
            vw = window_kv(v)
            scores = jnp.einsum('bhnqd,bhnkd->bhnqk', qb, kw) * scale
            t = jnp.arange(2 * W)
            s_ = jnp.arange(W)[:, None]
            n = jnp.arange(nb)[:, None, None]
            valid = (t <= s_ + W) & (t >= s_ + 1) & (n * W - W + t >= 0)
            scores = jnp.where(valid, scores, NEG)
            attn = jax.nn.softmax(scores, axis=-1)
            out = jnp.einsum('bhnqk,bhnkd->bhnqd', attn, vw)
            out = out.reshape(B, H, S, hd).transpose(0, 2, 1, 3).reshape(B, S, D)
            return out @ Wo.T + bo
        return _sliding_window_attn(x, Wq, bq, Wk, bk, Wv, bv, Wo, bo)

    def _L0_ffn_ref(x, wqkv, q_scale, k_scale, wo, ln_g, ln_b, w1, b1, w2, b2):
        import jax, jax.numpy as jnp
        import numpy as np
        DIM = 128
        DEPTH = 2
        HEADS = 8
        DIM_HEAD = 64
        WINDOW = 64
        INNER = HEADS * DIM_HEAD
        HID = int(DIM * 4 * 2 / 3)
        B, N = (2, 1024)
        QK_SCALE = 8.0

        def shift_token(t):
            t1, t2 = jnp.split(t, 2, axis=-1)
            t2 = jnp.pad(t2, ((0, 0), (1, 0), (0, 0)))[:, :-1]
            return jnp.concatenate([t1, t2], axis=-1)

        def l2norm(t):
            return t / jnp.clip(jnp.linalg.norm(t, axis=-1, keepdims=True), 1e-12)

        def rotate_half(x):
            x1, x2 = jnp.split(x, 2, axis=-1)
            return jnp.concatenate([-x2, x1], axis=-1)

        def rotary_xpos(q, k):
            n = q.shape[-2]
            half_idx = jnp.arange(0, DIM_HEAD, 2, dtype=jnp.float32)
            inv_freq = 1.0 / 10000.0 ** (half_idx / DIM_HEAD)
            t = jnp.arange(n, dtype=jnp.float32)
            freqs = t[:, None] * inv_freq[None, :]
            freqs = jnp.concatenate([freqs, freqs], axis=-1)
            base = (half_idx + 0.4 * DIM_HEAD) / (1.4 * DIM_HEAD)
            power = (t - n // 2) / float(WINDOW // 2)
            scale = base[None, :] ** power[:, None]
            scale = jnp.concatenate([scale, scale], axis=-1)
            cos, sin = (jnp.cos(freqs), jnp.sin(freqs))
            q = q * cos * scale + rotate_half(q) * sin * scale
            k = k * cos / scale + rotate_half(k) * sin / scale
            return (q, k)

        def local_attention(q, k, v):
            b, h, n, d = q.shape
            w = n // WINDOW
            bq = q.reshape(b, h, w, WINDOW, d) * QK_SCALE
            bk = k.reshape(b, h, w, WINDOW, d)
            bv = v.reshape(b, h, w, WINDOW, d)

            def look_around(t):
                p = jnp.pad(t, ((0, 0), (0, 0), (1, 0), (0, 0), (0, 0)))
                return jnp.concatenate([p[:, :, :w], p[:, :, 1:]], axis=3)
            bk, bv = (look_around(bk), look_around(bv))
            bt = jnp.arange(n).reshape(w, WINDOW)
            btp = jnp.pad(bt, ((1, 0), (0, 0)), constant_values=-1)
            btk = jnp.concatenate([btp[:w], btp[1:]], axis=1)
            sim = jnp.einsum('bhwid,bhwjd->bhwij', bq, bk)
            i = bt[:, :, None]
            j = btk[:, None, :]
            mask = (i < j) | (i > j + WINDOW) | (j == -1)
            sim = jnp.where(mask, -jnp.finfo(sim.dtype).max, sim)
            attn = jax.nn.softmax(sim, axis=-1)
            out = jnp.einsum('bhwij,bhwjd->bhwid', attn, bv)
            return out.reshape(b, h, n, d)

        def _layer(x, wqkv, qs, ksc, wo, lg, lb, w1, b1, w2, b2):
            b, n, _ = x.shape
            h = shift_token(x)
            qkv = h @ wqkv
            q, k, v = jnp.split(qkv, 3, axis=-1)
            to_heads = lambda t: t.reshape(b, n, HEADS, DIM_HEAD).transpose(0, 2, 1, 3)
            q, k, v = (to_heads(q), to_heads(k), to_heads(v))
            q = l2norm(q) * qs
            k = l2norm(k) * ksc
            q, k = rotary_xpos(q, k)
            o = local_attention(q, k, v)
            o = o.transpose(0, 2, 1, 3).reshape(b, n, INNER)
            x = x + o @ wo
            h = shift_token(x)
            mu = h.mean(-1, keepdims=True)
            var = h.var(-1, keepdims=True)
            h = (h - mu) / jnp.sqrt(var + 1e-05) * lg + lb
            h = h @ w1 + b1
            a, g = jnp.split(h, 2, axis=-1)
            h = a * jax.nn.gelu(g, approximate=False)
            x = x + h @ w2 + b2
            return x
        for l in range(DEPTH):
            x = _layer(x, wqkv[l], q_scale[l], k_scale[l], wo[l], ln_g[l], ln_b[l], w1[l], b1[l], w2[l], b2[l])
        return x
    x = L0_attn_a_x
    x = x + _L0_attn_a_ref(_layernorm(x, axis=-1), L0_attn_a_Wq, L0_attn_a_Wk, L0_attn_a_Wv, L0_attn_a_Wb, L0_attn_a_Wa, L0_attn_a_A_log, L0_attn_a_dt_bias, L0_attn_a_conv_q_w, L0_attn_a_conv_k_w, L0_attn_a_conv_v_w, L0_attn_a_Wg, L0_attn_a_onorm_w, L0_attn_a_Wo, L0_attn_a_norm1_w, L0_attn_a_norm2_w, L0_attn_a_Wgate, L0_attn_a_Wup, L0_attn_a_Wdown)
    x = x + _L0_ffn_ref(_layernorm(x, axis=-1), L0_ffn_wqkv, L0_ffn_q_scale, L0_ffn_k_scale, L0_ffn_wo, L0_ffn_ln_g, L0_ffn_ln_b, L0_ffn_w1, L0_ffn_b1, L0_ffn_w2, L0_ffn_b2)
    x = x + _L0_attn_b_ref(_layernorm(x, axis=-1), L0_attn_b_Wq, L0_attn_b_bq, L0_attn_b_Wk, L0_attn_b_bk, L0_attn_b_Wv, L0_attn_b_bv, L0_attn_b_Wo, L0_attn_b_bo)
    x = x + _L0_ffn_ref(_layernorm(x, axis=-1), L0_ffn_wqkv, L0_ffn_q_scale, L0_ffn_k_scale, L0_ffn_wo, L0_ffn_ln_g, L0_ffn_ln_b, L0_ffn_w1, L0_ffn_b1, L0_ffn_w2, L0_ffn_b2)
    return x

_drawn_inputs = setup_inputs


def setup_inputs(seed=0):
    import zlib

    import numpy as np

    out = dict(_drawn_inputs(seed))
    spreads = {'L0_attn_a_onorm_w': (1.0, 0.6),
     'L0_attn_a_norm1_w': (1.0, 0.6),
     'L0_attn_a_norm2_w': (1.0, 0.6),
     'L0_ffn_q_scale': (1.0, 0.6),
     'L0_ffn_k_scale': (1.0, 0.6),
     'L0_ffn_ln_g': (1.0, 0.6),
     'L0_ffn_ln_b': (0.0, 0.8),
     'L0_ffn_b1': (0.0, 0.8),
     'L0_ffn_b2': (0.0, 0.33)}
    factors = {'L0_attn_a_Wq': 5.228,
     'L0_attn_a_Wk': 5.245,
     'L0_attn_a_Wv': 5.234,
     'L0_attn_a_Wb': 8.0,
     'L0_attn_a_Wa': 8.0,
     'L0_attn_a_A_log': 8.0,
     'L0_attn_a_dt_bias': 32.841,
     'L0_attn_a_conv_q_w': 5.241,
     'L0_attn_a_conv_k_w': 5.083,
     'L0_attn_a_conv_v_w': 5.265,
     'L0_attn_a_Wg': 5.24,
     'L0_attn_a_Wo': 5.205,
     'L0_attn_a_Wgate': 8.0,
     'L0_attn_a_Wup': 8.0,
     'L0_attn_a_Wdown': 8.0,
     'L0_attn_b_Wq': 8.0,
     'L0_attn_b_bq': 8.0,
     'L0_attn_b_Wk': 8.0,
     'L0_attn_b_bk': 64.0,
     'L0_attn_b_Wv': 3.418,
     'L0_attn_b_bv': 5.504,
     'L0_attn_b_Wo': 2.96,
     'L0_attn_b_bo': 13.616,
     'L0_ffn_wqkv': 3.363,
     'L0_ffn_wo': 3.327,
     'L0_ffn_w1': 5.297,
     'L0_ffn_w2': 5.219}
    for name, (base, spread) in spreads.items():
        noise = np.random.default_rng([zlib.crc32(name.encode()), seed]).standard_normal(out[name].shape)
        drawn = base * np.exp(spread * noise) if base else spread * noise
        out[name] = jnp.asarray(drawn.astype(out[name].dtype))
    for name, factor in factors.items():
        out[name] = (out[name] * factor).astype(out[name].dtype)
    return out
```

```python
from contextlib import ExitStack, contextmanager

import concourse.bass as bass
from concourse import mybir

F32 = mybir.dt.float32
BF16 = mybir.dt.bfloat16
ALU = mybir.AluOpType
ACT = mybir.ActivationFunctionType
AX = mybir.AxisListType

P = 128
NB, T, D = 4, 1024, 128
GT = 4
G = GT * P
NG = T // G
TURNS = NB * NG
PAD = P
ROWS = PAD + T
DEPTH = 2


class Signal:

    def __init__(self, sem, per):
        self.sem = sem
        self.per = per

    def at(self, n, k):
        return self.sem, n * self.per + k


class Phase:

    def __init__(self, nc, name):
        self.nc, self.name, self.stack, self.counters, self.sems = nc, name, ExitStack(), [], []

    def sb(self, name, shape, dt=F32):
        return self.stack.enter_context(self.nc.sbuf_tensor(f"{self.name}_{name}", shape, dt))

    def banks(self):
        return self.stack.enter_context(self.nc.psum_tensor(f"{self.name}_ps", [P, 8, 512], F32))

    def semaphore(self, name):
        self.sems.append(self.stack.enter_context(self.nc.semaphore(f"{self.name}_{name}")))
        return self.sems[-1]

    def counter(self, name, per, owner):
        s = Signal(self.semaphore(name), per)
        self.counters.append((s, owner))
        return s

    def start(self, eng, owner):
        for s, o in self.counters:
            if o == owner:
                eng.sem_inc(s.sem, s.per)

    def close(self):
        for sem in self.sems:
            self.nc.gpsimd.sem_clear(sem)
        self.nc.all_engine_barrier()
        self.stack.close()


def freed(i, slots, total):
    if i >= slots:
        return i - slots + 1
    return max(j for j in range(total) if j % slots == i % slots) + 1 - total


def scratch_row(b, g):
    return b * ROWS + PAD + g * G


def tiles(rows):
    return rows.rearrange("(n p) c -> p n c", p=P)


def local_attention(nc, name, src, dst, l, w, c):
    H, DH, W = 8, 64, 64
    INNER = H * DH
    KEYS = W + P
    PAIRS = H // 2
    ph = Phase(nc, name)
    sb, signal = ph.sb, ph.counter
    ps = ph.banks()
    wqkv = sb("wqkv", [P, 3 * INNER])
    wo = sb("wo", [P, 4, D])
    ident = sb("ident", [P, P])
    identb = sb("identb", [P, P], BF16)
    mask = sb("mask", [P, 2, 2, KEYS])
    maskb = sb("maskb", [P, 2, 2, KEYS], BF16)
    scales = sb("scales", [P, 4, DH])
    table = sb("table", [P, 4, T // P, DH])
    h = sb("h", [P, GT, D])
    x = sb("x", [P, GT, D])
    y = sb("y", [P, GT, D])
    ht = sb("ht", [P, G])
    sq = sb("sq", [P, 2, H, DH])
    ss = sb("ss", [P, 2, 2 * H])
    minus_half = sb("minus_half", [P, 2 * H])
    rn = sb("rn", [P, 2 * H])
    rot_c = sb("rot_c", [P, 2, H, DH])
    rot_s = sb("rot_s", [P, 2, H, DH])
    rot = sb("rot", [P, 2, H, DH])
    qk = sb("qk", [P, 2 * H, DH])
    qt = sb("qt", [P, PAIRS, P])
    kt = sb("kt", [P, PAIRS, W + G])
    v = sb("v", [P, 1 + GT, H, DH + 1])
    nmx = sb("nmx", [P, H])
    pr = sb("pr", [P, H, 2 * P])
    pt = sb("pt", [P, H, 2, P])
    rs = sb("rs", [P, H])
    o = sb("o", [P, H, DH])
    ot = sb("ot", [P, 4, P])

    wts_loaded = ph.semaphore("wts_loaded")
    prepared = ph.semaphore("prepared")
    h_loaded = signal("h_loaded", 32, "sp")
    x_loaded = signal("x_loaded", 16, "sp")
    stored = signal("stored", 16, "sp")
    ht_ps = signal("ht_ps", 1, "pe")
    ht_sb = signal("ht_sb", 1, "act")
    qkv_ps = signal("qkv_ps", GT, "pe")
    squared = signal("squared", GT, "act")
    v_sb = signal("v_sb", GT, "act")
    norm2 = signal("norm2", GT, "dve")
    clipped = signal("clipped", GT, "dve")
    rnorm = signal("rnorm", GT, "pool")
    rot_terms = signal("rot_terms", GT, "dve")
    rotated = signal("rotated", GT, "pool")
    qk_unit = signal("qk_unit", GT, "pool")
    qkt_ps = signal("qkt_ps", 2 * GT, "pe")
    qkt_sb = signal("qkt_sb", 2 * GT, "act")
    s_ps = signal("s_ps", PAIRS * GT, "pe")
    negmax = signal("negmax", PAIRS * GT, "dve")
    p_sb = signal("p_sb", PAIRS * GT, "act")
    pt_ps = signal("pt_ps", PAIRS * GT, "pe")
    pt_sb = [signal("pt_sb_dve", 2 * GT, "dve"), signal("pt_sb_act", 2 * GT, "act")]
    o_ps = signal("o_ps", GT, "pe")
    rsum = signal("rsum", GT, "dve")
    o_sb = signal("o_sb", GT, "dve")
    ot_ps = signal("ot_ps", GT, "pe")
    ot_sb = signal("ot_sb", GT, "act")
    y_ps = signal("y_ps", GT, "pe")
    y_sb = signal("y_sb", GT, "dve")
    halo = signal("halo", 2, "dve")

    WTS = 16 * 12
    QKV, QKT, SP_, OPS, OTB, YB = (0, 1, 2), (2, 3), (4, 5, 6, 7), (0, 1), 4, 5

    def head(i, s):
        return 4 * (i // 2) + i % 2 + 2 * s

    with nc.Block() as block:

        @block.sync
        def _(sp):
            ph.start(sp, "sp")
            sp.dma_start(wqkv[:], w["wqkv"][bass.ds(l * D, D), :]).then_inc(wts_loaded, 16)
            sp.dma_start(wo[:], tiles(w["wo"][bass.ds(l * INNER, INNER), :])).then_inc(wts_loaded, 16)
            sp.dma_start(ident[:], c["ident"]).then_inc(wts_loaded, 16)
            sp.dma_start(mask[:], c["ffn_mask"].rearrange("p (e h k) -> p e h k", e=2, h=2)).then_inc(wts_loaded, 16)
            sp.dma_start(table[:], c["rotation"].rearrange("p (r n i) -> p r n i", r=4, i=DH)).then_inc(wts_loaded, 16)
            sp.dma_start(minus_half[:], c["minus_half"][:, 0:2 * H]).then_inc(wts_loaded, 16)
            for n, scale in enumerate((w["q_scale"], w["k_scale"])):
                sp.dma_start(scales[:, 2 * n, :], scale[bass.ds(l, 1), :].to_broadcast([P, DH])).then_inc(wts_loaded, 16)
                for s in range(2):
                    sp.dma_start(scales[:, 2 * n + 1, 32 * s:32 * s + 32],
                                 scale[bass.ds(l, 1), 32 - 32 * s:64 - 32 * s].to_broadcast([P, 32]))\
                        .then_inc(wts_loaded, 16)
            with sp.Fori(0, NB) as b, sp.Fori(0, NG) as g:
                n = sp.snap(b * NG + g + 1)
                row = sp.snap(scratch_row(b, g))
                sp.wait_ge(*ht_ps.at(n, 0))
                sp.dma_start(h[:, :, 0:D // 2], tiles(src[bass.ds(row, G), 0:D // 2])).then_inc(h_loaded.sem, 16)
                sp.dma_start(h[:, :, D // 2:D], tiles(src[bass.ds(row - 1, G), D // 2:D])).then_inc(h_loaded.sem, 16)
                sp.wait_ge(*y_sb.at(n, 0))
                sp.dma_start(x[:], tiles(src[bass.ds(row, G), :])).then_inc(x_loaded.sem, 16)
                sp.wait_ge(*y_sb.at(n, GT))
                sp.dma_start(tiles(dst[bass.ds(row, G), :]), y[:]).then_inc(stored.sem, 16)
            sp.wait_ge(*stored.at(TURNS + 1, 0))

        @block.gpsimd
        def _(pool):
            ph.start(pool, "pool")
            pool.memset(kt[:, :, 0:W], 0.0).then_inc(prepared, 1)
            pool.memset(v[:, 0, :, :], 0.0).then_inc(prepared, 1)
            pool.memset(v[:, 1:, :, DH:], 1.0).then_inc(prepared, 1)
            pool.memset(pr[:, :, 0:P - W], 0.0).then_inc(prepared, 1)
            pool.wait_ge(wts_loaded, WTS)
            with pool.Fori(0, NB) as b, pool.Fori(0, NG) as g:
                n = pool.snap(b * NG + g + 1)

                def rotate(t):
                    pool.wait_ge(*clipped.at(n, t + 1))
                    pool.wait_ge(*qk_unit.at(n, t))
                    pool.tensor_tensor(rn[:], ss[:, 1, :], minus_half[:], ALU.pow).then_inc(rnorm.sem, 1)
                    pool.wait_ge(*rot_terms.at(n, t + 1))
                    pool.tensor_tensor(rot[:], rot_c[:], rot_s[:], ALU.add).then_inc(rotated.sem, 1)
                    pool.wait_ge(*rotated.at(n, t + 1))
                    pool.wait_ge(*rnorm.at(n, t + 1))
                    pool.wait_ge(*qkt_ps.at(n, 2 * t))
                    pool.tensor_tensor(qk[:], rot[:].rearrange("p r h i -> p (r h) i"),
                                       rn[:].unsqueeze(2).to_broadcast([P, 2 * H, DH]), ALU.mult).then_inc(qk_unit.sem, 1)

                for t in range(GT):
                    rotate(t)

        @block.tensor
        def _(pe):
            ph.start(pe, "pe")
            pe.wait_ge(wts_loaded, WTS)
            pe.wait_ge(prepared, 6 + 4)
            with pe.Fori(0, NB) as b, pe.Fori(0, NG) as g:
                n = pe.snap(b * NG + g + 1)

                def transpose_h():
                    pe.wait_ge(*h_loaded.at(n, 32))
                    pe.wait_ge(*qkt_sb.at(n, 0))
                    for t in range(GT):
                        mm = pe.transpose(ps[:, 3, t * P:(t + 1) * P], h[:, t, :], ident[:])
                    mm.then_inc(ht_ps.sem, 1)

                def project(t):
                    if t == 0:
                        pe.wait_ge(*ht_sb.at(n, 1))
                    pe.wait_ge(*o_sb.at(n, t - 1))
                    pe.wait_ge(*qkt_sb.at(n, 2 * t))
                    for j in QKV:
                        mm = pe.matmul(ps[:, j, :], ht[:, t * P:(t + 1) * P], wqkv[:, j * INNER:(j + 1) * INNER],
                                       start=True, stop=True)
                    mm.then_inc(qkv_ps.sem, 1)

                def transpose_qk(t):
                    pe.wait_ge(*qk_unit.at(n, t + 1))
                    for j in range(2):
                        if j == 0:
                            pe.wait_ge(*v_sb.at(n, t + 1))
                        else:
                            pe.wait_ge(*qkt_sb.at(n, 2 * t))
                            pe.wait_ge(*ht_sb.at(n, 1))
                        for i in range(4):
                            mm = pe.transpose(ps[:, QKT[j], i * P:(i + 1) * P],
                                              qk[:, 8 * j + 2 * i:8 * j + 2 * i + 2, :], ident[:])
                        mm.then_inc(qkt_ps.sem, 1)

                def scores(t):
                    for i in range(PAIRS):
                        pe.wait_ge(*pt_sb[i % 2].at(n, 2 * t))
                        if i == 0:
                            pe.wait_ge(*pt_sb[1].at(n, 2 * t))
                            pe.wait_ge(*ot_sb.at(n, t))
                            pe.wait_ge(*qkt_sb.at(n, 2 * t + 2))
                            pe.wait_ge(*halo.at(n, 0))
                        if i == 1:
                            pe.wait_ge(*y_sb.at(n, t))
                        out = ps[:, SP_[i], 0:2 * KEYS]
                        if t == 0:
                            m = maskb[:, bass.ds(g, 1), :, :].rearrange("p e h k -> p (e h k)")
                        else:
                            m = maskb[:, 1, :, :].rearrange("p h k -> p (h k)")
                        pe.matmul(out, identb[:], m, start=True, stop=False, skip_group_check=True)
                        for s in range(2):
                            half, pair = 64 * (i % 2), head(i, s) // 2
                            mm = pe.matmul(ps[:, SP_[i], s * KEYS:(s + 1) * KEYS], qt[half:half + 64, pair, :],
                                           kt[half:half + 64, pair, t * P:t * P + KEYS],
                                           start=False, stop=s == 1, skip_group_check=True)
                        mm.then_inc(s_ps.sem, 1)

                def transpose_p(t):
                    for i in range(PAIRS):
                        pe.wait_ge(*p_sb.at(n, PAIRS * t + i + 1))
                        for s in range(2):
                            for k in range(2):
                                mm = pe.transpose(ps[:, SP_[i], (2 * s + k) * P:(2 * s + k + 1) * P],
                                                  pr[:, 2 * i + s, k * P:(k + 1) * P], ident[:])
                        mm.then_inc(pt_ps.sem, 1)

                def attend(t):
                    if t < GT - 1:
                        pe.wait_ge(*rot_terms.at(n, t + 2))
                    if t == 0:
                        pe.wait_ge(*halo.at(n, 0))
                    for i in range(PAIRS):
                        pe.wait_ge(*pt_sb[i % 2].at(n, 2 * t + i // 2 + 1))
                        for s in range(2):
                            j = head(i, s)
                            out = ps[:, OPS[j // 4], (j % 4) * (DH + 1):(j % 4 + 1) * (DH + 1)]
                            for k in range(2):
                                mm = pe.matmul(out, pt[:, 2 * i + s, k, :], v[:, t + k, j, :], start=k == 0, stop=k == 1)
                    mm.then_inc(o_ps.sem, 1)

                def finish(t):
                    pe.wait_ge(*o_sb.at(n, t + 1))
                    pe.wait_ge(*pt_sb[0].at(n, 2 * t + 2))
                    for i in range(4):
                        mm = pe.transpose(ps[:, OTB, i * P:(i + 1) * P], o[:, 2 * i:2 * i + 2, :], ident[:])
                    mm.then_inc(ot_ps.sem, 1)
                    pe.wait_ge(*ot_sb.at(n, t + 1))
                    pe.wait_ge(*pt_sb[1].at(n, 2 * t + 2))
                    for i in range(4):
                        mm = pe.matmul(ps[:, YB, 0:D], ot[:, i, :], wo[:, i, :], start=i == 0, stop=i == 3)
                    mm.then_inc(y_ps.sem, 1)

                transpose_h()
                project(0)
                transpose_qk(0)
                for t in range(GT):
                    scores(t)
                    if t + 1 < GT:
                        project(t + 1)
                    transpose_p(t)
                    attend(t)
                    if t + 1 < GT:
                        transpose_qk(t + 1)
                    finish(t)

        @block.scalar
        def _(act):
            ph.start(act, "act")
            with act.Fori(0, NB) as b, act.Fori(0, NG) as g:
                n = act.snap(b * NG + g + 1)

                def project(t):
                    act.wait_ge(*qkv_ps.at(n, t + 1))
                    act.wait_ge(*norm2.at(n, t))
                    act.activation(sq[:], ps[:, 0:2, :].rearrange("p r (h i) -> p r h i", i=DH), ACT.Square)\
                        .then_inc(squared.sem, 1)
                    if t == 0:
                        act.wait_ge(*o_ps.at(n, 0))
                        act.wait_ge(*halo.at(n, 0))
                    act.activation(v[:, 1 + t, :, 0:DH], ps[:, 2, :].rearrange("p (h i) -> p h i", i=DH), ACT.Copy)\
                        .then_inc(v_sb.sem, 1)

                def evacuate_qk(t):
                    act.wait_ge(*qkt_ps.at(n, 2 * t + 1))
                    act.wait_ge(*s_ps.at(n, PAIRS * t))
                    act.activation(qt[:], ps[:, QKT[0], :].rearrange("p (i k) -> p i k", k=P), ACT.Copy)\
                        .then_inc(qkt_sb.sem, 1)
                    act.wait_ge(*qkt_ps.at(n, 2 * t + 2))
                    if t == 0:
                        act.wait_ge(*halo.at(n, 0))
                    act.activation(kt[:, :, W + t * P:W + (t + 1) * P], ps[:, QKT[1], :].rearrange("p (i k) -> p i k", k=P),
                                   ACT.Copy).then_inc(qkt_sb.sem, 1)

                def softmax(t):
                    for i in range(PAIRS):
                        act.wait_ge(*negmax.at(n, PAIRS * t + i + 1))
                        act.wait_ge(*pt_ps.at(n, PAIRS * (t - 1) + i + 1))
                        for s in range(2):
                            e = act.activation(pr[:, 2 * i + s, P - W:2 * P], ps[:, SP_[i], s * KEYS:(s + 1) * KEYS], ACT.Exp,
                                               bias=nmx[:, 2 * i + s:2 * i + s + 1])
                        e.then_inc(p_sb.sem, 1)

                act.wait_ge(*ht_ps.at(n, 1))
                act.wait_ge(*qkv_ps.at(n, 0))
                act.activation(ht[:], ps[:, 3, :], ACT.Copy).then_inc(ht_sb.sem, 1)
                project(0)
                evacuate_qk(0)
                for t in range(GT):
                    softmax(t)
                    if t + 1 < GT:
                        project(t + 1)
                    for i in (1, 3):
                        act.wait_ge(*pt_ps.at(n, PAIRS * t + i + 1))
                        act.wait_ge(*o_ps.at(n, t))
                        act.activation(pt[:, 2 * i:2 * i + 2, :, :],
                                       ps[:, SP_[i], :].rearrange("p (s k q) -> p s k q", s=2, k=2), ACT.Copy)\
                            .then_inc(pt_sb[1].sem, 1)
                    if t + 1 < GT:
                        evacuate_qk(t + 1)
                    act.wait_ge(*ot_ps.at(n, t + 1))
                    act.wait_ge(*y_ps.at(n, t))
                    act.activation(ot[:], ps[:, OTB, :].rearrange("p (i k) -> p i k", k=P), ACT.Copy).then_inc(ot_sb.sem, 1)

        @block.vector
        def _(dve):
            ph.start(dve, "dve")
            dve.wait_ge(wts_loaded, WTS)
            dve.tensor_copy(identb[:], ident[:]).then_inc(prepared, 1)
            dve.tensor_copy(maskb[:], mask[:]).then_inc(prepared, 1)
            for r in range(4):
                dve.tensor_tensor(table[:, r], table[:, r], scales[:, r, :].unsqueeze(1).to_broadcast([P, T // P, DH]),
                                  ALU.mult).then_inc(prepared, 1)
            dve.wait_ge(prepared, 6 + 4)
            with dve.Fori(0, NB) as b, dve.Fori(0, NG) as g:
                n = dve.snap(b * NG + g + 1)

                def rotation(t):
                    dve.wait_ge(*squared.at(n, t + 1))
                    dve.wait_ge(*rotated.at(n, t))
                    for r in range(2):
                        qk_ps = ps[:, r, :].rearrange("p (h i) -> p h i", i=DH)
                        cos = table[:, 2 * r, bass.ds(g * GT + t, 1), :].to_broadcast([P, H, DH])
                        dve.tensor_tensor(rot_c[:, r], qk_ps, cos, ALU.mult)
                    for r in range(2):
                        swapped = ps[:, r, :].rearrange("p (h s i) -> p h s i", s=2, i=DH // 2)[:, :, ::-1, :]
                        sin = table[:, 2 * r + 1, bass.ds(g * GT + t, 1), :].to_broadcast([P, H, DH])\
                            .rearrange("p h (s i) -> p h s i", s=2)
                        terms = dve.tensor_tensor(rot_s[:, r].rearrange("p h (s i) -> p h s i", s=2), swapped, sin, ALU.mult)
                    terms.then_inc(rot_terms.sem, 1)
                    dve.tensor_reduce(ss[:, 0, :], sq[:].rearrange("p r h i -> p (r h) i"), AX.X, ALU.add).then_inc(norm2.sem, 1)
                    dve.wait_ge(*norm2.at(n, t + 1))
                    dve.wait_ge(*rnorm.at(n, t))
                    dve.tensor_scalar(ss[:, 1, :], ss[:, 0, :], 1e-24, None, ALU.max).then_inc(clipped.sem, 1)

                def maxima(t):
                    for i in range(PAIRS):
                        dve.wait_ge(*s_ps.at(n, PAIRS * t + i + 1))
                        dve.wait_ge(*p_sb.at(n, PAIRS * (t - 1) + i + 1))
                        dve.tensor_reduce(nmx[:, 2 * i:2 * i + 2],
                                          ps[:, SP_[i], 0:2 * KEYS].rearrange("p (s k) -> p s k", s=2), AX.X, ALU.max,
                                          negate=True).then_inc(negmax.sem, 1)

                rotation(0)
                for t in range(GT):
                    maxima(t)
                    if t + 1 < GT:
                        rotation(t + 1)
                    for i in (0, 2):
                        dve.wait_ge(*pt_ps.at(n, PAIRS * t + i + 1))
                        dve.wait_ge(*o_ps.at(n, t))
                        dve.tensor_copy(pt[:, 2 * i:2 * i + 2, :, :],
                                        ps[:, SP_[i], :].rearrange("p (s k q) -> p s k q", s=2, k=2)).then_inc(pt_sb[0].sem, 1)
                    dve.wait_ge(*o_ps.at(n, t + 1))
                    o4 = ps[:, 0:2, 0:4 * (DH + 1)].rearrange("p a (h i) -> p a h i", i=DH + 1)
                    dve.reciprocal(rs[:].rearrange("p (a h) -> p a h", a=2), o4[:, :, :, DH]).then_inc(rsum.sem, 1)
                    dve.wait_ge(*rsum.at(n, t + 1))
                    dve.wait_ge(*ot_ps.at(n, t))
                    for a in range(2):
                        on = dve.tensor_tensor(o[:, 4 * a:4 * a + 4, :], o4[:, a, :, 0:DH],
                                               rs[:, 4 * a:4 * a + 4].unsqueeze(2).to_broadcast([P, 4, DH]), ALU.mult)
                    on.then_inc(o_sb.sem, 1)
                    dve.wait_ge(*y_ps.at(n, t + 1))
                    if t == 0:
                        dve.wait_ge(*x_loaded.at(n, 16))
                        dve.wait_ge(*stored.at(n, 0))
                    dve.tensor_tensor(y[:, t, :], ps[:, YB, 0:D], x[:, t, :], ALU.add).then_inc(y_sb.sem, 1)
                dve.wait_ge(*qkt_sb.at(n, 2 * GT))
                dve.tensor_copy(kt[:, :, 0:W], kt[:, :, G:G + W]).then_inc(halo.sem, 1)
                dve.wait_ge(*v_sb.at(n, GT))
                dve.tensor_copy(v[:, 0, :, :], v[:, GT, :, :]).then_inc(halo.sem, 1)
    ph.close()


def window_attention(nc, name, src, x_in, dst, w, c):
    H, DH, W = 16, 8, 64
    KEYS = W + P
    PAIRS = H // 2
    RING = 4
    HALF = PAIRS // 2
    SCALE = float(DH) ** -0.5
    ph = Phase(nc, name)
    sb, signal = ph.sb, ph.counter
    ps = ph.banks()
    wq, wk, wv, wo = (sb(n, [P, D]) for n in ("wq", "wk", "wv", "wo"))
    bq, bk, bv, bqs = (sb(n, [P, 1]) for n in ("bq", "bk", "bv", "bqs"))
    bo = sb("bo", [P, D])
    ident = sb("ident", [P, P])
    identb = sb("identb", [P, P], BF16)
    mask = sb("mask", [P, 2, 2, KEYS])
    maskb = sb("maskb", [P, 2, 2, KEYS], BF16)
    own = sb("own", [P, 4])
    bk_own = sb("bk_own", [P, 4])
    h = sb("h", [P, GT, D])
    x = sb("x", [P, GT, D])
    xb = sb("xb", [P, GT, D])
    y = sb("y", [P, GT, D])
    ht = sb("ht", [P, G])
    qt = sb("qt", [P, G])
    kt = sb("kt", [P, 4, W + G])
    v = sb("v", [P, 1 + GT, H, DH + 1])
    nmx = sb("nmx", [P, H])
    pr = sb("pr", [P, H, 2 * P])
    pt = sb("pt", [P, H, 2, P])
    rs = sb("rs", [P, H])
    o = sb("o", [P, H, DH])
    ot = sb("ot", [P, P])

    wts_loaded = ph.semaphore("wts_loaded")
    prepared = ph.semaphore("prepared")
    h_loaded = signal("h_loaded", 16, "sp")
    x_loaded = signal("x_loaded", 16, "sp")
    stored = signal("stored", 16, "sp")
    xb_done = signal("xb_done", 1, "pool")
    ht_ps = signal("ht_ps", 1, "pe")
    ht_sb = signal("ht_sb", 1, "act")
    qkv_ps = signal("qkv_ps", 3, "pe")
    qkv_sb = signal("qkv_sb", 3, "act")
    s_ps = signal("s_ps", PAIRS * GT, "pe")
    negmax = signal("negmax", PAIRS * GT, "dve")
    p_sb = signal("p_sb", PAIRS * GT, "act")
    pt_ps = signal("pt_ps", PAIRS * GT, "pe")
    pt_sb = [signal("pt_sb_dve", HALF * GT, "dve"), signal("pt_sb_act", HALF * GT, "act")]
    o_ps = signal("o_ps", GT, "pe")
    rsum = signal("rsum", GT, "dve")
    o_sb = signal("o_sb", GT, "dve")
    ot_ps = signal("ot_ps", GT, "pe")
    ot_sb = signal("ot_sb", GT, "act")
    y_ps = signal("y_ps", GT, "pe")
    y_sb = signal("y_sb", GT, "dve")
    halo = signal("halo", 2, "dve")

    loads = [(wq[:], w["Wq"]), (wk[:], w["Wk"]), (wv[:], w["Wv"]), (wo[:], w["Wo"]), (bq[:], w["bq"]), (bk[:], w["bk"]),
             (bv[:], w["bv"]), (bo[:], w["bo"].to_broadcast([P, D])), (ident[:], c["ident"]), (own[:], c["own_head"]),
             (mask[:], c["attn_mask"].rearrange("p (e h k) -> p e h k", e=2, h=2))]
    LOADED, PREPARED = 16 * len(loads), 3 + 4

    with nc.Block() as block:

        @block.sync
        def _(sp):
            ph.start(sp, "sp")
            for out, in_ in loads:
                sp.dma_start(out, in_).then_inc(wts_loaded, 16)
            with sp.Fori(0, NB) as b, sp.Fori(0, NG) as g:
                n = sp.snap(b * NG + g + 1)
                row = sp.snap(scratch_row(b, g))
                sp.wait_ge(*ht_ps.at(n, 0))
                sp.dma_start(h[:], tiles(src[bass.ds(row, G), :])).then_inc(h_loaded.sem, 16)
                sp.wait_ge(*xb_done.at(n, 0))
                sp.dma_start(x[:], tiles(x_in[bass.ds(row, G), :])).then_inc(x_loaded.sem, 16)
                sp.wait_ge(*y_sb.at(n, GT))
                sp.dma_start(tiles(dst[bass.ds(row, G), :]), y[:]).then_inc(stored.sem, 16)
            sp.wait_ge(*stored.at(TURNS + 1, 0))

        @block.gpsimd
        def _(pool):
            ph.start(pool, "pool")
            pool.memset(kt[:, :, 0:W], 0.0).then_inc(prepared, 1)
            pool.memset(v[:, 0, :, :], 0.0).then_inc(prepared, 1)
            pool.memset(v[:, 1:, :, DH:], 1.0).then_inc(prepared, 1)
            pool.memset(pr[:, :, 0:P - W], 0.0).then_inc(prepared, 1)
            pool.wait_ge(wts_loaded, LOADED)
            with pool.Fori(0, NB) as b, pool.Fori(0, NG) as g:
                n = pool.snap(b * NG + g + 1)
                pool.wait_ge(*x_loaded.at(n, 16))
                pool.wait_ge(*y_sb.at(n, 0))
                pool.tensor_tensor(xb[:], x[:], bo[:].unsqueeze(1).to_broadcast([P, GT, D]), ALU.add).then_inc(xb_done.sem, 1)

        @block.tensor
        def _(pe):
            ph.start(pe, "pe")
            pe.wait_ge(wts_loaded, LOADED)
            pe.wait_ge(prepared, PREPARED)
            with pe.Fori(0, NB) as b, pe.Fori(0, NG) as g:
                n = pe.snap(b * NG + g + 1)

                def scores(t, i):
                    j = PAIRS * t + i - RING
                    pe.wait_ge(*pt_sb[i % 2].at(n, j // 2 + 1))
                    if t == 0 and i == 0:
                        pe.wait_ge(*qkv_sb.at(n, 3))
                        pe.wait_ge(*halo.at(n, 0))
                    if t == 0:
                        m = maskb[:, bass.ds(g, 1), :, :].rearrange("p e h k -> p (e h k)")
                    else:
                        m = maskb[:, 1, :, :].rearrange("p h k -> p (h k)")
                    bank, at = 4 + i % RING, 32 * (i // 2)
                    pe.matmul(ps[:, bank, 0:2 * KEYS], identb[:], m, start=True, stop=False, skip_group_check=True)
                    for s in range(2):
                        mm = pe.matmul(ps[:, bank, s * KEYS:(s + 1) * KEYS], qt[at:at + 32, t * P:(t + 1) * P],
                                       kt[at:at + 32, (2 * i + s) % 4, t * P:t * P + KEYS],
                                       start=False, stop=s == 1, skip_group_check=True, tile_position=(at, 0))
                    mm.then_inc(s_ps.sem, 1)

                def transpose_p(t, i):
                    pe.wait_ge(*p_sb.at(n, PAIRS * t + i + 1))
                    for s in range(2):
                        for k in range(2):
                            mm = pe.transpose(ps[:, 4 + i % RING, (2 * s + k) * P:(2 * s + k + 1) * P],
                                              pr[:, 2 * i + s, k * P:(k + 1) * P], ident[:])
                    mm.then_inc(pt_ps.sem, 1)

                def attend(t):
                    pe.wait_ge(*o_sb.at(n, t))
                    if t == 0:
                        pe.wait_ge(*ht_sb.at(n, 1))
                    for i in range(PAIRS):
                        pe.wait_ge(*pt_sb[i % 2].at(n, HALF * t + i // 2 + 1))
                        for s in range(2):
                            j = 2 * i + s
                            for k in range(2):
                                mm = pe.matmul(ps[:, 0, j * (DH + 1):(j + 1) * (DH + 1)], pt[:, j, k, :], v[:, t + k, j, :],
                                               start=k == 0, stop=k == 1)
                    mm.then_inc(o_ps.sem, 1)

                def finish(t):
                    pe.wait_ge(*o_sb.at(n, t + 1))
                    pe.wait_ge(*ot_sb.at(n, t))
                    pe.transpose(ps[:, 1, 0:P], o[:].rearrange("p h i -> p (h i)"), ident[:]).then_inc(ot_ps.sem, 1)
                    pe.wait_ge(*ot_sb.at(n, t + 1))
                    pe.wait_ge(*y_sb.at(n, t))
                    pe.matmul(ps[:, 2, 0:D], ot[:], wo[:], start=True, stop=True).then_inc(y_ps.sem, 1)

                pe.wait_ge(*h_loaded.at(n, 16))
                pe.wait_ge(*o_sb.at(n, 0))
                for t in range(GT):
                    mm = pe.transpose(ps[:, 0, t * P:(t + 1) * P], h[:, t, :], ident[:])
                mm.then_inc(ht_ps.sem, 1)
                pe.wait_ge(*ht_sb.at(n, 1))
                pe.wait_ge(*ot_sb.at(n, 0))
                pe.matmul(ps[:, 1, :], wq[:], ht[:], start=True, stop=True).then_inc(qkv_ps.sem, 1)
                pe.wait_ge(*y_sb.at(n, 0))
                pe.matmul(ps[:, 2, :], wk[:], ht[:], start=True, stop=True).then_inc(qkv_ps.sem, 1)
                pe.wait_ge(*qkv_sb.at(n, 0))
                for t in range(GT):
                    mm = pe.matmul(ps[:, 3, t * P:(t + 1) * P], ht[:, t * P:(t + 1) * P], wv[:], start=True, stop=True)
                mm.then_inc(qkv_ps.sem, 1)
                for t in range(GT):
                    for i in range(RING):
                        scores(t, i)
                    for i in range(PAIRS):
                        transpose_p(t, i)
                        if i + RING < PAIRS:
                            scores(t, i + RING)
                    attend(t)
                    finish(t)

        @block.scalar
        def _(act):
            ph.start(act, "act")
            act.wait_ge(wts_loaded, LOADED)
            act.wait_ge(prepared, PREPARED)
            with act.Fori(0, NB) as b, act.Fori(0, NG) as g:
                n = act.snap(b * NG + g + 1)
                act.wait_ge(*ht_ps.at(n, 1))
                act.wait_ge(*qkv_ps.at(n, 0))
                act.activation(ht[:], ps[:, 0, :], ACT.Copy).then_inc(ht_sb.sem, 1)
                act.wait_ge(*qkv_ps.at(n, 1))
                act.wait_ge(*s_ps.at(n, 0))
                act.activation(qt[:], ps[:, 1, :], ACT.Identity, scale=SCALE, bias=bqs[:]).then_inc(qkv_sb.sem, 1)
                act.wait_ge(*qkv_ps.at(n, 2))
                act.wait_ge(*halo.at(n, 0))
                for m in range(4):
                    k = act.activation(kt[:, m, W:W + G], ps[:, 2, :], ACT.Identity, scale=own[:, m:m + 1], bias=bk_own[:, m:m + 1])
                k.then_inc(qkv_sb.sem, 1)
                act.wait_ge(*qkv_ps.at(n, 3))
                act.wait_ge(*o_ps.at(n, 0))
                act.activation(v[:, 1:, :, 0:DH], ps[:, 3, :].rearrange("p (t h i) -> p t h i", t=GT, i=DH), ACT.Copy)\
                    .then_inc(qkv_sb.sem, 1)

                def exponentials(t, i):
                    act.wait_ge(*negmax.at(n, PAIRS * t + i + 1))
                    act.wait_ge(*pt_ps.at(n, PAIRS * (t - 1) + i + 1))
                    for s in range(2):
                        e = act.activation(pr[:, 2 * i + s, P - W:2 * P], ps[:, 4 + i % RING, s * KEYS:(s + 1) * KEYS],
                                           ACT.Exp, bias=nmx[:, 2 * i + s:2 * i + s + 1])
                    e.then_inc(p_sb.sem, 1)

                def evacuate_p(t, i):
                    act.wait_ge(*pt_ps.at(n, PAIRS * t + i + 1))
                    act.wait_ge(*o_ps.at(n, t))
                    act.activation(pt[:, 2 * i:2 * i + 2, :, :],
                                   ps[:, 4 + i % RING, :].rearrange("p (s k q) -> p s k q", s=2, k=2), ACT.Copy)\
                        .then_inc(pt_sb[1].sem, 1)

                for t in range(GT):
                    for i in range(PAIRS):
                        exponentials(t, i)
                        if i >= 2 and i % 2 == 1:
                            evacuate_p(t, i - 2)
                    evacuate_p(t, PAIRS - 1)
                    act.wait_ge(*ot_ps.at(n, t + 1))
                    act.wait_ge(*y_ps.at(n, t))
                    act.activation(ot[:], ps[:, 1, 0:P], ACT.Identity, bias=bv[:]).then_inc(ot_sb.sem, 1)

        @block.vector
        def _(dve):
            ph.start(dve, "dve")
            dve.wait_ge(wts_loaded, LOADED)
            dve.tensor_copy(identb[:], ident[:])
            dve.tensor_copy(maskb[:], mask[:])
            dve.tensor_scalar(bqs[:], bq[:], SCALE, None, ALU.mult)
            dve.tensor_scalar(bk_own[:], own[:], bk[:], None, ALU.mult).then_inc(prepared, 3)
            with dve.Fori(0, NB) as b, dve.Fori(0, NG) as g:
                n = dve.snap(b * NG + g + 1)

                def maxima(t, i):
                    dve.wait_ge(*s_ps.at(n, PAIRS * t + i + 1))
                    dve.wait_ge(*p_sb.at(n, PAIRS * (t - 1) + i + 1))
                    dve.tensor_reduce(nmx[:, 2 * i:2 * i + 2],
                                      ps[:, 4 + i % RING, 0:2 * KEYS].rearrange("p (s k) -> p s k", s=2), AX.X, ALU.max,
                                      negate=True).then_inc(negmax.sem, 1)

                def evacuate_p(t, i):
                    dve.wait_ge(*pt_ps.at(n, PAIRS * t + i + 1))
                    dve.wait_ge(*o_ps.at(n, t))
                    dve.tensor_copy(pt[:, 2 * i:2 * i + 2, :, :],
                                    ps[:, 4 + i % RING, :].rearrange("p (s k q) -> p s k q", s=2, k=2)).then_inc(pt_sb[0].sem, 1)

                for t in range(GT):
                    for i in range(RING):
                        maxima(t, i)
                    for i in range(0, PAIRS, 2):
                        evacuate_p(t, i)
                        if i + RING < PAIRS:
                            maxima(t, i + RING)
                            maxima(t, i + RING + 1)
                    dve.wait_ge(*o_ps.at(n, t + 1))
                    oh = ps[:, 0, 0:H * (DH + 1)].rearrange("p (h i) -> p h i", i=DH + 1)
                    dve.reciprocal(rs[:], oh[:, :, DH]).then_inc(rsum.sem, 1)
                    dve.wait_ge(*rsum.at(n, t + 1))
                    dve.wait_ge(*ot_ps.at(n, t))
                    dve.tensor_tensor(o[:], oh[:, :, 0:DH], rs[:].unsqueeze(2).to_broadcast([P, H, DH]), ALU.mult)\
                        .then_inc(o_sb.sem, 1)
                    dve.wait_ge(*y_ps.at(n, t + 1))
                    if t == 0:
                        dve.wait_ge(*xb_done.at(n, 1))
                        dve.wait_ge(*stored.at(n, 0))
                    dve.tensor_tensor(y[:, t, :], ps[:, 2, 0:D], xb[:, t, :], ALU.add).then_inc(y_sb.sem, 1)
                dve.tensor_copy(kt[:, :, 0:W], kt[:, :, G:G + W]).then_inc(halo.sem, 1)
                dve.wait_ge(*qkv_sb.at(n, 3))
                dve.tensor_copy(v[:, 0, :, :], v[:, GT, :, :]).then_inc(halo.sem, 1)
    ph.close()


def delta_attention(nc, name, x_in, dst, w, c):
    H, DK, DV = 8, 96, 192
    HG = 4
    VD = H * DV
    LEVELS = 7
    NQK, NV = 2 * H, VD // P
    NG3 = GT * 3 // 2
    SLOTS = 3
    USES = NQK + NV + NG3
    ph = Phase(nc, name)
    sb, signal = ph.sb, ph.counter
    ps = ph.banks()
    wq = sb("wq", [P, H * DK])
    wk = sb("wk", [P, H * DK])
    wv = sb("wv", [P, VD])
    wg = sb("wg", [P, VD])
    wo = sb("wo", [P, NV, D])
    onorm = sb("onorm", [P, NV])
    wba = sb("wba", [P, 2 * H])
    conv_qk = sb("conv_qk", [DK, H, 2, 4])
    conv_v = sb("conv_v", [P, NV, 4])
    norm1 = sb("norm1", [P, 1])
    decay_rate = sb("decay_rate", [P, H])
    dt_bias = sb("dt_bias", [P, H])
    ident = sb("ident", [P, P])
    ident4 = sb("ident4", [P, HG, P])
    sums = sb("sums", [P, 3, P])
    not_first = sb("not_first", [P, 1])
    blocks = sb("blocks", [P, LEVELS, P // 2])
    minus_half = sb("minus_half", [P, 4 * H])
    x = sb("x", [P, GT, D])
    y = sb("y", [P, GT, D])
    hn = sb("hn", [P, GT, D])
    out = sb("out", [P, GT, D])
    stats = sb("stats", [P, GT, 6])
    mv = sb("mv", [P, GT, 2])
    ms = sb("ms", [P, 2, GT])
    rstd = sb("rstd", [P, 2, GT])
    ht = sb("ht", [P, 3 + G])
    raw = sb("raw", [P, SLOTS, 3 + G])
    conv = sb("conv", [P, SLOTS, G])
    qk = sb("qk", [DK, H, 2, G])
    vt = sb("vt", [P, NV, G])
    gate = sb("gate", [P, GT, VD])
    za = sb("za", [P, 12, GT * H])
    ex = sb("ex", [P, 6, GT, H])
    sq = sb("sq", [DK, H, 2, P])
    cf = sb("cf", [P, 14, 2 * H])
    gd = sb("gd", [P, H, P])
    al = sb("al", [P, H, 2, P])
    tm = sb("tm", [P, H, P])
    tt = sb("tt", [P, H, P])
    am = sb("am", [P, H, P // 2])
    kd = sb("kd", [P, H, DK])
    vr = sb("vr", [P, H, DV])
    delta = sb("delta", [P, H, DV])
    o = sb("o", [P, H, DV])
    ot = sb("ot", [P, NV, P])
    state = sb("state", [DK, H, DV])

    wts_loaded = ph.semaphore("wts_loaded")
    prepared = ph.semaphore("prepared")
    x_loaded = signal("x_loaded", 16, "sp")
    stored = signal("stored", 16, "sp")
    stats_done = signal("stats_done", GT, "dve")
    seen = signal("seen", 1, "dve").sem
    moments = signal("moments", GT, "dve")
    root1 = signal("root1", 1, "dve")
    root1_done = signal("root1_done", 1, "pool")
    root2 = signal("root2", 4, "dve")
    root2_done = signal("root2_done", 1, "pool")
    y_sb = signal("y_sb", 1, "dve")
    hn_sb = signal("hn_sb", 1, "dve")
    ht_ps = signal("ht_ps", 1, "pe")
    ht_sb = signal("ht_sb", 1, "act")
    ht_halo = signal("ht_halo", 1, "dve")
    ba_ps = signal("ba_ps", 1, "pe")
    za_step = signal("za_step", 22, "dve")
    za_exp = signal("za_exp", 2, "act")
    cum_ps = signal("cum_ps", 1, "pe")
    ex_sb = signal("ex_sb", 2, "act")
    decay_cut = signal("decay_cut", 1, "dve")
    use_ps = signal("use_ps", USES, "pe")
    use_sb = signal("use_sb", USES, "act")
    tap = signal("tap", 3 * (NQK + NV), "dve")
    silu = signal("silu", NQK + NV, "act")
    zeroed = signal("zeroed", 2, "dve")
    sq_sb = signal("sq_sb", GT, "pool")
    n2_ps = signal("n2_ps", GT, "pe")
    n2_sb = signal("n2_sb", GT, "dve")
    rn_sb = signal("rn_sb", GT, "pool")
    coef = signal("coef", 4 * GT, "dve")

    def both(n, per, owner):
        return [signal(f"{n}{i}", per, owner) for i in range(2)]
    dec_ps = both("dec_ps", GT, "pe")
    gd_sb = both("gd_sb", GT, "dve")
    kq_ps = both("kq_ps", GT, "pe")
    al_sb = both("al_sb", GT, "dve")
    kt_ps = both("kt_ps", GT, "pe")
    kd_sb = both("kd_sb", GT, "act")
    vt_ps = both("vt_ps", GT, "pe")
    vb_sb = both("vb_sb", GT, "act")
    tm_one = both("tm_one", GT, "act")
    lx_ps = both("lx_ps", LEVELS * GT, "pe")
    am_sb = both("am_sb", LEVELS * GT, "dve")
    ty_ps = both("ty_ps", (LEVELS - 1) * GT, "pe")
    tm_sb = both("tm_sb", LEVELS * GT, "dve")
    tt_ps = both("tt_ps", LEVELS * GT, "pe")
    tt_sb = both("tt_sb", LEVELS * GT, "act")
    ks_ps = both("ks_ps", GT, "pe")
    r_sb = both("r_sb", GT, "dve")
    delta_ps = both("delta_ps", GT, "pe")
    delta_sb = both("delta_sb", GT, "act")
    qs_ps = both("qs_ps", GT, "pe")
    qs_sb = both("qs_sb", GT, "act")
    ad_ps = both("ad_ps", GT, "pe")
    o_sb = both("o_sb", GT, "dve")
    up_ps = both("up_ps", GT, "pe")
    state_sb = both("state_sb", GT, "dve")
    osq = signal("osq", GT, "act")
    om = signal("om", 4 * GT, "dve")
    orn = signal("orn", GT, "pool")
    og_sb = signal("og_sb", GT, "dve")
    ot_ps = signal("ot_ps", 3 * GT, "pe")
    ot_sb = signal("ot_sb", 3 * GT, "act")
    y_ps = signal("y_ps", GT, "pe")
    out_sb = signal("out_sb", GT, "dve")

    loads = [(wq[:], w["Wq"]), (wk[:], w["Wk"]), (wv[:], w["Wv"]), (wg[:], w["Wg"]), (wo[:], tiles(w["Wo"])),
             (wba[:, 0:H], w["Wb"]), (wba[:, H:2 * H], w["Wa"]),
             (conv_qk[:, :, 0, :], w["conv_q_w"].rearrange("(h d) i -> d h i", d=DK)),
             (conv_qk[:, :, 1, :], w["conv_k_w"].rearrange("(h d) i -> d h i", d=DK)),
             (conv_v[:], tiles(w["conv_v_w"])), (norm1[:], w["norm1_w"]),
             (decay_rate[:], w["A_log"].to_broadcast([P, H])), (dt_bias[:], w["dt_bias"].to_broadcast([P, H])),
             (ident[:], c["ident"]), (sums[:], c["sums"].rearrange("p (k i) -> p k i", k=3)),
             (not_first[:], c["not_first"]), (blocks[:], c["blocks"].rearrange("p (m i) -> p m i", m=LEVELS)),
             (minus_half[:], c["minus_half"][:, 0:4 * H])]
    ow = w["onorm_w"]
    for m, (p0, p1, a) in ((0, (0, P, 0)), (1, (0, DV - P, P)), (1, (DV - P, P, 0)), (2, (0, P, DV - P))):
        for n in range(m, NV, 3):
            loads.append((onorm[p0:p1, n:n + 1], ow[a:a + p1 - p0, :]))
    for i in range(HG):
        loads.append((ident4[:, i, :], c["ident"]))
    LOADED = 16 * len(loads)

    N2, N2E, RN, BRK, NPB, KDF, OSUM, OMS, OME, ORN, OF, RQ2, PBK, RQS = range(14)
    BETA, DEC, DCUT, PI, PLAST, DLAST = range(6)

    def left(t, m):
        s = 1 << m
        return t.rearrange("p (n two s) -> p n two s", two=2, s=s)[:, :, 0, :]

    def left4(t, m):
        s = 1 << m
        return t.rearrange("p h (n two s) -> p h n two s", two=2, s=s)[:, :, :, 0, :]

    with nc.Block() as block:

        @block.sync
        def _(sp):
            ph.start(sp, "sp")
            for dst_, src_ in loads:
                sp.dma_start(dst_, src_).then_inc(wts_loaded, 16)
            with sp.Fori(0, NB) as b, sp.Fori(0, NG) as g:
                n = sp.snap(b * NG + g + 1)
                sp.wait_ge(*y_sb.at(n, 0))
                sp.dma_start(x[:], tiles(x_in[bass.ds((b * NG + g) * G, G), :])).then_inc(x_loaded.sem, 16)
                sp.wait_ge(*out_sb.at(n, GT))
                sp.dma_start(tiles(dst[bass.ds(scratch_row(b, g), G), :]), out[:]).then_inc(stored.sem, 16)
            sp.wait_ge(*stored.at(TURNS + 1, 0))

        @block.gpsimd
        def _(pool):
            ph.start(pool, "pool")
            pool.wait_ge(wts_loaded, LOADED)
            with pool.Fori(0, NB) as b, pool.Fori(0, NG) as g:
                n = pool.snap(b * NG + g + 1)
                pool.wait_ge(*root1.at(n, 1))
                pool.tensor_tensor(rstd[:, 0, :], ms[:, 0, :], minus_half[:, 0:GT], ALU.pow).then_inc(root1_done.sem, 1)
                pool.wait_ge(*root2.at(n, 4))
                pool.tensor_tensor(rstd[:, 1, :], ms[:, 1, :], minus_half[:, 0:GT], ALU.pow).then_inc(root2_done.sem, 1)
                for t in range(GT):
                    if t == 0:
                        pool.wait_ge(*silu.at(n, NQK))
                    pool.wait_ge(*n2_ps.at(n, t))
                    now = qk[:, :, :, t * P:(t + 1) * P]
                    pool.tensor_tensor(sq[:].rearrange("p h r i -> p (h r) i"), now.rearrange("p h r i -> p (h r) i"),
                                       now.rearrange("p h r i -> p (h r) i"), ALU.mult).then_inc(sq_sb.sem, 1)
                    pool.wait_ge(*n2_sb.at(n, t + 1))
                    pool.tensor_tensor(cf[:, RN, :], cf[:, N2E, :], minus_half[:, 0:2 * H], ALU.pow).then_inc(rn_sb.sem, 1)
                    pool.wait_ge(*om.at(n, 4 * t + 3))
                    pool.tensor_tensor(cf[:, ORN, 0:H], cf[:, OME, 0:H], minus_half[:, 0:H], ALU.pow).then_inc(orn.sem, 1)

        @block.tensor
        def _(pe):
            ph.start(pe, "pe")
            pe.wait_ge(wts_loaded, LOADED)
            pe.wait_ge(prepared, 3)
            with pe.Fori(0, NB) as b, pe.Fori(0, NG) as g:
                n = pe.snap(b * NG + g + 1)
                pe.wait_ge(*hn_sb.at(n, 1))
                pe.wait_ge(*out_sb.at(n, 0))
                for i in range(2):
                    pe.wait_ge(*state_sb[i].at(n, 0))
                for t in range(GT):
                    mm = pe.transpose(ps[:, 6, t * P:(t + 1) * P], hn[:, t, :], ident[:])
                mm.then_inc(ht_ps.sem, 1)
                pe.wait_ge(*ht_sb.at(n, 1))
                for t in range(GT):
                    mm = pe.matmul(ps[:, 6, t * 2 * H:(t + 1) * 2 * H], ht[:, 3 + t * P:3 + (t + 1) * P], wba[:],
                                   start=True, stop=True)
                mm.then_inc(ba_ps.sem, 1)
                for u in range(NQK + NV):
                    pe.wait_ge(*use_sb.at(n, freed(u, SLOTS, USES)))
                    if u < NQK:
                        M, lhs = DK, (wq, wk)[u % 2][:, u // 2 * DK:(u // 2 + 1) * DK]
                    else:
                        M, lhs = P, wv[:, (u - NQK) * P:(u - NQK + 1) * P]
                    slot = 2 * (u % SLOTS)
                    pe.matmul(ps[0:M, slot, :], lhs, ht[:, 0:G], start=True, stop=True)
                    pe.matmul(ps[0:M, slot + 1, 0:3], lhs, ht[:, G:G + 3], start=True, stop=True).then_inc(use_ps.sem, 1)
                for u in range(NQK + NV, USES):
                    pe.wait_ge(*use_sb.at(n, freed(u, SLOTS, USES)))
                    for i in range(2):
                        k = 2 * (u - NQK - NV) + i
                        mm = pe.matmul(ps[:, 2 * (u % SLOTS) + i, :], ht[:, 3 + k // 3 * P:3 + (k // 3 + 1) * P],
                                       wg[:, k % 3 * 512:(k % 3 + 1) * 512], start=True, stop=True)
                    mm.then_inc(use_ps.sem, 1)
                pe.wait_ge(*za_step.at(n, 22))
                for i in range(3):
                    mm = pe.matmul(ps[:, 7, i * GT * H:(i + 1) * GT * H], sums[:, i, :], za[:, 0, :], start=True, stop=True)
                mm.then_inc(cum_ps.sem, 1)

                def heads(i):
                    return [(j, HG * i + j) for j in range(HG)]

                def start_chunk(t, i):
                    B = 4 * i
                    if t == 0:
                        pe.wait_ge(*decay_cut.at(n, 1))
                        pe.wait_ge(*use_sb.at(n, USES))
                        pe.wait_ge(*silu.at(n, NQK + NV))
                    pe.wait_ge(*state_sb[i].at(n, t))
                    for j, h in heads(i):
                        mm = pe.matmul(ps[:, B, j * P:(j + 1) * P], ex[:, DCUT, t, h:h + 1].to_broadcast([P, P]), ident[:],
                                       start=True, stop=True)
                    mm.then_inc(dec_ps[i].sem, 1)
                    pe.wait_ge(*ot_sb.at(n, 3 * t))
                    pe.wait_ge(*out_sb.at(n, t))
                    pe.wait_ge(*o_sb[i].at(n, t))
                    for j, h in heads(i):
                        mm = pe.matmul(ps[:, B + 1 + j // 2, j % 2 * 2 * P:(j % 2 + 1) * 2 * P], qk[:, h, 1, t * P:(t + 1) * P],
                                       qk[:, h, :, t * P:(t + 1) * P], start=True, stop=True)
                    mm.then_inc(kq_ps[i].sem, 1)

                def norms(t):
                    pe.wait_ge(*sq_sb.at(n, t + 1))
                    pe.wait_ge(*gd_sb[0].at(n, t + 1))
                    for k in range(2 * H):
                        mm = pe.matmul(ps[:, 0, k:k + 1], sq[:, k // 2, k % 2, :], sums[0:DK, 1, 0:1], start=True, stop=True)
                    mm.then_inc(n2_ps.sem, 1)

                def tokens_first(t, i):
                    B = 4 * i
                    pe.wait_ge(*(n2_sb.at(n, t + 1) if i == 0 else gd_sb[i].at(n, t + 1)))
                    for j, h in heads(i):
                        mm = pe.transpose(ps[:, B, j * DK:(j + 1) * DK], qk[:, h, 1, t * P:(t + 1) * P], ident[0:DK, 0:DK])
                    mm.then_inc(kt_ps[i].sem, 1)
                    pe.wait_ge(*al_sb[i].at(n, t + 1))
                    for j, h in heads(i):
                        mm = pe.transpose(ps[:, B + 3, j * P:(j + 1) * P], al[:, h, 1, :], ident[:])
                    mm.then_inc(lx_ps[i].sem, 1)
                    for k in range(6):
                        mm = pe.transpose(ps[:, B + 1 + k // 3, k % 3 * P:(k % 3 + 1) * P],
                                          vt[:, 6 * i + k, t * P:(t + 1) * P], ident[:])
                    mm.then_inc(vt_ps[i].sem, 1)

                def level_lx(t, i, m):
                    pe.wait_ge(*tm_sb[i].at(n, LEVELS * t + m))
                    pe.wait_ge(*am_sb[i].at(n, LEVELS * t + m))
                    for j, h in heads(i):
                        mm = pe.matmul(ps[:, 4 * i + 3, j * 64:(j + 1) * 64], al[:, h, 1, :], left(tm[:, h, :], m),
                                       start=True, stop=True)
                    mm.then_inc(lx_ps[i].sem, 1)

                def level_ty(t, i, m):
                    pe.wait_ge(*am_sb[i].at(n, LEVELS * t + m + 1))
                    pe.wait_ge(*tt_sb[i].at(n, LEVELS * t + m))
                    pe.wait_ge(*vb_sb[i].at(n, t + 1))
                    for j, h in heads(i):
                        mm = pe.matmul(ps[:, 4 * i + 2, j * 64:(j + 1) * 64], tt[:, h, :], am[:, h, :], start=True, stop=True)
                    mm.then_inc(ty_ps[i].sem, 1)

                def level_tt(t, i, m):
                    pe.wait_ge(*tm_sb[i].at(n, LEVELS * t + m + 1))
                    pe.wait_ge(*(vb_sb[i].at(n, t + 1) if m == 0 else tt_sb[i].at(n, LEVELS * t + m)))
                    for j, h in heads(i):
                        mm = pe.transpose(ps[:, 4 * i + 1, j * P:(j + 1) * P], tm[:, h, :], ident[:])
                    mm.then_inc(tt_ps[i].sem, 1)

                def pairs(i, banks, M, lhs, rhs, done):
                    for j, h in heads(i):
                        mm = pe.matmul(ps[0:M, 4 * i + banks[j // 2], j % 2 * DV:(j % 2 + 1) * DV], lhs(h), rhs(h),
                                       start=True, stop=True)
                    mm.then_inc(done.sem, 1)

                def from_state(t, i):
                    pe.wait_ge(*state_sb[i].at(n, t))
                    pe.wait_ge(*zeroed.at(b + 1, 2))
                    pe.wait_ge(*kd_sb[i].at(n, t + 1))
                    pe.wait_ge(*am_sb[i].at(n, LEVELS * t + LEVELS))
                    pairs(i, (0, 3), P, lambda h: qk[:, h, 1, t * P:(t + 1) * P], lambda h: state[:, h, :], ks_ps[i])

                def solve(t, i):
                    pe.wait_ge(*r_sb[i].at(n, t + 1))
                    pe.wait_ge(*tt_sb[i].at(n, LEVELS * t + LEVELS))
                    pairs(i, (1, 2), P, lambda h: tt[:, h, :], lambda h: vr[:, h, :], delta_ps[i])
                    pairs(i, (0, 3), P, lambda h: qk[:, h, 0, t * P:(t + 1) * P], lambda h: state[:, h, :], qs_ps[i])

                def outputs(t, i):
                    pe.wait_ge(*delta_sb[i].at(n, t + 1))
                    pairs(i, (1, 2), P, lambda h: al[:, h, 0, :], lambda h: delta[:, h, :], ad_ps[i])
                    pe.wait_ge(*qs_sb[i].at(n, t + 1))
                    pairs(i, (0, 3), DK, lambda h: kd[:, h, :], lambda h: delta[:, h, :], up_ps[i])

                def project_out(t):
                    for k in range(3):
                        if k == 0:
                            pe.wait_ge(*og_sb.at(n, t + 1))
                        for i in range(4):
                            m = 4 * k + i
                            mm = pe.transpose(ps[:, (1, 2, 5)[k], i * P:(i + 1) * P],
                                              o[:].rearrange("p h v -> p (h v)")[:, m * P:(m + 1) * P], ident[:])
                        mm.then_inc(ot_ps.sem, 1)
                    for m in range(NV):
                        pe.wait_ge(*ot_sb.at(n, 3 * t + m // 4 + 1))
                        mm = pe.matmul(ps[:, 6, 0:D], ot[:, m, :], wo[:, m, :], start=m == 0, stop=m == NV - 1)
                    mm.then_inc(y_ps.sem, 1)

                for t in range(GT):
                    for i in range(2):
                        start_chunk(t, i)
                    norms(t)
                    for i in range(2):
                        tokens_first(t, i)
                    for i in range(2):
                        level_tt(t, i, 0)
                    for m in range(1, LEVELS):
                        for i in range(2):
                            level_lx(t, i, m)
                        for i in range(2):
                            level_ty(t, i, m)
                        for i in range(2):
                            level_tt(t, i, m)
                    for i in range(2):
                        from_state(t, i)
                    for i in range(2):
                        solve(t, i)
                    for i in range(2):
                        outputs(t, i)
                    project_out(t)

        @block.scalar
        def _(act):
            ph.start(act, "act")
            act.wait_ge(wts_loaded, LOADED)
            act.activation(decay_rate[:], decay_rate[:], ACT.Exp).then_inc(prepared, 1)
            with act.Fori(0, NB) as b, act.Fori(0, NG) as g:
                n = act.snap(b * NG + g + 1)
                act.wait_ge(*ht_ps.at(n, 1))
                act.wait_ge(*use_ps.at(n, 0))
                act.wait_ge(*ht_halo.at(n, 0))
                act.activation(ht[:, 3:], ps[:, 6, :], ACT.Copy).then_inc(ht_sb.sem, 1)
                act.wait_ge(*za_step.at(n, 4))
                act.activation(za[:, 4, :], za[:, 3, :], ACT.Exp).then_inc(za_exp.sem, 1)
                act.activation(za[:, 5, :], za[:, 1, :], ACT.Exp, scale=-1.0).then_inc(za_exp.sem, 1)

                def taps(u):
                    M = DK if u < NQK else P
                    slot, k = 2 * (u % SLOTS), u % SLOTS
                    wts = conv_qk[:, u // 2, u % 2, :] if u < NQK else conv_v[:, u - NQK, :]
                    act.wait_ge(*use_ps.at(n, u + 1))
                    act.wait_ge(*tap.at(n, 3 * freed(u, SLOTS, NQK + NV)))
                    act.wait_ge(*silu.at(n, freed(u, SLOTS, NQK + NV)))
                    both_banks = ps[0:M, slot:slot + 2, :].rearrange("p a i -> p (a i)")
                    act.activation(raw[0:M, k, :], both_banks[:, 0:3 + G], ACT.Copy)
                    act.activation(conv[0:M, k, :], both_banks[:, 0:G], ACT.Copy, scale=wts[:, 0:1]).then_inc(use_sb.sem, 1)

                def activate(u):
                    M, k = (DK if u < NQK else P), u % SLOTS
                    act.wait_ge(*tap.at(n, 3 * u + 3))
                    to = qk[:, u // 2, u % 2, :] if u < NQK else vt[:, u - NQK, :]
                    if u == 0:
                        for i in range(2):
                            act.wait_ge(*qs_ps[i].at(n, 0))
                            act.wait_ge(*vt_ps[i].at(n, 0))
                    act.activation(to, conv[0:M, k, :], ACT.Silu).then_inc(silu.sem, 1)

                for u in range(NQK + NV):
                    taps(u)
                    if u >= 1:
                        activate(u - 1)
                activate(NQK + NV - 1)
                for u in range(NQK + NV, USES):
                    act.wait_ge(*use_ps.at(n, u + 1))
                    if u == NQK + NV:
                        act.wait_ge(*og_sb.at(n, 0))
                    k = 2 * (u - NQK - NV)
                    act.activation(gate[:].rearrange("p t v -> p (t v)")[:, k * 512:(k + 2) * 512],
                                   ps[:, 2 * (u % SLOTS):2 * (u % SLOTS) + 2, :].rearrange("p a i -> p (a i)"),
                                   ACT.Silu).then_inc(use_sb.sem, 1)
                act.wait_ge(*za_step.at(n, 22))
                act.activation(ex[:, DEC, :, :], za[:, 0, :].rearrange("p (t h) -> p t h", h=H), ACT.Exp).then_inc(ex_sb.sem, 1)
                act.wait_ge(*cum_ps.at(n, 1))
                act.activation(ex[:, PI:PI + 3, :, :].rearrange("p k t h -> p (k t h)"), ps[:, 7, 0:3 * GT * H], ACT.Exp)\
                    .then_inc(ex_sb.sem, 1)

                def heads(i):
                    return [(j, HG * i + j) for j in range(HG)]

                def tokens_first(t, i):
                    B = 4 * i
                    act.wait_ge(*kt_ps[i].at(n, t + 1))
                    act.wait_ge(*coef.at(n, 4 * t + 4))
                    act.wait_ge(*up_ps[i].at(n, t))
                    for j, h in heads(i):
                        e = act.activation(kd[:, h, :], ps[:, B, j * DK:(j + 1) * DK], ACT.Copy, scale=cf[:, KDF, h:h + 1])
                    e.then_inc(kd_sb[i].sem, 1)
                    act.wait_ge(*lx_ps[i].at(n, LEVELS * t))
                    act.wait_ge(*tt_ps[i].at(n, LEVELS * t))
                    act.activation(tm[:, HG * i:HG * i + HG, :], ident4[:], ACT.Copy).then_inc(tm_one[i].sem, 1)
                    act.wait_ge(*vt_ps[i].at(n, t + 1))
                    act.wait_ge(*delta_ps[i].at(n, t))
                    act.wait_ge(*om.at(n, 4 * t))
                    for j, h in heads(i):
                        e = act.activation(vr[:, h, :], ps[:, B + 1 + j // 2, j % 2 * DV:(j % 2 + 1) * DV], ACT.Copy,
                                           scale=ex[:, BETA, t, h:h + 1])
                    e.then_inc(vb_sb[i].sem, 1)

                def level_tt(t, i, m):
                    act.wait_ge(*tt_ps[i].at(n, LEVELS * t + m + 1))
                    if m == 0:
                        act.wait_ge(*delta_ps[i].at(n, t))
                    act.activation(tt[:, HG * i:HG * i + HG, :], ps[:, 4 * i + 1, :].rearrange("p (h k) -> p h k", k=P),
                                   ACT.Copy).then_inc(tt_sb[i].sem, 1)

                def solve(t, i):
                    act.wait_ge(*delta_ps[i].at(n, t + 1))
                    act.wait_ge(*up_ps[i].at(n, t))
                    act.activation(delta[:, HG * i:HG * i + HG, :].rearrange("p (a h) v -> p a (h v)", a=2),
                                   ps[:, 4 * i + 1:4 * i + 3, 0:2 * DV], ACT.Copy).then_inc(delta_sb[i].sem, 1)
                    act.wait_ge(*qs_ps[i].at(n, t + 1))
                    act.wait_ge(*ot_ps.at(n, 3 * t))
                    for j, h in heads(i):
                        e = act.activation(o[:, h, :], ps[:, 4 * i + 3 * (j // 2), j % 2 * DV:(j % 2 + 1) * DV], ACT.Copy,
                                           scale=ex[:, PI, t, h:h + 1])
                    e.then_inc(qs_sb[i].sem, 1)

                for t in range(GT):
                    for i in range(2):
                        tokens_first(t, i)
                    for m in range(LEVELS):
                        for i in range(2):
                            level_tt(t, i, m)
                    for i in range(2):
                        solve(t, i)
                    for i in range(2):
                        act.wait_ge(*o_sb[i].at(n, t + 1))
                        act.wait_ge(*delta_ps[i].at(n, t + 1))
                    act.activation(vr[:], o[:], ACT.Square).then_inc(osq.sem, 1)
                    for k in range(3):
                        act.wait_ge(*ot_ps.at(n, 3 * t + k + 1))
                        act.wait_ge(*y_ps.at(n, t))
                        act.activation(ot[:, 4 * k:4 * k + 4, :], ps[:, (1, 2, 5)[k], :].rearrange("p (m i) -> p m i", i=P),
                                       ACT.Copy).then_inc(ot_sb.sem, 1)

        @block.vector
        def _(dve):
            ph.start(dve, "dve")
            dve.memset(cf[:], 0.0).then_inc(seen, 1)
            dve.wait_ge(wts_loaded, LOADED)
            dve.tensor_tensor(wo[:], wo[:], onorm[:].unsqueeze(2).to_broadcast([P, NV, D]), ALU.mult)
            for wt in (wq, wk, wv, wg):
                dve.tensor_scalar(wt[:], wt[:], norm1[:], None, ALU.mult)
            dve.tensor_scalar(wba[:], wba[:], norm1[:], None, ALU.mult).then_inc(prepared, 1)
            dve.wait_ge(prepared, 2)
            dve.tensor_scalar(decay_rate[:], decay_rate[:], -1.0, None, ALU.mult).then_inc(prepared, 1)
            dve.wait_ge(prepared, 3)
            with dve.Fori(0, NB) as b:
                n0 = dve.snap(b * NG + 1)
                for i in range(2):
                    dve.wait_ge(*state_sb[i].at(n0, 0))
                dve.memset(state[:], 0.0).then_inc(zeroed.sem, 1)
                dve.wait_ge(*ht_halo.at(n0, 0))
                dve.memset(ht[:, 0:3], 0.0).then_inc(zeroed.sem, 1)
                with dve.Fori(0, NG) as g:
                    n = dve.snap(b * NG + g + 1)
                    dve.wait_ge(*x_loaded.at(n, 16))
                    for t in range(GT):
                        dve.bn_stats(stats[:, t, :], x[:, t, :]).then_inc(stats_done.sem, 1)
                    dve.wait_ge(*stats_done.at(n, GT))
                    dve.sem_inc(seen, 1)
                    for t in range(GT):
                        dve.bn_aggr(mv[:, t, :], stats[:, t, :]).then_inc(moments.sem, 1)
                    dve.wait_ge(*moments.at(n, GT))
                    dve.tensor_scalar(ms[:, 0, :], mv[:, :, 1], 1e-5, None, ALU.add).then_inc(root1.sem, 1)
                    dve.wait_ge(*root1_done.at(n, 1))
                    dve.tensor_tensor(ms[:, 1, :], rstd[:, 0, :], rstd[:, 0, :], ALU.mult).then_inc(root2.sem, 1)
                    for t in range(GT):
                        ln = dve.tensor_scalar(y[:, t, :], x[:, t, :], mv[:, t, 0:1], rstd[:, 0, t:t + 1], ALU.subtract, ALU.mult)
                    ln.then_inc(y_sb.sem, 1)
                    dve.wait_ge(*root2.at(n, 1))
                    dve.tensor_tensor(ms[:, 1, :], ms[:, 1, :], mv[:, :, 1], ALU.mult).then_inc(root2.sem, 1)
                    dve.wait_ge(*root2.at(n, 2))
                    dve.tensor_scalar(ms[:, 1, :], ms[:, 1, :], 1e-6, None, ALU.add).then_inc(root2.sem, 2)
                    dve.wait_ge(*root2_done.at(n, 1))
                    dve.wait_ge(*y_sb.at(n, 1))
                    dve.tensor_tensor(hn[:], y[:], rstd[:, 1, :].unsqueeze(2).to_broadcast([P, GT, D]), ALU.mult)\
                        .then_inc(hn_sb.sem, 1)

                    step = [0]

                    def then(ins):
                        step[0] += 1
                        ins.then_inc(za_step.sem, 1)
                        dve.wait_ge(*za_step.at(n, step[0]))

                    ba = ps[:, 6, 0:GT * 2 * H].rearrange("p (t r h) -> p r t h", t=GT, r=2)

                    def row(k):
                        return za[:, k, :]

                    def row3(k):
                        return za[:, k, :].rearrange("p (t h) -> p t h", h=H)

                    dve.wait_ge(*ba_ps.at(n, 1))
                    then(dve.tensor_copy(row3(1), ba[:, 0]))
                    then(dve.tensor_tensor(row3(2), ba[:, 1], dt_bias[:].unsqueeze(1).to_broadcast([P, GT, H]), ALU.add))
                    then(dve.tensor_scalar(row(3), row(2), -1.0, None, ALU.mult))
                    then(dve.tensor_tensor(row(3), row(3), row(2), ALU.min))
                    dve.wait_ge(*za_exp.at(n, 2))
                    then(dve.tensor_scalar(row(6), row(4), 2.0, None, ALU.add))
                    then(dve.reciprocal(row(6), row(6)))
                    then(dve.tensor_tensor(row(6), row(6), row(4), ALU.mult))
                    then(dve.tensor_tensor(row(7), row(6), row(6), ALU.mult))
                    then(dve.tensor_scalar(row(8), row(7), 1.0 / 17, None, ALU.mult))
                    for k in (15, 13, 11, 9, 7, 5, 3):
                        then(dve.scalar_tensor_tensor(out=row(8), in0=row(8), scalar=1.0 / k, in1=row(7), op0=ALU.add, op1=ALU.mult))
                    then(dve.scalar_tensor_tensor(out=row(8), in0=row(8), scalar=1.0, in1=row(6), op0=ALU.add, op1=ALU.mult))
                    then(dve.tensor_scalar(row(9), row(2), 0.0, None, ALU.max))
                    then(dve.scalar_tensor_tensor(out=row(9), in0=row(8), scalar=2.0, in1=row(9), op0=ALU.mult, op1=ALU.add))
                    then(dve.tensor_tensor(row3(9), row3(9), decay_rate[:].unsqueeze(1).to_broadcast([P, GT, H]), ALU.mult))
                    then(dve.tensor_scalar(row(5), row(5), 1.0, None, ALU.add))
                    for i in range(2):
                        dve.wait_ge(*vb_sb[i].at(n, 0))
                        dve.wait_ge(*dec_ps[i].at(n, 0))
                    dve.wait_ge(*cum_ps.at(n, 0))
                    dve.tensor_scalar(row(0), row(9), -1e4, None, ALU.max)
                    dve.reciprocal(ex[:, BETA, :, :], row3(5)).then_inc(za_step.sem, 1)

                    for u in range(NQK + NV):
                        M, k = (DK if u < NQK else P), u % SLOTS
                        wts = conv_qk[:, u // 2, u % 2, :] if u < NQK else conv_v[:, u - NQK, :]
                        dve.wait_ge(*use_sb.at(n, u + 1))
                        for i in range(1, 4):
                            if i > 1:
                                dve.wait_ge(*tap.at(n, 3 * u + i - 1))
                            dve.scalar_tensor_tensor(out=conv[0:M, k, :], in0=raw[0:M, k, i:i + G], scalar=wts[:, i:i + 1],
                                                     in1=conv[0:M, k, :], op0=ALU.mult, op1=ALU.add).then_inc(tap.sem, 1)
                    dve.wait_ge(*use_ps.at(n, USES))
                    dve.tensor_copy(ht[:, 0:3], ht[:, G:G + 3]).then_inc(ht_halo.sem, 1)
                    dve.wait_ge(*ex_sb.at(n, 2))
                    dve.tensor_scalar(ex[:, DCUT, :, :], ex[:, DEC, :, :], not_first[:], None, ALU.mult).then_inc(decay_cut.sem, 1)

                    def heads(i):
                        return [(j, HG * i + j) for j in range(HG)]

                    def decays(t, i):
                        dve.wait_ge(*dec_ps[i].at(n, t + 1))
                        dve.tensor_tensor_scan(gd[:, HG * i:HG * i + HG, :].rearrange("p h k -> p (h k)"), ps[:, 4 * i, :],
                                               ident4[:].rearrange("p h k -> p (h k)"), 0.0, ALU.mult, ALU.add)\
                            .then_inc(gd_sb[i].sem, 1)

                    def norms(t):
                        dve.wait_ge(*n2_ps.at(n, t + 1))
                        dve.wait_ge(*rn_sb.at(n, t))
                        dve.tensor_scalar(cf[:, N2E, :], ps[:, 0, 0:2 * H], 1e-6, None, ALU.add).then_inc(n2_sb.sem, 1)
                        dve.wait_ge(*rn_sb.at(n, t + 1))
                        rk = cf[:, RN, :].rearrange("p (h r) -> p h r", r=2)[:, :, 1]
                        rq = cf[:, RN, :].rearrange("p (h r) -> p h r", r=2)[:, :, 0]
                        dve.tensor_tensor(cf[:, BRK, 0:H], rk, ex[:, BETA, t, :], ALU.mult).then_inc(coef.sem, 1)
                        dve.tensor_tensor(cf[:, KDF, 0:H], rk, ex[:, DLAST, t, :], ALU.mult)
                        dve.tensor_scalar(cf[:, RQS, 0:H], rq, DK ** -0.5, None, ALU.mult).then_inc(coef.sem, 1)
                        dve.wait_ge(*coef.at(n, 4 * t + 1))
                        dve.scalar_tensor_tensor(out=cf[:, NPB, 0:H], in0=cf[:, BRK, 0:H], scalar=-1.0, in1=ex[:, PI, t, :],
                                                 op0=ALU.mult, op1=ALU.mult).then_inc(coef.sem, 1)
                        dve.wait_ge(*coef.at(n, 4 * t + 2))
                        dve.tensor_tensor(cf[:, RQ2, 0:H], cf[:, RQS, 0:H], cf[:, RQS, 0:H], ALU.mult).then_inc(coef.sem, 1)
                        dve.wait_ge(*coef.at(n, 4 * t + 4))

                    def products(t, i):
                        dve.wait_ge(*kq_ps[i].at(n, t + 1))
                        dve.wait_ge(*gd_sb[i].at(n, t + 1))
                        for j, h in heads(i):
                            qk_ps = ps[:, 4 * i + 1 + j // 2, j % 2 * 2 * P:(j % 2 + 1) * 2 * P].rearrange("p (r k) -> p r k", r=2)
                            rk = cf[:, RN, 2 * h + 1:2 * h + 2]
                            e = dve.scalar_tensor_tensor(out=al[:, h, :, :], in0=qk_ps, scalar=rk,
                                                         in1=gd[:, h, :].unsqueeze(1).to_broadcast([P, 2, P]),
                                                         op0=ALU.mult, op1=ALU.mult)
                        e.then_inc(al_sb[i].sem, 1)

                    def level_am(t, i, m):
                        dve.wait_ge(*lx_ps[i].at(n, LEVELS * t + m + 1))
                        for j, h in heads(i):
                            if m == 0:
                                lx = left(ps[:, 4 * i + 3, j * P:(j + 1) * P], 0)
                                e = dve.scalar_tensor_tensor(out=am[:, h, :].unsqueeze(2), in0=lx, scalar=cf[:, BRK, h:h + 1],
                                                             in1=blocks[:, 0, :].unsqueeze(2), op0=ALU.mult, op1=ALU.mult)
                            else:
                                lx = ps[:, 4 * i + 3, j * 64:(j + 1) * 64]
                                e = dve.scalar_tensor_tensor(out=am[:, h, :], in0=lx, scalar=cf[:, BRK, h:h + 1],
                                                             in1=blocks[:, m, :], op0=ALU.mult, op1=ALU.mult)
                        e.then_inc(am_sb[i].sem, 1)

                    def level_tm(t, i, m):
                        half = left4(tm[:, HG * i:HG * i + HG, :], m)
                        if m == 0:
                            dve.wait_ge(*tm_one[i].at(n, t + 1))
                            dve.wait_ge(*am_sb[i].at(n, LEVELS * t + 1))
                            more = am[:, HG * i:HG * i + HG, :].rearrange("p h (n s) -> p h n s", s=1)
                        else:
                            dve.wait_ge(*ty_ps[i].at(n, (LEVELS - 1) * t + m))
                            dve.wait_ge(*tm_sb[i].at(n, LEVELS * t + m))
                            more = ps[:, 4 * i + 2, 0:HG * 64].rearrange("p (h n s) -> p h n s", h=HG, s=1 << m)
                        dve.tensor_tensor(half, half, more, ALU.add).then_inc(tm_sb[i].sem, 1)

                    def rest(t, i):
                        dve.wait_ge(*ks_ps[i].at(n, t + 1))
                        dve.wait_ge(*vb_sb[i].at(n, t + 1))
                        for j, h in heads(i):
                            e = dve.scalar_tensor_tensor(out=vr[:, h, :],
                                                         in0=ps[:, 4 * i + 3 * (j // 2), j % 2 * DV:(j % 2 + 1) * DV],
                                                         scalar=cf[:, NPB, h:h + 1], in1=vr[:, h, :], op0=ALU.mult, op1=ALU.add)
                        e.then_inc(r_sb[i].sem, 1)

                    def outputs(t, i):
                        dve.wait_ge(*ad_ps[i].at(n, t + 1))
                        dve.wait_ge(*qs_sb[i].at(n, t + 1))
                        mine = o[:, HG * i:HG * i + HG, :].rearrange("p (a h) v -> p a (h v)", a=2)
                        dve.tensor_tensor(mine, mine, ps[:, 4 * i + 1:4 * i + 3, 0:2 * DV], ALU.add).then_inc(o_sb[i].sem, 1)
                        dve.wait_ge(*up_ps[i].at(n, t + 1))
                        dve.wait_ge(*qs_ps[i].at(n, t + 1))
                        dve.wait_ge(*state_sb[i].at(n, t))
                        dve.wait_ge(*zeroed.at(b + 1, 2))
                        for j, h in heads(i):
                            e = dve.scalar_tensor_tensor(out=state[:, h, :], in0=state[:, h, :], scalar=ex[0:DK, PLAST, t, h:h + 1],
                                                         in1=ps[0:DK, 4 * i + 3 * (j // 2), j % 2 * DV:(j % 2 + 1) * DV],
                                                         op0=ALU.mult, op1=ALU.add)
                        e.then_inc(state_sb[i].sem, 1)

                    def gated_norm(t):
                        dve.wait_ge(*osq.at(n, t + 1))
                        dve.tensor_reduce(cf[:, OSUM, 0:H], vr[:], AX.X, ALU.add).then_inc(om.sem, 1)
                        dve.wait_ge(*om.at(n, 4 * t + 1))
                        dve.scalar_tensor_tensor(out=cf[:, OMS, 0:H], in0=cf[:, OSUM, 0:H], scalar=1.0 / DV,
                                                 in1=cf[:, RQ2, 0:H], op0=ALU.mult, op1=ALU.mult).then_inc(om.sem, 1)
                        dve.wait_ge(*om.at(n, 4 * t + 2))
                        dve.tensor_scalar(cf[:, OME, 0:H], cf[:, OMS, 0:H], 1e-6, None, ALU.add).then_inc(om.sem, 1)
                        dve.wait_ge(*orn.at(n, t + 1))
                        dve.tensor_tensor(cf[:, OF, 0:H], cf[:, ORN, 0:H], cf[:, RQS, 0:H], ALU.mult).then_inc(om.sem, 1)
                        dve.wait_ge(*om.at(n, 4 * t + 4))
                        for h in range(H):
                            e = dve.scalar_tensor_tensor(out=o[:, h, :], in0=o[:, h, :], scalar=cf[:, OF, h:h + 1],
                                                         in1=gate[:, t, h * DV:(h + 1) * DV], op0=ALU.mult, op1=ALU.mult)
                        e.then_inc(og_sb.sem, 1)

                    def add_out(t):
                        dve.wait_ge(*y_ps.at(n, t + 1))
                        if t == 0:
                            dve.wait_ge(*stored.at(n, 0))
                        dve.tensor_tensor(out[:, t, :], ps[:, 6, 0:D], y[:, t, :], ALU.add).then_inc(out_sb.sem, 1)

                    for t in range(GT):
                        for i in range(2):
                            decays(t, i)
                        norms(t)
                        for i in range(2):
                            products(t, i)
                        for m in range(LEVELS):
                            for i in range(2):
                                level_am(t, i, m)
                            for i in range(2):
                                level_tm(t, i, m)
                        for i in range(2):
                            rest(t, i)
                        for i in range(2):
                            outputs(t, i)
                        gated_norm(t)
                        add_out(t)
    ph.close()


def gated_mlp(nc, name, src, dst, c, hidden, func, layernorm, eps, w_up, w_gate, w_down, norm_w, norm_b=None,
              b_up=None, b_gate=None, b_down=None, shifted=False, skip=None):
    chunks = [(a, min(P, hidden - a)) for a in range(0, hidden, P)]
    NC = len(chunks)
    biased = b_up is not None
    extra = int(biased)
    assert not biased or chunks[-1][1] < P
    ph = Phase(nc, name)
    sb, signal = ph.sb, ph.counter
    ps = ph.banks()
    up_w = sb("up_w", [P, hidden])
    gate_w = sb("gate_w", [P, hidden])
    down_w = sb("down_w", [P, NC, D])
    scale = sb("scale", [P, 1])
    shift = sb("shift", [P, 1])
    up_b = sb("up_b", [P, NC])
    gate_b = sb("gate_b", [P, NC])
    ident = sb("ident", [P, P])
    minus_half = sb("minus_half", [P, GT])
    h = sb("h", [P, GT, D])
    x = sb("x", [P, GT, D])
    x2 = sb("x2", [P, GT, D])
    y = sb("y", [P, GT, D])
    stats = sb("stats", [P, GT, 6])
    mv = sb("mv", [P, GT, 2])
    ms = sb("ms", [P, 2, GT])
    rstd = sb("rstd", [P, GT])
    hn = sb("hn", [P, GT, D])
    ht = sb("ht", [P, G])
    gate = sb("gate", [P, 2, G])
    prod = sb("prod", [P, NC, G])

    loaded = ph.semaphore("loaded")
    prepared = ph.semaphore("prepared")
    NH = 2 if shifted else 1
    NX = 2 if skip is not None else 1
    h_loaded = signal("h_loaded", 16 * NH, "sp")
    x_loaded = signal("x_loaded", 16 * NX, "sp")
    stored = signal("stored", 16, "sp")
    stats_done = signal("stats_done", GT, "dve")
    seen = signal("seen", 1, "dve").sem
    moments = signal("moments", GT, "dve")
    under_root = signal("under_root", 3, "dve")
    root = signal("root", 1, "pool")
    normed = signal("normed", GT, "dve")
    ht_ps = signal("ht_ps", 1, "pe")
    ht_sb = signal("ht_sb", 1, "act")
    up_gate_ps = signal("up_gate_ps", NC, "pe")
    gated = signal("gated", NC, "act")
    prod_sb = signal("prod_sb", NC, "dve")
    y_ps = signal("y_ps", 1, "pe")
    y_sb = signal("y_sb", NX, "dve")

    loads = [(up_w[:], w_up), (gate_w[:], w_gate), (ident[:], c["ident"]), (minus_half[:], c["minus_half"][:, 0:GT]),
             (scale[:], norm_w)]
    for n, (a, m) in enumerate(chunks):
        loads.append((down_w[0:m, n, :], w_down(a, m)))
        if biased:
            loads += [(up_b[0:m, n:n + 1], b_up(a, m)), (gate_b[0:m, n:n + 1], b_gate(a, m))]
    if biased:
        loads += [(shift[:], norm_b), (down_w[chunks[-1][1]:chunks[-1][1] + 1, NC - 1, :], b_down)]

    with nc.Block() as block:

        @block.sync
        def _(sp):
            ph.start(sp, "sp")
            for out, in_ in loads:
                sp.dma_start(out, in_).then_inc(loaded, 16)
            with sp.Fori(0, NB) as b, sp.Fori(0, NG) as g:
                n = sp.snap(b * NG + g + 1)
                row = sp.snap(scratch_row(b, g))
                sp.wait_ge(*normed.at(n, 0))
                if shifted:
                    sp.dma_start(h[:, :, 0:D // 2], tiles(src[bass.ds(row, G), 0:D // 2])).then_inc(h_loaded.sem, 16)
                    sp.dma_start(h[:, :, D // 2:D], tiles(src[bass.ds(row - 1, G), D // 2:D])).then_inc(h_loaded.sem, 16)
                else:
                    sp.dma_start(h[:], tiles(src[bass.ds(row, G), :])).then_inc(h_loaded.sem, 16)
                sp.wait_ge(*y_sb.at(n, 0))
                sp.dma_start(x[:], tiles(src[bass.ds(row, G), :])).then_inc(x_loaded.sem, 16)
                if skip is not None:
                    sp.dma_start(x2[:], tiles(skip[bass.ds((b * NG + g) * G, G), :])).then_inc(x_loaded.sem, 16)
                sp.wait_ge(*y_sb.at(n, NX))
                sp.dma_start(tiles(dst[bass.ds(row, G), :]), y[:]).then_inc(stored.sem, 16)
            sp.wait_ge(*stored.at(TURNS + 1, 0))

        @block.gpsimd
        def _(pool):
            ph.start(pool, "pool")
            pool.memset(prod[:, NC - 1, :], 1.0).then_inc(prepared, 1)
            pool.wait_ge(loaded, 16 * len(loads))
            with pool.Fori(0, NB) as b, pool.Fori(0, NG) as g:
                n = pool.snap(b * NG + g + 1)
                pool.wait_ge(*under_root.at(n, 3))
                pool.wait_ge(*normed.at(n, 0))
                pool.tensor_tensor(rstd[:], ms[:, 1, :], minus_half[:], ALU.pow).then_inc(root.sem, 1)

        @block.tensor
        def _(pe):
            ph.start(pe, "pe")
            pe.wait_ge(loaded, 16 * len(loads))
            pe.wait_ge(prepared, 1)
            with pe.Fori(0, NB) as b, pe.Fori(0, NG) as g:
                n = pe.snap(b * NG + g + 1)
                for t in range(GT):
                    pe.wait_ge(*normed.at(n, t + 1))
                    mm = pe.transpose(ps[:, 0, t * P:(t + 1) * P], hn[:, t, :], ident[:])
                mm.then_inc(ht_ps.sem, 1)
                pe.wait_ge(*ht_sb.at(n, 1))
                for i, (a, m) in enumerate(chunks):
                    pe.wait_ge(*prod_sb.at(n, freed(i, 3, NC)))
                    pe.matmul(ps[0:m, 1 + 2 * (i % 3), :], gate_w[:, a:a + m], ht[:], start=True, stop=True)
                    pe.matmul(ps[0:m, 2 + 2 * (i % 3), :], up_w[:, a:a + m], ht[:], start=True, stop=True)\
                        .then_inc(up_gate_ps.sem, 1)
                pe.wait_ge(*prod_sb.at(n, NC))
                pe.wait_ge(*y_sb.at(n, 0))
                for t in range(GT):
                    for i, (a, m) in enumerate(chunks):
                        k = m + (extra if i == NC - 1 else 0)
                        mm = pe.matmul(ps[:, 7, t * P:(t + 1) * P], prod[0:k, i, t * P:(t + 1) * P], down_w[0:k, i, :],
                                       start=i == 0, stop=i == NC - 1)
                mm.then_inc(y_ps.sem, 1)

        @block.scalar
        def _(act):
            ph.start(act, "act")
            act.wait_ge(loaded, 16 * len(loads))
            with act.Fori(0, NB) as b, act.Fori(0, NG) as g:
                n = act.snap(b * NG + g + 1)
                act.wait_ge(*ht_ps.at(n, 1))
                act.wait_ge(*up_gate_ps.at(n, 0))
                act.activation(ht[:], ps[:, 0, :], ACT.Identity, scale=scale[:],
                               bias=shift[:] if biased else 0.0).then_inc(ht_sb.sem, 1)
                for i, (a, m) in enumerate(chunks):
                    act.wait_ge(*up_gate_ps.at(n, i + 1))
                    act.wait_ge(*prod_sb.at(n, freed(i, 2, NC)))
                    act.activation(gate[0:m, i % 2, :], ps[0:m, 1 + 2 * (i % 3), :], func,
                                   bias=gate_b[0:m, i:i + 1] if biased else 0.0).then_inc(gated.sem, 1)

        @block.vector
        def _(dve):
            ph.start(dve, "dve")
            dve.wait_ge(loaded, 16 * len(loads))
            dve.wait_ge(prepared, 1)
            with dve.Fori(0, NB) as b, dve.Fori(0, NG) as g:
                n = dve.snap(b * NG + g + 1)
                dve.wait_ge(*h_loaded.at(n, 16 * NH))
                for t in range(GT):
                    dve.bn_stats(stats[:, t, :], h[:, t, :]).then_inc(stats_done.sem, 1)
                dve.wait_ge(*stats_done.at(n, GT))
                dve.sem_inc(seen, 1)
                for t in range(GT):
                    dve.bn_aggr(mv[:, t, :], stats[:, t, :]).then_inc(moments.sem, 1)
                dve.wait_ge(*moments.at(n, GT))
                if layernorm:
                    dve.tensor_scalar(ms[:, 1, :], mv[:, :, 1], eps, None, ALU.add).then_inc(under_root.sem, 3)
                else:
                    dve.tensor_tensor(ms[:, 0, :], mv[:, :, 0], mv[:, :, 0], ALU.mult).then_inc(under_root.sem, 1)
                    dve.wait_ge(*under_root.at(n, 1))
                    dve.tensor_tensor(ms[:, 0, :], ms[:, 0, :], mv[:, :, 1], ALU.add).then_inc(under_root.sem, 1)
                    dve.wait_ge(*under_root.at(n, 2))
                    dve.tensor_scalar(ms[:, 1, :], ms[:, 0, :], eps, None, ALU.add).then_inc(under_root.sem, 1)
                dve.wait_ge(*root.at(n, 1))
                dve.wait_ge(*ht_ps.at(n, 0))
                for t in range(GT):
                    if layernorm:
                        dve.tensor_scalar(hn[:, t, :], h[:, t, :], mv[:, t, 0:1], rstd[:, t:t + 1], ALU.subtract, ALU.mult)\
                            .then_inc(normed.sem, 1)
                    else:
                        dve.tensor_scalar(hn[:, t, :], h[:, t, :], rstd[:, t:t + 1], None, ALU.mult)\
                            .then_inc(normed.sem, 1)
                for i, (a, m) in enumerate(chunks):
                    dve.wait_ge(*gated.at(n, i + 1))
                    if i == 0:
                        dve.wait_ge(*y_ps.at(n, 0))
                    up = ps[0:m, 2 + 2 * (i % 3), :]
                    if biased:
                        dve.scalar_tensor_tensor(out=prod[0:m, i, :], in0=up, scalar=up_b[0:m, i:i + 1],
                                                 in1=gate[0:m, i % 2, :], op0=ALU.add, op1=ALU.mult).then_inc(prod_sb.sem, 1)
                    else:
                        dve.tensor_tensor(prod[0:m, i, :], up, gate[0:m, i % 2, :], ALU.mult).then_inc(prod_sb.sem, 1)
                dve.wait_ge(*x_loaded.at(n, 16 * NX))
                dve.wait_ge(*stored.at(n, 0))
                dve.wait_ge(*y_ps.at(n, 1))
                dve.tensor_tensor(y[:], ps[:, 7, :].rearrange("p (t d) -> p t d", d=D), x[:], ALU.add).then_inc(y_sb.sem, 1)
                if skip is not None:
                    dve.wait_ge(*y_sb.at(n, 1))
                    dve.tensor_tensor(y[:], y[:], x2[:], ALU.add).then_inc(y_sb.sem, 1)
    ph.close()


def add_and_norm(nc, name, a, b_, x_out, y_out, c):
    ph = Phase(nc, name)
    sb, signal = ph.sb, ph.counter
    minus_half = sb("minus_half", [P, GT])
    x = sb("x", [P, GT, D])
    more = sb("more", [P, GT, D])
    total = sb("total", [P, GT, D])
    y = sb("y", [P, GT, D])
    stats = sb("stats", [P, GT, 6])
    mv = sb("mv", [P, GT, 2])
    var = sb("var", [P, GT])
    rstd = sb("rstd", [P, GT])
    const_loaded = ph.semaphore("const_loaded")
    N_IN = 1 + (b_ is not None)
    N_OUT = (x_out is not None) + (y_out is not None)
    loaded = signal("loaded", 16 * N_IN, "sp")
    stored = signal("stored", 16 * N_OUT, "sp")
    added = signal("added", 1, "dve")
    stats_done = signal("stats_done", GT, "dve")
    seen = signal("seen", 1, "dve").sem
    moments = signal("moments", GT, "dve")
    under_root = signal("under_root", 1, "dve")
    root = signal("root", 1, "pool")
    normed = signal("normed", GT, "dve")

    with nc.Block() as block:

        @block.sync
        def _(sp):
            ph.start(sp, "sp")
            sp.dma_start(minus_half[:], c["minus_half"][:, 0:GT]).then_inc(const_loaded, 16)
            with sp.Fori(0, NB) as b, sp.Fori(0, NG) as g:
                n = sp.snap(b * NG + g + 1)
                sp.wait_ge(*added.at(n, 0))
                sp.dma_start(x[:], tiles(a[0][bass.ds(a[1](b, g), G), :])).then_inc(loaded.sem, 16)
                if b_ is not None:
                    sp.dma_start(more[:], tiles(b_[0][bass.ds(b_[1](b, g), G), :])).then_inc(loaded.sem, 16)
                sp.wait_ge(*added.at(n, 1))
                if x_out is not None:
                    sp.dma_start(tiles(x_out[0][bass.ds(x_out[1](b, g), G), :]), total[:]).then_inc(stored.sem, 16)
                if y_out is not None:
                    sp.wait_ge(*normed.at(n, GT))
                    sp.dma_start(tiles(y_out[0][bass.ds(y_out[1](b, g), G), :]), y[:]).then_inc(stored.sem, 16)
            sp.wait_ge(*stored.at(TURNS + 1, 0))

        @block.gpsimd
        def _(pool):
            ph.start(pool, "pool")
            pool.wait_ge(const_loaded, 16)
            if y_out is not None:
                with pool.Fori(0, NB) as b, pool.Fori(0, NG) as g:
                    n = pool.snap(b * NG + g + 1)
                    pool.wait_ge(*under_root.at(n, 1))
                    pool.tensor_tensor(rstd[:], var[:], minus_half[:], ALU.pow).then_inc(root.sem, 1)

        @block.vector
        def _(dve):
            ph.start(dve, "dve")
            with dve.Fori(0, NB) as b, dve.Fori(0, NG) as g:
                n = dve.snap(b * NG + g + 1)
                dve.wait_ge(*loaded.at(n, 16 * N_IN))
                dve.wait_ge(*stored.at(n, 0))
                if b_ is not None:
                    dve.tensor_tensor(total[:], x[:], more[:], ALU.add).then_inc(added.sem, 1)
                else:
                    dve.tensor_copy(total[:], x[:]).then_inc(added.sem, 1)
                if y_out is not None:
                    dve.wait_ge(*added.at(n, 1))
                    for t in range(GT):
                        dve.bn_stats(stats[:, t, :], total[:, t, :]).then_inc(stats_done.sem, 1)
                    dve.wait_ge(*stats_done.at(n, GT))
                    dve.sem_inc(seen, 1)
                    for t in range(GT):
                        dve.bn_aggr(mv[:, t, :], stats[:, t, :]).then_inc(moments.sem, 1)
                    dve.wait_ge(*moments.at(n, GT))
                    dve.tensor_scalar(var[:], mv[:, :, 1], 1e-5, None, ALU.add).then_inc(under_root.sem, 1)
                    dve.wait_ge(*root.at(n, 1))
                    for t in range(GT):
                        dve.tensor_scalar(y[:, t, :], total[:, t, :], mv[:, t, 0:1], rstd[:, t:t + 1],
                                          ALU.subtract, ALU.mult).then_inc(normed.sem, 1)
    ph.close()


def token_row(b, g):
    return (b * NG + g) * G


def clear_padding(nc, arrays, c):
    ph = Phase(nc, "padding")
    cleared = ph.semaphore("cleared")
    with nc.Block() as block:
        @block.sync
        def _(sp):
            for a in arrays:
                sp.dma_start(a.rearrange("(b r) c -> b r c", b=NB)[:, PAD - 1, :], c["zero_rows"]).then_inc(cleared, 16)
            sp.wait_ge(cleared, 16 * len(arrays))
    ph.close()


def ffn_block(nc, name, y0, y1, w, c):
    HID = w["w2"].shape[0] // DEPTH
    with nc.Fori(0, DEPTH) as l:
        local_attention(nc, name + "a", y0, y1, l, w, c)
        gated_mlp(nc, name + "m", y1, y0, c, HID, ACT.Gelu, True, 1e-5,
                  w_up=w["w1"][bass.ds(l * D, D), 0:HID], w_gate=w["w1"][bass.ds(l * D, D), HID:2 * HID],
                  w_down=lambda a, m: w["w2"][bass.ds(l * HID + a, m), :],
                  norm_w=w["ln_g"][bass.ds(l * D, D), :], norm_b=w["ln_b"][bass.ds(l * D, D), :],
                  b_up=lambda a, m: w["b1"][bass.ds(l * 2 * HID + a, m), :],
                  b_gate=lambda a, m: w["b1"][bass.ds(l * 2 * HID + HID + a, m), :],
                  b_down=w["b2"][bass.ds(l, 1), :], shifted=True)


def hybrid_block(nc, x, a, b, f, c, out):
    def scratch(name):
        return nc.dram_tensor(name, (NB * ROWS, D), F32).ap()
    x1, x2, x3, y0, y1 = (scratch(n) for n in ("x1", "x2", "x3", "y0", "y1"))
    clear_padding(nc, (y0, y1), c)
    delta_attention(nc, "delta", x, y0, a, c)
    gated_mlp(nc, "mlp", y0, x1, c, a["Wup"].shape[1], ACT.Silu, False, 1e-6, w_up=a["Wup"], w_gate=a["Wgate"],
              w_down=lambda r, m: a["Wdown"][r:r + m, :], norm_w=a["norm2_w"], skip=x)
    add_and_norm(nc, "norm_a", (x1, scratch_row), None, None, (y0, scratch_row), c)
    ffn_block(nc, "f", y0, y1, f, c)
    add_and_norm(nc, "norm_b", (x1, scratch_row), (y0, scratch_row), (x2, scratch_row), (y1, scratch_row), c)
    window_attention(nc, "window", y1, x2, x3, b, c)
    add_and_norm(nc, "norm_c", (x3, scratch_row), None, None, (y0, scratch_row), c)
    ffn_block(nc, "g", y0, y1, f, c)
    add_and_norm(nc, "last", (x3, scratch_row), (y0, scratch_row), (out, token_row), None, c)



def shape_constants():
    import numpy as np

    T, P, W, DH = 1024, 128, 64, 64
    c = {"ident": np.eye(P, dtype=np.float32)}
    c["minus_half"] = np.full((P, 64), -0.5, np.float32)
    c["own_head"] = (np.arange(P)[:, None] // 8 % 4 == np.arange(4)[None, :]).astype(np.float32)
    i = np.arange(P)
    c["sums"] = np.concatenate([i[:, None] <= i, np.ones((P, P)), i[:, None] > i], 1).astype(np.float32)
    c["not_first"] = (i[:, None] > 0).astype(np.float32)
    levels = []
    for m in range(7):
        s = 1 << m
        cols = i[i // s % 2 == 0]
        levels.append(-((i[:, None] // s % 2 == 1) & (i[:, None] // (2 * s) == cols // (2 * s))).astype(np.float32))
    c["blocks"] = np.concatenate(levels, 1)
    c["zero_rows"] = np.zeros((4, 128), np.float32)
    q = np.arange(P)[:, None]
    k = np.arange(W + P)[None, :]
    for name, first in (("ffn_mask", q), ("attn_mask", q + 1)):
        seen = (k >= first) & (k <= q + W)
        edge = seen & (k >= W)
        m = np.where(np.stack([edge, edge, seen, seen], 1), 0.0, -1e30)
        c[name] = np.ascontiguousarray(m.reshape(P, 4 * (W + P)).astype(np.float32))
    half = np.arange(0, DH, 2, dtype=np.float32)
    inv_freq = (1.0 / 10000.0 ** (half / DH)).astype(np.float32)
    t = np.arange(T, dtype=np.float32)
    f = (t[:, None] * inv_freq[None, :]).astype(np.float32)
    f = np.concatenate([f, f], 1)
    base = ((half + 0.4 * DH) / (1.4 * DH)).astype(np.float32)
    s = (base[None, :] ** ((t - T // 2) / float(W // 2))[:, None]).astype(np.float32)
    s = np.concatenate([s, s], 1)
    sign = np.where(np.arange(DH) < DH // 2, -1.0, 1.0).astype(np.float32)
    cos, sin = np.cos(f), np.sin(f) * sign
    r = np.stack([cos * s * 8.0, sin * s * 8.0, cos / s, sin / s]).astype(np.float32)
    c["rotation"] = np.ascontiguousarray(r.reshape(4, T // P, P, DH).transpose(2, 0, 1, 3).reshape(P, 4 * (T // P) * DH))
    return c


def kernel(**inputs):
    import numpy as np
    import concourse.bacc as bacc
    from concourse import mybir as mb
    from concourse.bass_utils import run_bass_kernel_spmd

    nc = bacc.Bacc("TRN2", target_bir_lowering=False, num_devices=1)
    arrays = {}

    def give(name, array):
        arrays[name] = np.ascontiguousarray(array)
        return nc.dram_tensor(name, arrays[name].shape, mb.dt.from_np(arrays[name].dtype), kind="ExternalInput").ap()

    def group(prefix):
        given = {}
        for name, array in inputs.items():
            if name.startswith(prefix) and not name.endswith("_x"):
                key, array = name[len(prefix):], np.asarray(array)
                if prefix == "L0_attn_b_" and key.startswith("W"):
                    array = array.T
                elif key in ("A_log", "dt_bias", "bo"):
                    array = array.reshape(1, -1)
                elif array.ndim == 1 or key in ("ln_g", "ln_b", "b1"):
                    array = array.reshape(-1, 1)
                elif array.ndim == 3:
                    array = array.reshape(-1, array.shape[-1])
                given[key] = give(name, array)
        return given

    x = np.asarray(inputs["L0_attn_a_x"])
    shape = x.shape
    x = give("x", x.reshape(-1, shape[-1]))
    a, b, f = (group(p) for p in ("L0_attn_a_", "L0_attn_b_", "L0_ffn_"))
    c = {name: give("const_" + name, array) for name, array in shape_constants().items()}
    out = nc.dram_tensor("out", (shape[0] * shape[1], shape[2]), mb.dt.float32, kind="ExternalOutput").ap()
    hybrid_block(nc, x, a, b, f, c, out)
    r = run_bass_kernel_spmd(nc, [arrays], core_ids=[0])
    return r.results[0]["out"].reshape(shape)
```

```python
from contextlib import ExitStack, contextmanager

import concourse.bass as bass
from concourse import mybir

F32 = mybir.dt.float32
BF16 = mybir.dt.bfloat16
ALU = mybir.AluOpType
ACT = mybir.ActivationFunctionType
AX = mybir.AxisListType

P = 128
NB, T, D = 4, 1024, 128
GT = 4
G = GT * P
NG = T // G
TURNS = NB * NG
PAD = P
ROWS = PAD + T
DEPTH = 2


class Signal:

    def __init__(self, sem, per):
        self.sem = sem
        self.per = per

    def at(self, n, k):
        return self.sem, n * self.per + k


class Phase:

    def __init__(self, nc, name):
        self.nc, self.name, self.stack, self.counters, self.sems = nc, name, ExitStack(), [], []

    def sb(self, name, shape, dt=F32):
        return self.stack.enter_context(self.nc.sbuf_tensor(f"{self.name}_{name}", shape, dt))

    def banks(self):
        return self.stack.enter_context(self.nc.psum_tensor(f"{self.name}_ps", [P, 8, 512], F32))

    def semaphore(self, name):
        self.sems.append(self.stack.enter_context(self.nc.semaphore(f"{self.name}_{name}")))
        return self.sems[-1]

    def counter(self, name, per, owner):
        s = Signal(self.semaphore(name), per)
        self.counters.append((s, owner))
        return s

    def start(self, eng, owner):
        for s, o in self.counters:
            if o == owner:
                eng.sem_inc(s.sem, s.per)

    def close(self):
        for sem in self.sems:
            self.nc.gpsimd.sem_clear(sem)
        self.nc.all_engine_barrier()
        self.stack.close()


def freed(i, slots, total):
    if i >= slots:
        return i - slots + 1
    return max(j for j in range(total) if j % slots == i % slots) + 1 - total


def scratch_row(b, g):
    return b * ROWS + PAD + g * G


def tiles(rows):
    return rows.rearrange("(n p) c -> p n c", p=P)


def local_attention(nc, name, src, dst, l, w, c):
    H, DH, W = 8, 64, 64
    INNER = H * DH
    KEYS = W + P
    PAIRS = H // 2
    NT = T // P
    assert NG == 2 and GT % 2 == 0
    ph = Phase(nc, name)
    sb, signal = ph.sb, ph.counter
    ps = ph.banks()
    wqkv = sb("wqkv", [P, 3 * INNER])
    wo = sb("wo", [P, 4, D])
    ident = sb("ident", [P, P])
    identb = sb("identb", [P, P], BF16)
    mask = sb("mask", [P, 2, 2, KEYS])
    maskb = sb("maskb", [P, 2, 2, KEYS], BF16)
    scales = sb("scales", [P, 4, DH])
    table = sb("table", [P, 4, NT, DH])
    h = sb("h", [P, GT, D])
    x = sb("x", [P, GT, D])
    y = sb("y", [P, GT, D])
    ht = sb("ht", [P, G])
    raw = sb("raw", [P, 2, H, DH])
    sq = sb("sq", [P, 2, H, DH])
    ss = sb("ss", [P, 2, 2 * H])
    minus_half = sb("minus_half", [P, 2 * H])
    rn = sb("rn", [P, 2 * H])
    rot_c = sb("rot_c", [P, 2, H, DH])
    rot_s = sb("rot_s", [P, 2, H, DH])
    rot = sb("rot", [P, 2, H, DH])
    qk = sb("qk", [P, 2 * H, DH])
    qt = sb("qt", [P, 2, PAIRS, P])
    kt = sb("kt", [P, PAIRS, W + G])
    v = sb("v", [P, NT, H, DH])
    nmx = sb("nmx", [P, H])
    rowsum = sb("rowsum", [P, 2, H])
    pr = sb("pr", [P, H, 2 * P])
    pt = sb("pt", [P, H, 2, P])
    rs = sb("rs", [P, H])
    o = sb("o", [P, H, DH])
    ot = sb("ot", [P, 4, P])

    wts_loaded = ph.semaphore("wts_loaded")
    prepared = ph.semaphore("prepared")
    h_loaded = signal("h_loaded", 32, "sp")
    x_loaded = signal("x_loaded", 16, "sp")
    stored = signal("stored", 16, "sp")
    ht_ps = signal("ht_ps", 1, "pe")
    ht_sb = signal("ht_sb", 1, "act")
    qkv_ps = signal("qkv_ps", 2 * GT, "pe")
    raw_sb = signal("raw_sb", GT, "act")
    squared = signal("squared", GT, "act")
    v_sb = signal("v_sb", GT, "act")
    norm2 = signal("norm2", GT, "dve")
    clipped = signal("clipped", GT, "dve")
    rnorm = signal("rnorm", GT, "pool")
    rot_terms = signal("rot_terms", GT, "dve")
    rotated = signal("rotated", GT, "pool")
    qk_unit = signal("qk_unit", GT, "pool")
    qkt_ps = signal("qkt_ps", 2 * GT, "pe")
    qkt_sb = signal("qkt_sb", 2 * GT, "act")
    s_ps = signal("s_ps", PAIRS * GT, "pe")
    negmax = signal("negmax", PAIRS * GT, "dve")
    p_sb = signal("p_sb", PAIRS * GT, "act")
    pt_ps = signal("pt_ps", PAIRS * GT, "pe")
    EVAC = (0, 1, 1, 0)
    NEVAC = (EVAC.count(0), EVAC.count(1))
    pt_sb = [signal("pt_sb_dve", NEVAC[0] * GT, "dve"), signal("pt_sb_act", NEVAC[1] * GT, "act")]
    attended = signal("attended", PAIRS * GT, "pe")
    rsum = signal("rsum", GT, "dve")
    o_sb = signal("o_sb", GT, "dve")
    ot_ps = signal("ot_ps", GT, "pe")
    ot_sb = signal("ot_sb", GT, "act")
    y_ps = signal("y_ps", GT, "pe")
    y_sb = signal("y_sb", GT, "dve")
    halo = signal("halo", 1, "dve")

    WTS = 16 * 12
    OB, QKV, HTB, QKT, SP_ = 0, (1, 2, 3), 1, (1, 2), (4, 5, 6, 7)

    def out_bank(t):
        return 0 if t == GT - 1 else 3

    def head(i, s):
        return 4 * (i // 2) + i % 2 + 2 * s

    def pt_copied(n, t, i):
        return pt_sb[EVAC[i]].at(n, NEVAC[EVAC[i]] * t + 1 + EVAC[:i].count(EVAC[i]))

    def place(g, t):
        return g * GT + t if t < GT else g * -GT + t

    with nc.Block() as block:

        @block.sync
        def _(sp):
            ph.start(sp, "sp")
            sp.dma_start(wqkv[:], w["wqkv"][bass.ds(l * D, D), :]).then_inc(wts_loaded, 16)
            sp.dma_start(wo[:], tiles(w["wo"][bass.ds(l * INNER, INNER), :])).then_inc(wts_loaded, 16)
            sp.dma_start(ident[:], c["ident"]).then_inc(wts_loaded, 16)
            sp.dma_start(mask[:], c["ffn_mask"].rearrange("p (e h k) -> p e h k", e=2, h=2)).then_inc(wts_loaded, 16)
            sp.dma_start(table[:], c["rotation"].rearrange("p (r n i) -> p r n i", r=4, i=DH)).then_inc(wts_loaded, 16)
            sp.dma_start(minus_half[:], c["minus_half"][:, 0:2 * H]).then_inc(wts_loaded, 16)
            for n, scale in enumerate((w["q_scale"], w["k_scale"])):
                sp.dma_start(scales[:, 2 * n, :], scale[bass.ds(l, 1), :].to_broadcast([P, DH])).then_inc(wts_loaded, 16)
                for s in range(2):
                    sp.dma_start(scales[:, 2 * n + 1, 32 * s:32 * s + 32],
                                 scale[bass.ds(l, 1), 32 - 32 * s:64 - 32 * s].to_broadcast([P, 32]))\
                        .then_inc(wts_loaded, 16)

            def load_h(row):
                sp.dma_start(h[:, :, 0:D // 2], tiles(src[bass.ds(row, G), 0:D // 2])).then_inc(h_loaded.sem, 16)
                sp.dma_start(h[:, :, D // 2:D], tiles(src[bass.ds(row - 1, G), D // 2:D])).then_inc(h_loaded.sem, 16)

            load_h(scratch_row(0, 0))
            sp.wait_ge(*ht_ps.at(0, 2))
            load_h(scratch_row(0, 1))
            with sp.Fori(0, NB) as b, sp.Fori(0, NG) as g:
                n = sp.snap(b * NG + g + 1)
                row = sp.snap(scratch_row(b, g))
                ahead = sp.snap((n + 1) % TURNS)
                sp.wait_ge(*ht_ps.at(n, 2))
                load_h(sp.snap(ahead * G + ahead // NG * PAD + PAD))
                sp.wait_ge(*y_sb.at(n, 0))
                sp.dma_start(x[:], tiles(src[bass.ds(row, G), :])).then_inc(x_loaded.sem, 16)
                sp.wait_ge(*y_sb.at(n, GT))
                sp.dma_start(tiles(dst[bass.ds(row, G), :]), y[:]).then_inc(stored.sem, 16)
            sp.wait_ge(*stored.at(TURNS + 1, 0))
            sp.wait_ge(*h_loaded.at(TURNS + 1, 64))

        @block.gpsimd
        def _(pool):
            ph.start(pool, "pool")
            pool.memset(kt[:, :, 0:W], 0.0).then_inc(prepared, 1)
            pool.memset(v[:, NT - 1, :, :], 0.0).then_inc(prepared, 1)
            pool.memset(pr[:, :, 0:P - W], 0.0).then_inc(prepared, 1)
            pool.wait_ge(wts_loaded, WTS)

            def rotate(n, t):
                pool.wait_ge(*rot_terms.at(n, t + 1))
                pool.tensor_tensor(rot[:], rot_c[:], rot_s[:], ALU.add).then_inc(rotated.sem, 1)
                pool.wait_ge(*clipped.at(n, t + 1))
                pool.tensor_tensor(rn[:], ss[:, 1, :], minus_half[:], ALU.pow).then_inc(rnorm.sem, 1)
                pool.wait_ge(*rotated.at(n, t + 1))
                pool.wait_ge(*rnorm.at(n, t + 1))
                pool.wait_ge(*qkt_ps.at(n, 2 * t))
                pool.tensor_tensor(qk[:], rot[:].rearrange("p r h i -> p (r h) i"),
                                   rn[:].unsqueeze(2).to_broadcast([P, 2 * H, DH]), ALU.mult).then_inc(qk_unit.sem, 1)
                pool.wait_ge(*qk_unit.at(n, t + 1))

            for t in range(GT, 2 * GT - 1):
                rotate(0, t)
            with pool.Fori(0, NB) as b, pool.Fori(0, NG) as g:
                n = pool.snap(b * NG + g + 1)
                for t in range(GT):
                    rotate(n, t + GT - 1)

        @block.tensor
        def _(pe):
            ph.start(pe, "pe")
            pe.wait_ge(wts_loaded, WTS)
            pe.wait_ge(prepared, 6 + 3)

            def transpose_h(n):
                pe.wait_ge(*h_loaded.at(n, 64))
                pe.wait_ge(*qkt_sb.at(n, 2 * 1 + 1))
                for t in range(GT):
                    mm = pe.transpose(ps[:, HTB, t * P:(t + 1) * P], h[:, t, :], ident[:])
                mm.then_inc(ht_ps.sem, 1)

            def project(n, t, first=False):
                pe.wait_ge(*ht_sb.at(n, 2))
                pe.wait_ge(*raw_sb.at(n, t))
                pe.wait_ge(*v_sb.at(n, t))
                if not first:
                    pe.wait_ge(*qkt_sb.at(n, 2 * (t - GT + 2)))
                if t > GT and not first:
                    pe.wait_ge(*y_sb.at(n, t - GT))
                for j, bank in enumerate(QKV):
                    mm = pe.matmul(ps[:, bank, :], ht[:, t % GT * P:(t % GT + 1) * P], wqkv[:, j * INNER:(j + 1) * INNER],
                                   start=True, stop=True)
                    if j == 1:
                        mm.then_inc(qkv_ps.sem, 1)
                mm.then_inc(qkv_ps.sem, 1)

            def transpose_qk(n, t, projected):
                pe.wait_ge(*qk_unit.at(n, t + 1))
                pe.wait_ge(*raw_sb.at(n, projected))
                for j in range(2):
                    for i in range(4):
                        mm = pe.transpose(ps[:, QKT[j], i * P:(i + 1) * P],
                                          qk[:, 8 * j + 2 * i:8 * j + 2 * i + 2, :], ident[:])
                    mm.then_inc(qkt_ps.sem, 1)

            def scores(n, t, i, start_of_sequence):
                if i == 0:
                    pe.wait_ge(*qkt_sb.at(n, 2 * t + 2))
                    if t == GT:
                        pe.wait_ge(*halo.at(n, 1))
                pe.wait_ge(*pt_copied(n, t - 1, i))
                out = ps[:, SP_[i], 0:2 * KEYS]
                pe.matmul(out, identb[:], start_of_sequence, start=True, stop=False, skip_group_check=True)
                for s in range(2):
                    half, pair = 64 * (i % 2), head(i, s) // 2
                    mm = pe.matmul(ps[:, SP_[i], s * KEYS:(s + 1) * KEYS], qt[half:half + 64, t % 2, pair, :],
                                   kt[half:half + 64, pair, t % GT * P:t % GT * P + KEYS],
                                   start=False, stop=s == 1, skip_group_check=True)
                mm.then_inc(s_ps.sem, 1)

            first_mask = maskb[:, 0, :, :].rearrange("p h k -> p (h k)")
            other_mask = maskb[:, 1, :, :].rearrange("p h k -> p (h k)")

            transpose_h(0)
            for t in range(GT, 2 * GT):
                project(0, t, first=True)
            transpose_qk(0, GT, 2 * GT)
            scores(0, GT, 0, first_mask)
            scores(0, GT, 1, first_mask)
            with pe.Fori(0, NB) as b, pe.Fori(0, NG) as g:
                n = pe.snap(b * NG + g + 1)
                following = pe.snap(g * -1 + 1)
                slots = [pe.snap(g * -GT + (NT - 1))] + [pe.snap(g * GT + t) for t in range(GT)]

                def mask_of(t):
                    if t % GT:
                        return other_mask
                    return maskb[:, bass.ds(g if t == 0 else following, 1), :, :].rearrange("p e h k -> p (e h k)")

                def transpose_p(t, i):
                    pe.wait_ge(*p_sb.at(n, PAIRS * t + i + 1))
                    for s in range(2):
                        for k in range(2):
                            mm = pe.transpose(ps[:, SP_[i], (2 * s + k) * P:(2 * s + k + 1) * P],
                                              pr[:, 2 * i + s, k * P:(k + 1) * P], ident[:])
                    mm.then_inc(pt_ps.sem, 1)

                def attend(t, i):
                    if i == 0:
                        pe.wait_ge(*v_sb.at(n, t + 1))
                        pe.wait_ge(*o_sb.at(n, t))
                        if t == 0:
                            pe.wait_ge(*y_sb.at(n, 0))
                    pe.wait_ge(*pt_copied(n, t, i))
                    for s in range(2):
                        j = head(i, s)
                        for k in range(2):
                            mm = pe.matmul(ps[:, OB, j * DH:(j + 1) * DH], pt[:, 2 * i + s, k, :],
                                           v[:, bass.ds(slots[t + k], 1), j, :], start=k == 0, stop=k == 1)
                    mm.then_inc(attended.sem, 1)

                def transpose_o(t):
                    pe.wait_ge(*o_sb.at(n, t + 1))
                    pe.wait_ge(*v_sb.at(n, t + GT + 1))
                    for i in range(4):
                        mm = pe.transpose(ps[:, out_bank(t), i * P:(i + 1) * P], o[:, 2 * i:2 * i + 2, :], ident[:])
                    mm.then_inc(ot_ps.sem, 1)

                def project_out(t):
                    pe.wait_ge(*ot_sb.at(n, t + 1))
                    for i in range(4):
                        mm = pe.matmul(ps[:, out_bank(t), 0:D], ot[:, i, :], wo[:, i, :], start=i == 0, stop=i == 3)
                    mm.then_inc(y_ps.sem, 1)

                for t in range(GT):
                    scores(n, t, 2, mask_of(t))
                    transpose_p(t, 0)
                    if t > 0:
                        attend(t - 1, 3)
                    transpose_qk(n, t + 1, GT + t)

                    scores(n, t, 3, mask_of(t))
                    transpose_p(t, 1)
                    attend(t, 0)
                    if t > 0:
                        transpose_o(t - 1)

                    scores(n, t + 1, 0, mask_of(t + 1))
                    transpose_p(t, 2)
                    attend(t, 1)
                    if t > 0:
                        project_out(t - 1)
                    else:
                        transpose_h(n)

                    scores(n, t + 1, 1, mask_of(t + 1))
                    transpose_p(t, 3)
                    attend(t, 2)
                    project(n, t + GT)
                attend(GT - 1, 3)
                transpose_o(GT - 1)
                project_out(GT - 1)
            pe.wait_ge(*y_sb.at(TURNS + 1, 0))
            pe.sem_inc(qkt_ps.sem, 2 * (GT - 3))

        @block.scalar
        def _(act):
            ph.start(act, "act")

            def copy_ht(n):
                act.wait_ge(*ht_ps.at(n, 2))
                act.wait_ge(*qkv_ps.at(n, 2 * GT))
                act.activation(ht[:], ps[:, HTB, :], ACT.Copy).then_inc(ht_sb.sem, 1)

            def copy_qkv(n, t, slot, in_loop=True):
                act.wait_ge(*qkv_ps.at(n, 2 * t + 1))
                act.wait_ge(*rot_terms.at(n, t))
                act.wait_ge(*squared.at(n, t))
                act.activation(raw[:], ps[:, QKV[0]:QKV[1] + 1, :].rearrange("p r (h i) -> p r h i", i=DH), ACT.Copy)\
                    .then_inc(raw_sb.sem, 1)
                act.wait_ge(*qkv_ps.at(n, 2 * t + 2))
                if in_loop:
                    act.wait_ge(*attended.at(n, PAIRS * (t - GT - 2)))
                act.activation(v[:, slot, :, :], ps[:, QKV[2], :].rearrange("p (h i) -> p h i", i=DH), ACT.Copy)\
                    .then_inc(v_sb.sem, 1)

            def square(n, t):
                act.wait_ge(*raw_sb.at(n, t + 1))
                act.wait_ge(*norm2.at(n, t))
                act.activation(sq[:], raw[:], ACT.Square).then_inc(squared.sem, 1)

            def copy_qkt(n, t):
                act.wait_ge(*qkt_ps.at(n, 2 * t + 1))
                act.wait_ge(*s_ps.at(n, PAIRS * (t - 1)))
                act.activation(qt[:, t % 2], ps[:, QKT[0], :].rearrange("p (i k) -> p i k", k=P), ACT.Copy)\
                    .then_inc(qkt_sb.sem, 1)
                act.wait_ge(*qkt_ps.at(n, 2 * t + 2))
                if t % GT == GT - 1:
                    act.wait_ge(*halo.at(n, 0))
                act.activation(kt[:, :, W + t % GT * P:W + (t % GT + 1) * P],
                               ps[:, QKT[1], :].rearrange("p (i k) -> p i k", k=P), ACT.Copy).then_inc(qkt_sb.sem, 1)

            def softmax(n, t, i):
                act.wait_ge(*negmax.at(n, PAIRS * t + i + 1))
                act.wait_ge(*pt_ps.at(n, PAIRS * (t - 1) + i + 1))
                if i == 0:
                    act.wait_ge(*rsum.at(n, t - 1))
                for s in range(2):
                    e = act.activation(pr[:, 2 * i + s, P - W:2 * P], ps[:, SP_[i], s * KEYS:(s + 1) * KEYS], ACT.Exp,
                                       bias=nmx[:, 2 * i + s:2 * i + s + 1],
                                       accum_out=rowsum[:, t % 2, head(i, s):head(i, s) + 1])
                e.then_inc(p_sb.sem, 1)

            copy_ht(0)
            for t in range(GT, 2 * GT):
                if t > GT:
                    square(0, t - 1)
                copy_qkv(0, t, t - GT, in_loop=False)
            copy_qkt(0, GT)
            softmax(0, GT, 0)
            with act.Fori(0, NB) as b, act.Fori(0, NG) as g:
                n = act.snap(b * NG + g + 1)
                slots = [act.snap(place(g, GT + t)) for t in range(GT)]

                def copy_pt(t, i):
                    act.wait_ge(*pt_ps.at(n, PAIRS * t + i + 1))
                    act.wait_ge(*attended.at(n, PAIRS * (t - 1) + i + 1))
                    act.activation(pt[:, 2 * i:2 * i + 2, :, :],
                                   ps[:, SP_[i], :].rearrange("p (s k q) -> p s k q", s=2, k=2), ACT.Copy)\
                        .then_inc(pt_sb[1].sem, 1)

                def copy_ot(t):
                    act.wait_ge(*ot_ps.at(n, t + 1))
                    act.wait_ge(*y_ps.at(n, t))
                    act.activation(ot[:], ps[:, out_bank(t), :].rearrange("p (i k) -> p i k", k=P), ACT.Copy)\
                        .then_inc(ot_sb.sem, 1)

                for t in range(GT):
                    softmax(n, t, 1)
                    copy_qkt(n, t + 1)

                    softmax(n, t, 2)
                    copy_pt(t, 1)
                    if t > 0:
                        copy_ot(t - 1)

                    softmax(n, t, 3)
                    copy_pt(t, 2)
                    square(n, t + GT - 1)
                    if t == 0:
                        copy_ht(n)

                    softmax(n, t + 1, 0)
                    copy_qkv(n, t + GT, bass.ds(slots[t], 1))
                copy_ot(GT - 1)

        @block.vector
        def _(dve):
            ph.start(dve, "dve")
            dve.wait_ge(wts_loaded, WTS)
            dve.tensor_copy(identb[:], ident[:]).then_inc(prepared, 1)
            dve.tensor_copy(maskb[:], mask[:]).then_inc(prepared, 1)
            for r in range(4):
                dve.tensor_tensor(table[:, r], table[:, r], scales[:, r, :].unsqueeze(1).to_broadcast([P, NT, DH]),
                                  ALU.mult).then_inc(prepared, 1)
            dve.wait_ge(prepared, 6 + 3)

            def cosines(n, t, entry):
                dve.wait_ge(*raw_sb.at(n, t + 1))
                dve.wait_ge(*rotated.at(n, t))
                for r in range(2):
                    cos = table[:, 2 * r, entry, :].to_broadcast([P, H, DH])
                    dve.tensor_tensor(rot_c[:, r], raw[:, r], cos, ALU.mult)

            def sines(n, t, entry):
                for r in range(2):
                    swapped = raw[:, r].rearrange("p h (s i) -> p h s i", s=2)[:, :, ::-1, :]
                    sin = table[:, 2 * r + 1, entry, :].to_broadcast([P, H, DH]).rearrange("p h (s i) -> p h s i", s=2)
                    terms = dve.tensor_tensor(rot_s[:, r].rearrange("p h (s i) -> p h s i", s=2), swapped, sin, ALU.mult)
                terms.then_inc(rot_terms.sem, 1)

            def squared_norms(n, t):
                dve.wait_ge(*squared.at(n, t + 1))
                dve.wait_ge(*clipped.at(n, t))
                dve.tensor_reduce(ss[:, 0, :], sq[:].rearrange("p r h i -> p (r h) i"), AX.X, ALU.add).then_inc(norm2.sem, 1)
                dve.wait_ge(*norm2.at(n, t + 1))
                dve.wait_ge(*rnorm.at(n, t))
                dve.tensor_scalar(ss[:, 1, :], ss[:, 0, :], 1e-24, None, ALU.max).then_inc(clipped.sem, 1)

            def maximum(n, t, i):
                dve.wait_ge(*s_ps.at(n, PAIRS * t + i + 1))
                dve.wait_ge(*p_sb.at(n, PAIRS * (t - 1) + i + 1))
                dve.tensor_reduce(nmx[:, 2 * i:2 * i + 2], ps[:, SP_[i], 0:2 * KEYS].rearrange("p (s k) -> p s k", s=2),
                                  AX.X, ALU.max, negate=True).then_inc(negmax.sem, 1)

            for t in range(GT, 2 * GT - 1):
                cosines(0, t, slice(t - GT, t - GT + 1))
                sines(0, t, slice(t - GT, t - GT + 1))
                squared_norms(0, t)
            maximum(0, GT, 0)
            maximum(0, GT, 1)
            with dve.Fori(0, NB) as b, dve.Fori(0, NG) as g:
                n = dve.snap(b * NG + g + 1)
                entries = [dve.snap(place(g, GT - 1 + t)) for t in range(GT)]

                def copy_pt(t, i):
                    dve.wait_ge(*pt_ps.at(n, PAIRS * t + i + 1))
                    dve.wait_ge(*attended.at(n, PAIRS * (t - 1) + i + 1))
                    dve.tensor_copy(pt[:, 2 * i:2 * i + 2, :, :],
                                    ps[:, SP_[i], :].rearrange("p (s k q) -> p s k q", s=2, k=2)).then_inc(pt_sb[0].sem, 1)

                def normalize(t):
                    dve.wait_ge(*p_sb.at(n, PAIRS * t + PAIRS))
                    dve.wait_ge(*o_sb.at(n, t))
                    dve.reciprocal(rs[:], rowsum[:, t % 2, :]).then_inc(rsum.sem, 1)
                    dve.wait_ge(*rsum.at(n, t + 1))
                    dve.wait_ge(*attended.at(n, PAIRS * (t + 1)))
                    dve.wait_ge(*ot_ps.at(n, t))
                    dve.tensor_tensor(o[:], ps[:, OB, :].rearrange("p (h i) -> p h i", i=DH),
                                      rs[:].unsqueeze(2).to_broadcast([P, H, DH]), ALU.mult).then_inc(o_sb.sem, 1)

                def add(t):
                    dve.wait_ge(*y_ps.at(n, t + 1))
                    if t == 0:
                        dve.wait_ge(*x_loaded.at(n, 16))
                        dve.wait_ge(*stored.at(n, 0))
                    dve.tensor_tensor(y[:, t, :], ps[:, out_bank(t), 0:D], x[:, t, :], ALU.add).then_inc(y_sb.sem, 1)

                for t in range(GT):
                    entry = bass.ds(entries[t], 1)
                    maximum(n, t, 2)
                    copy_pt(t, 0)
                    if t > 0:
                        normalize(t - 1)
                    cosines(n, t + GT - 1, entry)

                    maximum(n, t, 3)
                    sines(n, t + GT - 1, entry)

                    maximum(n, t + 1, 0)
                    if t > 0:
                        add(t - 1)
                    if t == GT - 2:
                        dve.wait_ge(*qkt_sb.at(n, 2 * GT))
                        dve.wait_ge(*s_ps.at(n, PAIRS))
                        dve.tensor_copy(kt[:, :, 0:W], kt[:, :, G:G + W]).then_inc(halo.sem, 1)

                    maximum(n, t + 1, 1)
                    copy_pt(t, 3)
                    if t < GT - 1:
                        squared_norms(n, t + GT - 1)
                normalize(GT - 1)
                squared_norms(n, 2 * GT - 2)
                add(GT - 1)
    ph.close()


def window_attention(nc, name, src, x_in, dst, w, c):
    H, DH, W = 16, 8, 64
    KEYS = W + P
    PAIRS = H // 2
    RING = 4
    N = PAIRS * GT
    SCALE = float(DH) ** -0.5
    ph = Phase(nc, name)
    sb, signal = ph.sb, ph.counter
    ps = ph.banks()
    wq, wk, wv, wo = (sb(n, [P, D]) for n in ("wq", "wk", "wv", "wo"))
    bq, bk, bv, bqs = (sb(n, [P, 1]) for n in ("bq", "bk", "bv", "bqs"))
    bo = sb("bo", [P, D])
    ident = sb("ident", [P, P])
    identb = sb("identb", [P, P], BF16)
    mask = sb("mask", [P, 2, 2, KEYS])
    maskb = sb("maskb", [P, 2, 2, KEYS], BF16)
    own = sb("own", [P, 4])
    bk_own = sb("bk_own", [P, 4])
    h = sb("h", [P, GT, D])
    x = sb("x", [P, GT, D])
    xb = sb("xb", [P, GT, D])
    y = sb("y", [P, GT, D])
    ht = sb("ht", [P, G])
    qt = sb("qt", [P, G])
    kt = sb("kt", [P, 4, W + G])
    v = sb("v", [P, 1 + GT, H, DH + 1])
    nmx = sb("nmx", [P, H])
    pr = sb("pr", [P, H, 2 * P])
    pt = sb("pt", [P, H, 2, P])
    rs = sb("rs", [P, H])
    o = sb("o", [P, H, DH])
    ot = sb("ot", [P, P])

    wts_loaded = ph.semaphore("wts_loaded")
    prepared = ph.semaphore("prepared")
    h_loaded = signal("h_loaded", 16, "sp")
    x_loaded = signal("x_loaded", 16, "sp")
    stored = signal("stored", 16, "sp")
    xb_done = signal("xb_done", 1, "pool")
    ht_ps = signal("ht_ps", 1, "pe")
    ht_sb = signal("ht_sb", 1, "act")
    qkv_ps = signal("qkv_ps", 3, "pe")
    qkv_sb = signal("qkv_sb", 6, "act")
    s_ps = signal("s_ps", N, "pe")
    negmax = signal("negmax", N, "dve")
    p_sb = signal("p_sb", N, "act")
    pt_ps = signal("pt_ps", N, "pe")
    pt_sb = [signal("pt_sb_dve", N // 2, "dve"), signal("pt_sb_act", N // 2, "act")]
    attended = signal("attended", N, "pe")
    rsum = signal("rsum", GT, "dve")
    o_sb = signal("o_sb", GT, "dve")
    ot_ps = signal("ot_ps", GT, "pe")
    ot_sb = signal("ot_sb", GT, "act")
    y_ps = signal("y_ps", GT, "pe")
    y_sb = signal("y_sb", GT, "dve")
    halo = signal("halo", 2, "dve")

    loads = [(wq[:], w["Wq"]), (wk[:], w["Wk"]), (wv[:], w["Wv"]), (wo[:], w["Wo"]), (bq[:], w["bq"]), (bk[:], w["bk"]),
             (bv[:], w["bv"]), (bo[:], w["bo"].to_broadcast([P, D])), (ident[:], c["ident"]), (own[:], c["own_head"]),
             (mask[:], c["attn_mask"].rearrange("p (e h k) -> p e h k", e=2, h=2))]
    LOADED, PREPARED = 16 * len(loads), 3 + 4

    HTB, QB, KB, VB = 2, 3, 2, 0
    O_AT, OT_AT, Y_AT = 0, 256, 384

    def score_bank(j):
        return 4 + j % RING

    def pt_copied(n, j):
        return pt_sb[j % 2].at(n, j // 2 + 1)

    with nc.Block() as block:

        @block.sync
        def _(sp):
            ph.start(sp, "sp")
            for out, in_ in loads:
                sp.dma_start(out, in_).then_inc(wts_loaded, 16)
            sp.dma_start(h[:], tiles(src[bass.ds(scratch_row(0, 0), G), :])).then_inc(h_loaded.sem, 16)
            with sp.Fori(0, NB) as b, sp.Fori(0, NG) as g:
                n = sp.snap(b * NG + g + 1)
                row = sp.snap(scratch_row(b, g))
                ahead = sp.snap(n % TURNS)
                sp.wait_ge(*ht_ps.at(n, 1))
                sp.dma_start(h[:], tiles(src[bass.ds(sp.snap(ahead * G + ahead // NG * PAD + PAD), G), :]))\
                    .then_inc(h_loaded.sem, 16)
                sp.wait_ge(*xb_done.at(n, 0))
                sp.dma_start(x[:], tiles(x_in[bass.ds(row, G), :])).then_inc(x_loaded.sem, 16)
                sp.wait_ge(*y_sb.at(n, GT))
                sp.dma_start(tiles(dst[bass.ds(row, G), :]), y[:]).then_inc(stored.sem, 16)
            sp.wait_ge(*stored.at(TURNS + 1, 0))
            sp.wait_ge(*h_loaded.at(TURNS + 1, 16))

        @block.gpsimd
        def _(pool):
            ph.start(pool, "pool")
            pool.memset(kt[:, :, 0:W], 0.0).then_inc(prepared, 1)
            pool.memset(v[:, 0, :, :], 0.0).then_inc(prepared, 1)
            pool.memset(v[:, 1:, :, DH:], 1.0).then_inc(prepared, 1)
            pool.memset(pr[:, :, 0:P - W], 0.0).then_inc(prepared, 1)
            pool.wait_ge(wts_loaded, LOADED)
            with pool.Fori(0, NB) as b, pool.Fori(0, NG) as g:
                n = pool.snap(b * NG + g + 1)
                pool.wait_ge(*x_loaded.at(n, 16))
                pool.wait_ge(*y_sb.at(n, 0))
                pool.tensor_tensor(xb[:], x[:], bo[:].unsqueeze(1).to_broadcast([P, GT, D]), ALU.add).then_inc(xb_done.sem, 1)

        @block.tensor
        def _(pe):
            ph.start(pe, "pe")
            pe.wait_ge(wts_loaded, LOADED)
            pe.wait_ge(prepared, PREPARED)

            def transpose_h(n):
                pe.wait_ge(*h_loaded.at(n, 32))
                pe.wait_ge(*qkv_sb.at(n, 5))
                for t in range(GT):
                    mm = pe.transpose(ps[:, HTB, t * P:(t + 1) * P], h[:, t, :], ident[:])
                mm.then_inc(ht_ps.sem, 1)

            def project_qk(n):
                pe.wait_ge(*ht_sb.at(n, 2))
                pe.wait_ge(*qkv_sb.at(n, 1))
                pe.matmul(ps[:, QB, :], wq[:], ht[:], start=True, stop=True).then_inc(qkv_ps.sem, 1)
                pe.matmul(ps[:, KB, :], wk[:], ht[:], start=True, stop=True).then_inc(qkv_ps.sem, 1)

            def project_v(n):
                pe.wait_ge(*y_sb.at(n, GT - 1))
                for t in range(GT):
                    mm = pe.matmul(ps[:, VB, t * P:(t + 1) * P], ht[:, t * P:(t + 1) * P], wv[:], start=True, stop=True)
                mm.then_inc(qkv_ps.sem, 1)

            def scores(n, j, m):
                t, i = j // PAIRS % GT, j % PAIRS
                if j >= N:
                    pe.wait_ge(*qkv_sb.at(n, 6 + (3 if j == N else 5)))
                    pe.wait_ge(*halo.at(n, 1))
                pe.wait_ge(*pt_copied(n, j - RING))
                bank, at = score_bank(j), 32 * (i // 2)
                pe.matmul(ps[:, bank, 0:2 * KEYS], identb[:], m, start=True, stop=False, skip_group_check=True)
                for s in range(2):
                    mm = pe.matmul(ps[:, bank, s * KEYS:(s + 1) * KEYS], qt[at:at + 32, t * P:(t + 1) * P],
                                   kt[at:at + 32, (2 * i + s) % 4, t * P:t * P + KEYS],
                                   start=False, stop=s == 1, skip_group_check=True, tile_position=(at, 0))
                mm.then_inc(s_ps.sem, 1)

            first_mask = maskb[:, 0, :, :].rearrange("p h k -> p (h k)")
            other_mask = maskb[:, 1, :, :].rearrange("p h k -> p (h k)")

            transpose_h(0)
            project_qk(0)
            project_v(0)
            scores(0, N, first_mask)
            scores(0, N + 1, first_mask)
            with pe.Fori(0, NB) as b, pe.Fori(0, NG) as g:
                n = pe.snap(b * NG + g + 1)
                following = pe.snap(g * -1 + 1)

                def mask_of(j):
                    if j // PAIRS % GT:
                        return other_mask
                    return maskb[:, bass.ds(g if j < N else following, 1), :, :].rearrange("p e h k -> p (e h k)")

                def transpose_p(j):
                    pe.wait_ge(*p_sb.at(n, j + 1))
                    for s in range(2):
                        for k in range(2):
                            mm = pe.transpose(ps[:, score_bank(j), (2 * s + k) * P:(2 * s + k + 1) * P],
                                              pr[:, 2 * (j % PAIRS) + s, k * P:(k + 1) * P], ident[:])
                    mm.then_inc(pt_ps.sem, 1)

                def attend(j):
                    t = j // PAIRS
                    if j % PAIRS == 0:
                        pe.wait_ge(*y_sb.at(n, t - 1))
                        if t == 0:
                            pe.wait_ge(*qkv_sb.at(n, 6))
                    pe.wait_ge(*pt_copied(n, j))
                    for s in range(2):
                        head = 2 * (j % PAIRS) + s
                        for k in range(2):
                            mm = pe.matmul(ps[:, t % 2, O_AT + head * (DH + 1):O_AT + (head + 1) * (DH + 1)],
                                           pt[:, head, k, :], v[:, t + k, head, :], start=k == 0, stop=k == 1)
                    mm.then_inc(attended.sem, 1)

                def transpose_o(t):
                    pe.wait_ge(*o_sb.at(n, t + 1))
                    pe.transpose(ps[:, t % 2, OT_AT:OT_AT + P], o[:].rearrange("p h i -> p (h i)"), ident[:])\
                        .then_inc(ot_ps.sem, 1)

                def project_out(t):
                    pe.wait_ge(*ot_sb.at(n, t + 1))
                    pe.matmul(ps[:, t % 2, Y_AT:Y_AT + D], ot[:], wo[:], start=True, stop=True).then_inc(y_ps.sem, 1)

                for j in range(N):
                    t, i = j // PAIRS, j % PAIRS
                    if j + 2 < N:
                        scores(n, j + 2, mask_of(j + 2))
                    transpose_p(j)
                    if j > 0:
                        attend(j - 1)
                    if t > 0 and i == 2:
                        transpose_o(t - 1)
                    if t > 0 and i == 4:
                        project_out(t - 1)
                    if t == GT - 1 and i == 1:
                        transpose_h(n)
                    if t == GT - 1 and i == 5:
                        project_qk(n)
                    if t == GT - 1 and i == 7:
                        project_v(n)
                attend(N - 1)
                transpose_o(GT - 1)
                scores(n, N, mask_of(N))
                project_out(GT - 1)
                scores(n, N + 1, mask_of(N + 1))

        @block.scalar
        def _(act):
            ph.start(act, "act")
            act.wait_ge(wts_loaded, LOADED)
            act.wait_ge(prepared, PREPARED)

            def copy_ht(n):
                act.wait_ge(*ht_ps.at(n, 2))
                act.wait_ge(*qkv_ps.at(n, 3))
                act.activation(ht[:], ps[:, HTB, :], ACT.Copy).then_inc(ht_sb.sem, 1)

            def copy_q(n):
                act.wait_ge(*qkv_ps.at(n, 3 + 1))
                act.wait_ge(*s_ps.at(n, N))
                act.activation(qt[:], ps[:, QB, :], ACT.Identity, scale=SCALE, bias=bqs[:]).then_inc(qkv_sb.sem, 1)

            def copy_k(n, parts):
                act.wait_ge(*qkv_ps.at(n, 3 + 2))
                act.wait_ge(*halo.at(n, 1))
                for m in parts:
                    act.activation(kt[:, m, W:W + G], ps[:, KB, :], ACT.Identity, scale=own[:, m:m + 1],
                                   bias=bk_own[:, m:m + 1]).then_inc(qkv_sb.sem, 1)

            def copy_v(n):
                act.wait_ge(*qkv_ps.at(n, 3 + 3))
                act.wait_ge(*attended.at(n, N))
                act.wait_ge(*halo.at(n, 2))
                act.activation(v[:, 1:, :, 0:DH], ps[:, VB, :].rearrange("p (t h i) -> p t h i", t=GT, i=DH), ACT.Copy)\
                    .then_inc(qkv_sb.sem, 1)

            def exponentials(n, j):
                act.wait_ge(*negmax.at(n, j + 1))
                act.wait_ge(*pt_ps.at(n, j + 1 - PAIRS))
                i = j % PAIRS
                for s in range(2):
                    e = act.activation(pr[:, 2 * i + s, P - W:2 * P], ps[:, score_bank(j), s * KEYS:(s + 1) * KEYS],
                                       ACT.Exp, bias=nmx[:, 2 * i + s:2 * i + s + 1])
                e.then_inc(p_sb.sem, 1)

            copy_ht(0)
            copy_q(0)
            copy_k(0, range(4))
            exponentials(0, N)
            copy_v(0)
            with act.Fori(0, NB) as b, act.Fori(0, NG) as g:
                n = act.snap(b * NG + g + 1)

                def copy_pt(j):
                    act.wait_ge(*pt_ps.at(n, j + 1))
                    act.wait_ge(*attended.at(n, j + 1 - PAIRS))
                    i = j % PAIRS
                    act.activation(pt[:, 2 * i:2 * i + 2, :, :],
                                   ps[:, score_bank(j), :].rearrange("p (s k q) -> p s k q", s=2, k=2), ACT.Copy)\
                        .then_inc(pt_sb[1].sem, 1)

                def copy_ot(t):
                    act.wait_ge(*ot_ps.at(n, t + 1))
                    act.wait_ge(*y_ps.at(n, t))
                    act.activation(ot[:], ps[:, t % 2, OT_AT:OT_AT + P], ACT.Identity, bias=bv[:]).then_inc(ot_sb.sem, 1)

                for j in range(N):
                    t, i = j // PAIRS, j % PAIRS
                    if j + 1 < N:
                        exponentials(n, j + 1)
                    if j % 2 == 1:
                        copy_pt(j)
                    if t > 0 and i == 3:
                        copy_ot(t - 1)
                    if t == GT - 1 and i == 2:
                        copy_ht(n)
                copy_q(n)
                copy_k(n, (0, 1))
                copy_ot(GT - 1)
                copy_k(n, (2, 3))
                exponentials(n, N)
                copy_v(n)

        @block.vector
        def _(dve):
            ph.start(dve, "dve")
            dve.wait_ge(wts_loaded, LOADED)
            dve.tensor_copy(identb[:], ident[:])
            dve.tensor_copy(maskb[:], mask[:])
            dve.tensor_scalar(bqs[:], bq[:], SCALE, None, ALU.mult)
            dve.tensor_scalar(bk_own[:], own[:], bk[:], None, ALU.mult).then_inc(prepared, 3)

            def maximum(n, j):
                dve.wait_ge(*s_ps.at(n, j + 1))
                dve.wait_ge(*p_sb.at(n, j + 1 - PAIRS))
                i = j % PAIRS
                dve.tensor_reduce(nmx[:, 2 * i:2 * i + 2], ps[:, score_bank(j), 0:2 * KEYS].rearrange("p (s k) -> p s k", s=2),
                                  AX.X, ALU.max, negate=True).then_inc(negmax.sem, 1)

            maximum(0, N)
            maximum(0, N + 1)
            with dve.Fori(0, NB) as b, dve.Fori(0, NG) as g:
                n = dve.snap(b * NG + g + 1)

                def copy_pt(j):
                    dve.wait_ge(*pt_ps.at(n, j + 1))
                    dve.wait_ge(*attended.at(n, j + 1 - PAIRS))
                    i = j % PAIRS
                    dve.tensor_copy(pt[:, 2 * i:2 * i + 2, :, :],
                                    ps[:, score_bank(j), :].rearrange("p (s k q) -> p s k q", s=2, k=2)).then_inc(pt_sb[0].sem, 1)

                def normalize(t):
                    dve.wait_ge(*attended.at(n, PAIRS * (t + 1)))
                    dve.wait_ge(*o_sb.at(n, t))
                    oh = ps[:, t % 2, O_AT:O_AT + H * (DH + 1)].rearrange("p (h i) -> p h i", i=DH + 1)
                    dve.reciprocal(rs[:], oh[:, :, DH]).then_inc(rsum.sem, 1)
                    dve.wait_ge(*rsum.at(n, t + 1))
                    dve.wait_ge(*ot_ps.at(n, t))
                    dve.tensor_tensor(o[:], oh[:, :, 0:DH], rs[:].unsqueeze(2).to_broadcast([P, H, DH]), ALU.mult)\
                        .then_inc(o_sb.sem, 1)

                def add(t):
                    dve.wait_ge(*y_ps.at(n, t + 1))
                    if t == 0:
                        dve.wait_ge(*xb_done.at(n, 1))
                        dve.wait_ge(*stored.at(n, 0))
                    dve.tensor_tensor(y[:, t, :], ps[:, t % 2, Y_AT:Y_AT + D], xb[:, t, :], ALU.add).then_inc(y_sb.sem, 1)

                for j in range(N):
                    t, i = j // PAIRS, j % PAIRS
                    if j + 2 < N:
                        maximum(n, j + 2)
                    if j % 2 == 0:
                        copy_pt(j)
                    if t > 0 and i == 0:
                        normalize(t - 1)
                    if t > 0 and i == 5:
                        add(t - 1)
                    if t == 1 and i == 6:
                        dve.tensor_copy(kt[:, :, 0:W], kt[:, :, G:G + W]).then_inc(halo.sem, 1)
                    if t == 2 and i == 6:
                        dve.tensor_copy(v[:, 0, :, :], v[:, GT, :, :]).then_inc(halo.sem, 1)
                normalize(GT - 1)
                maximum(n, N)
                maximum(n, N + 1)
                add(GT - 1)
    ph.close()


def delta_attention(nc, name, x_in, dst, w, c):
    H, DK, DV = 8, 96, 192
    HG = 4
    VD = H * DV
    LEVELS = 7
    NQK, NV = 2 * H, VD // P
    NG3 = GT * 3 // 2
    SLOTS = 3
    USES = NQK + NV + NG3
    ph = Phase(nc, name)
    sb, signal = ph.sb, ph.counter
    ps = ph.banks()
    wq = sb("wq", [P, H * DK])
    wk = sb("wk", [P, H * DK])
    wv = sb("wv", [P, VD])
    wg = sb("wg", [P, VD])
    wo = sb("wo", [P, NV, D])
    onorm = sb("onorm", [P, NV])
    wba = sb("wba", [P, 2 * H])
    conv_qk = sb("conv_qk", [DK, H, 2, 4])
    conv_v = sb("conv_v", [P, NV, 4])
    norm1 = sb("norm1", [P, 1])
    decay_rate = sb("decay_rate", [P, H])
    dt_bias = sb("dt_bias", [P, H])
    ident = sb("ident", [P, P])
    ident4 = sb("ident4", [P, HG, P])
    sums = sb("sums", [P, 3, P])
    not_first = sb("not_first", [P, 1])
    blocks = sb("blocks", [P, LEVELS, P // 2])
    minus_half = sb("minus_half", [P, 4 * H])
    x = sb("x", [P, GT, D])
    y = sb("y", [P, GT, D])
    hn = sb("hn", [P, GT, D])
    out = sb("out", [P, GT, D])
    stats = sb("stats", [P, GT, 6])
    mv = sb("mv", [P, GT, 2])
    ms = sb("ms", [P, 2, GT])
    rstd = sb("rstd", [P, 2, GT])
    ht = sb("ht", [P, 3 + G])
    raw = sb("raw", [P, SLOTS, 3 + G])
    conv = sb("conv", [P, SLOTS, G])
    qk = sb("qk", [DK, H, 2, G])
    vt = sb("vt", [P, NV, G])
    gate = sb("gate", [P, GT, VD])
    za = sb("za", [P, 12, GT * H])
    ex = sb("ex", [P, 6, GT, H])
    sq = sb("sq", [DK, H, 2, P])
    cf = sb("cf", [P, 14, 2 * H])
    gd = sb("gd", [P, H, P])
    al = sb("al", [P, H, 2, P])
    tm = sb("tm", [P, H, P])
    tt = sb("tt", [P, H, P])
    am = sb("am", [P, H, P // 2])
    kd = sb("kd", [P, H, DK])
    vr = sb("vr", [P, H, DV])
    delta = sb("delta", [P, H, DV])
    o = sb("o", [P, H, DV])
    ot = sb("ot", [P, NV, P])
    state = sb("state", [DK, H, DV])

    wts_loaded = ph.semaphore("wts_loaded")
    prepared = ph.semaphore("prepared")
    x_loaded = signal("x_loaded", 16, "sp")
    stored = signal("stored", 16, "sp")
    stats_done = signal("stats_done", GT, "dve")
    seen = signal("seen", 1, "dve").sem
    moments = signal("moments", GT, "dve")
    root1 = signal("root1", 1, "dve")
    root1_done = signal("root1_done", 1, "pool")
    root2 = signal("root2", 4, "dve")
    root2_done = signal("root2_done", 1, "pool")
    y_sb = signal("y_sb", 1, "dve")
    hn_sb = signal("hn_sb", 1, "dve")
    ht_ps = signal("ht_ps", 1, "pe")
    ht_sb = signal("ht_sb", 1, "act")
    ht_halo = signal("ht_halo", 1, "dve")
    ba_ps = signal("ba_ps", 1, "pe")
    za_step = signal("za_step", 22, "dve")
    za_exp = signal("za_exp", 2, "act")
    cum_ps = signal("cum_ps", 1, "pe")
    ex_sb = signal("ex_sb", 2, "act")
    decay_cut = signal("decay_cut", 1, "dve")
    use_ps = signal("use_ps", USES, "pe")
    use_sb = signal("use_sb", USES, "act")
    tap = signal("tap", 3 * (NQK + NV), "dve")
    silu = signal("silu", NQK + NV, "act")
    zeroed = signal("zeroed", 2, "dve")
    sq_sb = signal("sq_sb", GT, "pool")
    n2_ps = signal("n2_ps", GT, "pe")
    n2_sb = signal("n2_sb", GT, "dve")
    rn_sb = signal("rn_sb", GT, "pool")
    coef = signal("coef", 4 * GT, "dve")

    def both(n, per, owner):
        return [signal(f"{n}{i}", per, owner) for i in range(2)]
    dec_ps = both("dec_ps", GT, "pe")
    gd_sb = both("gd_sb", GT, "dve")
    kq_ps = both("kq_ps", GT, "pe")
    al_sb = both("al_sb", GT, "dve")
    kt_ps = both("kt_ps", GT, "pe")
    kd_sb = both("kd_sb", GT, "act")
    vt_ps = both("vt_ps", GT, "pe")
    vb_sb = both("vb_sb", GT, "act")
    tm_one = both("tm_one", GT, "act")
    lx_ps = both("lx_ps", LEVELS * GT, "pe")
    am_sb = both("am_sb", LEVELS * GT, "dve")
    ty_ps = both("ty_ps", (LEVELS - 1) * GT, "pe")
    tm_sb = both("tm_sb", LEVELS * GT, "dve")
    tt_ps = both("tt_ps", LEVELS * GT, "pe")
    tt_sb = both("tt_sb", LEVELS * GT, "act")
    ks_ps = both("ks_ps", GT, "pe")
    r_sb = both("r_sb", GT, "dve")
    delta_ps = both("delta_ps", GT, "pe")
    delta_sb = both("delta_sb", GT, "act")
    qs_ps = both("qs_ps", GT, "pe")
    qs_sb = both("qs_sb", GT, "act")
    ad_ps = both("ad_ps", GT, "pe")
    o_sb = both("o_sb", GT, "dve")
    up_ps = both("up_ps", GT, "pe")
    state_sb = both("state_sb", GT, "dve")
    osq = signal("osq", GT, "act")
    om = signal("om", 4 * GT, "dve")
    orn = signal("orn", GT, "pool")
    og_sb = signal("og_sb", GT, "dve")
    ot_ps = signal("ot_ps", 3 * GT, "pe")
    ot_sb = signal("ot_sb", 3 * GT, "act")
    y_ps = signal("y_ps", GT, "pe")
    out_sb = signal("out_sb", GT, "dve")

    loads = [(wq[:], w["Wq"]), (wk[:], w["Wk"]), (wv[:], w["Wv"]), (wg[:], w["Wg"]), (wo[:], tiles(w["Wo"])),
             (wba[:, 0:H], w["Wb"]), (wba[:, H:2 * H], w["Wa"]),
             (conv_qk[:, :, 0, :], w["conv_q_w"].rearrange("(h d) i -> d h i", d=DK)),
             (conv_qk[:, :, 1, :], w["conv_k_w"].rearrange("(h d) i -> d h i", d=DK)),
             (conv_v[:], tiles(w["conv_v_w"])), (norm1[:], w["norm1_w"]),
             (decay_rate[:], w["A_log"].to_broadcast([P, H])), (dt_bias[:], w["dt_bias"].to_broadcast([P, H])),
             (ident[:], c["ident"]), (sums[:], c["sums"].rearrange("p (k i) -> p k i", k=3)),
             (not_first[:], c["not_first"]), (blocks[:], c["blocks"].rearrange("p (m i) -> p m i", m=LEVELS)),
             (minus_half[:], c["minus_half"][:, 0:4 * H])]
    ow = w["onorm_w"]
    for m, (p0, p1, a) in ((0, (0, P, 0)), (1, (0, DV - P, P)), (1, (DV - P, P, 0)), (2, (0, P, DV - P))):
        for n in range(m, NV, 3):
            loads.append((onorm[p0:p1, n:n + 1], ow[a:a + p1 - p0, :]))
    for i in range(HG):
        loads.append((ident4[:, i, :], c["ident"]))
    LOADED = 16 * len(loads)

    N2, N2E, RN, BRK, NPB, KDF, OSUM, OMS, OME, ORN, OF, RQ2, PBK, RQS = range(14)
    BETA, DEC, DCUT, PI, PLAST, DLAST = range(6)

    def left(t, m):
        s = 1 << m
        return t.rearrange("p (n two s) -> p n two s", two=2, s=s)[:, :, 0, :]

    def left4(t, m):
        s = 1 << m
        return t.rearrange("p h (n two s) -> p h n two s", two=2, s=s)[:, :, :, 0, :]

    with nc.Block() as block:

        @block.sync
        def _(sp):
            ph.start(sp, "sp")
            for dst_, src_ in loads:
                sp.dma_start(dst_, src_).then_inc(wts_loaded, 16)
            with sp.Fori(0, NB) as b, sp.Fori(0, NG) as g:
                n = sp.snap(b * NG + g + 1)
                sp.wait_ge(*y_sb.at(n, 0))
                sp.dma_start(x[:], tiles(x_in[bass.ds((b * NG + g) * G, G), :])).then_inc(x_loaded.sem, 16)
                sp.wait_ge(*out_sb.at(n, GT))
                sp.dma_start(tiles(dst[bass.ds(scratch_row(b, g), G), :]), out[:]).then_inc(stored.sem, 16)
            sp.wait_ge(*stored.at(TURNS + 1, 0))

        @block.gpsimd
        def _(pool):
            ph.start(pool, "pool")
            pool.wait_ge(wts_loaded, LOADED)
            with pool.Fori(0, NB) as b, pool.Fori(0, NG) as g:
                n = pool.snap(b * NG + g + 1)
                pool.wait_ge(*root1.at(n, 1))
                pool.tensor_tensor(rstd[:, 0, :], ms[:, 0, :], minus_half[:, 0:GT], ALU.pow).then_inc(root1_done.sem, 1)
                pool.wait_ge(*root2.at(n, 4))
                pool.tensor_tensor(rstd[:, 1, :], ms[:, 1, :], minus_half[:, 0:GT], ALU.pow).then_inc(root2_done.sem, 1)
                for t in range(GT):
                    if t == 0:
                        pool.wait_ge(*silu.at(n, NQK))
                    pool.wait_ge(*n2_ps.at(n, t))
                    now = qk[:, :, :, t * P:(t + 1) * P]
                    pool.tensor_tensor(sq[:].rearrange("p h r i -> p (h r) i"), now.rearrange("p h r i -> p (h r) i"),
                                       now.rearrange("p h r i -> p (h r) i"), ALU.mult).then_inc(sq_sb.sem, 1)
                    pool.wait_ge(*n2_sb.at(n, t + 1))
                    pool.tensor_tensor(cf[:, RN, :], cf[:, N2E, :], minus_half[:, 0:2 * H], ALU.pow).then_inc(rn_sb.sem, 1)
                    pool.wait_ge(*om.at(n, 4 * t + 3))
                    pool.tensor_tensor(cf[:, ORN, 0:H], cf[:, OME, 0:H], minus_half[:, 0:H], ALU.pow).then_inc(orn.sem, 1)

        @block.tensor
        def _(pe):
            ph.start(pe, "pe")
            pe.wait_ge(wts_loaded, LOADED)
            pe.wait_ge(prepared, 3)
            with pe.Fori(0, NB) as b, pe.Fori(0, NG) as g:
                n = pe.snap(b * NG + g + 1)
                pe.wait_ge(*hn_sb.at(n, 1))
                pe.wait_ge(*out_sb.at(n, 0))
                for i in range(2):
                    pe.wait_ge(*state_sb[i].at(n, 0))
                for t in range(GT):
                    mm = pe.transpose(ps[:, 6, t * P:(t + 1) * P], hn[:, t, :], ident[:])
                mm.then_inc(ht_ps.sem, 1)
                pe.wait_ge(*ht_sb.at(n, 1))
                for t in range(GT):
                    mm = pe.matmul(ps[:, 6, t * 2 * H:(t + 1) * 2 * H], ht[:, 3 + t * P:3 + (t + 1) * P], wba[:],
                                   start=True, stop=True)
                mm.then_inc(ba_ps.sem, 1)
                for u in range(NQK + NV):
                    pe.wait_ge(*use_sb.at(n, freed(u, SLOTS, USES)))
                    if u < NQK:
                        M, lhs = DK, (wq, wk)[u % 2][:, u // 2 * DK:(u // 2 + 1) * DK]
                    else:
                        M, lhs = P, wv[:, (u - NQK) * P:(u - NQK + 1) * P]
                    slot = 2 * (u % SLOTS)
                    pe.matmul(ps[0:M, slot, :], lhs, ht[:, 0:G], start=True, stop=True)
                    pe.matmul(ps[0:M, slot + 1, 0:3], lhs, ht[:, G:G + 3], start=True, stop=True).then_inc(use_ps.sem, 1)
                for u in range(NQK + NV, USES):
                    pe.wait_ge(*use_sb.at(n, freed(u, SLOTS, USES)))
                    for i in range(2):
                        k = 2 * (u - NQK - NV) + i
                        mm = pe.matmul(ps[:, 2 * (u % SLOTS) + i, :], ht[:, 3 + k // 3 * P:3 + (k // 3 + 1) * P],
                                       wg[:, k % 3 * 512:(k % 3 + 1) * 512], start=True, stop=True)
                    mm.then_inc(use_ps.sem, 1)
                pe.wait_ge(*za_step.at(n, 22))
                for i in range(3):
                    mm = pe.matmul(ps[:, 7, i * GT * H:(i + 1) * GT * H], sums[:, i, :], za[:, 0, :], start=True, stop=True)
                mm.then_inc(cum_ps.sem, 1)

                def heads(i):
                    return [(j, HG * i + j) for j in range(HG)]

                def start_chunk(t, i):
                    B = 4 * i
                    if t == 0:
                        pe.wait_ge(*decay_cut.at(n, 1))
                        pe.wait_ge(*use_sb.at(n, USES))
                        pe.wait_ge(*silu.at(n, NQK + NV))
                    pe.wait_ge(*state_sb[i].at(n, t))
                    for j, h in heads(i):
                        mm = pe.matmul(ps[:, B, j * P:(j + 1) * P], ex[:, DCUT, t, h:h + 1].to_broadcast([P, P]), ident[:],
                                       start=True, stop=True)
                    mm.then_inc(dec_ps[i].sem, 1)
                    pe.wait_ge(*ot_sb.at(n, 3 * t))
                    pe.wait_ge(*out_sb.at(n, t))
                    pe.wait_ge(*o_sb[i].at(n, t))
                    for j, h in heads(i):
                        mm = pe.matmul(ps[:, B + 1 + j // 2, j % 2 * 2 * P:(j % 2 + 1) * 2 * P], qk[:, h, 1, t * P:(t + 1) * P],
                                       qk[:, h, :, t * P:(t + 1) * P], start=True, stop=True)
                    mm.then_inc(kq_ps[i].sem, 1)

                def norms(t):
                    pe.wait_ge(*sq_sb.at(n, t + 1))
                    pe.wait_ge(*gd_sb[0].at(n, t + 1))
                    for k in range(2 * H):
                        mm = pe.matmul(ps[:, 0, k:k + 1], sq[:, k // 2, k % 2, :], sums[0:DK, 1, 0:1], start=True, stop=True)
                    mm.then_inc(n2_ps.sem, 1)

                def tokens_first(t, i):
                    B = 4 * i
                    pe.wait_ge(*(n2_sb.at(n, t + 1) if i == 0 else gd_sb[i].at(n, t + 1)))
                    for j, h in heads(i):
                        mm = pe.transpose(ps[:, B, j * DK:(j + 1) * DK], qk[:, h, 1, t * P:(t + 1) * P], ident[0:DK, 0:DK])
                    mm.then_inc(kt_ps[i].sem, 1)
                    pe.wait_ge(*al_sb[i].at(n, t + 1))
                    for j, h in heads(i):
                        mm = pe.transpose(ps[:, B + 3, j * P:(j + 1) * P], al[:, h, 1, :], ident[:])
                    mm.then_inc(lx_ps[i].sem, 1)
                    for k in range(6):
                        mm = pe.transpose(ps[:, B + 1 + k // 3, k % 3 * P:(k % 3 + 1) * P],
                                          vt[:, 6 * i + k, t * P:(t + 1) * P], ident[:])
                    mm.then_inc(vt_ps[i].sem, 1)

                def level_lx(t, i, m):
                    pe.wait_ge(*tm_sb[i].at(n, LEVELS * t + m))
                    pe.wait_ge(*am_sb[i].at(n, LEVELS * t + m))
                    for j, h in heads(i):
                        mm = pe.matmul(ps[:, 4 * i + 3, j * 64:(j + 1) * 64], al[:, h, 1, :], left(tm[:, h, :], m),
                                       start=True, stop=True)
                    mm.then_inc(lx_ps[i].sem, 1)

                def level_ty(t, i, m):
                    pe.wait_ge(*am_sb[i].at(n, LEVELS * t + m + 1))
                    pe.wait_ge(*tt_sb[i].at(n, LEVELS * t + m))
                    pe.wait_ge(*vb_sb[i].at(n, t + 1))
                    for j, h in heads(i):
                        mm = pe.matmul(ps[:, 4 * i + 2, j * 64:(j + 1) * 64], tt[:, h, :], am[:, h, :], start=True, stop=True)
                    mm.then_inc(ty_ps[i].sem, 1)

                def level_tt(t, i, m):
                    pe.wait_ge(*tm_sb[i].at(n, LEVELS * t + m + 1))
                    pe.wait_ge(*(vb_sb[i].at(n, t + 1) if m == 0 else tt_sb[i].at(n, LEVELS * t + m)))
                    for j, h in heads(i):
                        mm = pe.transpose(ps[:, 4 * i + 1, j * P:(j + 1) * P], tm[:, h, :], ident[:])
                    mm.then_inc(tt_ps[i].sem, 1)

                def pairs(i, banks, M, lhs, rhs, done):
                    for j, h in heads(i):
                        mm = pe.matmul(ps[0:M, 4 * i + banks[j // 2], j % 2 * DV:(j % 2 + 1) * DV], lhs(h), rhs(h),
                                       start=True, stop=True)
                    mm.then_inc(done.sem, 1)

                def from_state(t, i):
                    pe.wait_ge(*state_sb[i].at(n, t))
                    pe.wait_ge(*zeroed.at(b + 1, 2))
                    pe.wait_ge(*kd_sb[i].at(n, t + 1))
                    pe.wait_ge(*am_sb[i].at(n, LEVELS * t + LEVELS))
                    pairs(i, (0, 3), P, lambda h: qk[:, h, 1, t * P:(t + 1) * P], lambda h: state[:, h, :], ks_ps[i])

                def solve(t, i):
                    pe.wait_ge(*r_sb[i].at(n, t + 1))
                    pe.wait_ge(*tt_sb[i].at(n, LEVELS * t + LEVELS))
                    pairs(i, (1, 2), P, lambda h: tt[:, h, :], lambda h: vr[:, h, :], delta_ps[i])
                    pairs(i, (0, 3), P, lambda h: qk[:, h, 0, t * P:(t + 1) * P], lambda h: state[:, h, :], qs_ps[i])

                def outputs(t, i):
                    pe.wait_ge(*delta_sb[i].at(n, t + 1))
                    pairs(i, (1, 2), P, lambda h: al[:, h, 0, :], lambda h: delta[:, h, :], ad_ps[i])
                    pe.wait_ge(*qs_sb[i].at(n, t + 1))
                    pairs(i, (0, 3), DK, lambda h: kd[:, h, :], lambda h: delta[:, h, :], up_ps[i])

                def project_out(t):
                    for k in range(3):
                        if k == 0:
                            pe.wait_ge(*og_sb.at(n, t + 1))
                        for i in range(4):
                            m = 4 * k + i
                            mm = pe.transpose(ps[:, (1, 2, 5)[k], i * P:(i + 1) * P],
                                              o[:].rearrange("p h v -> p (h v)")[:, m * P:(m + 1) * P], ident[:])
                        mm.then_inc(ot_ps.sem, 1)
                    for m in range(NV):
                        pe.wait_ge(*ot_sb.at(n, 3 * t + m // 4 + 1))
                        mm = pe.matmul(ps[:, 6, 0:D], ot[:, m, :], wo[:, m, :], start=m == 0, stop=m == NV - 1)
                    mm.then_inc(y_ps.sem, 1)

                for t in range(GT):
                    for i in range(2):
                        start_chunk(t, i)
                    norms(t)
                    for i in range(2):
                        tokens_first(t, i)
                    for i in range(2):
                        level_tt(t, i, 0)
                    for m in range(1, LEVELS):
                        for i in range(2):
                            level_lx(t, i, m)
                        for i in range(2):
                            level_ty(t, i, m)
                        for i in range(2):
                            level_tt(t, i, m)
                    for i in range(2):
                        from_state(t, i)
                    for i in range(2):
                        solve(t, i)
                    for i in range(2):
                        outputs(t, i)
                    project_out(t)

        @block.scalar
        def _(act):
            ph.start(act, "act")
            act.wait_ge(wts_loaded, LOADED)
            act.activation(decay_rate[:], decay_rate[:], ACT.Exp).then_inc(prepared, 1)
            with act.Fori(0, NB) as b, act.Fori(0, NG) as g:
                n = act.snap(b * NG + g + 1)
                act.wait_ge(*ht_ps.at(n, 1))
                act.wait_ge(*use_ps.at(n, 0))
                act.wait_ge(*ht_halo.at(n, 0))
                act.activation(ht[:, 3:], ps[:, 6, :], ACT.Copy).then_inc(ht_sb.sem, 1)
                act.wait_ge(*za_step.at(n, 4))
                act.activation(za[:, 4, :], za[:, 3, :], ACT.Exp).then_inc(za_exp.sem, 1)
                act.activation(za[:, 5, :], za[:, 1, :], ACT.Exp, scale=-1.0).then_inc(za_exp.sem, 1)

                def taps(u):
                    M = DK if u < NQK else P
                    slot, k = 2 * (u % SLOTS), u % SLOTS
                    wts = conv_qk[:, u // 2, u % 2, :] if u < NQK else conv_v[:, u - NQK, :]
                    act.wait_ge(*use_ps.at(n, u + 1))
                    act.wait_ge(*tap.at(n, 3 * freed(u, SLOTS, NQK + NV)))
                    act.wait_ge(*silu.at(n, freed(u, SLOTS, NQK + NV)))
                    both_banks = ps[0:M, slot:slot + 2, :].rearrange("p a i -> p (a i)")
                    act.activation(raw[0:M, k, :], both_banks[:, 0:3 + G], ACT.Copy)
                    act.activation(conv[0:M, k, :], both_banks[:, 0:G], ACT.Copy, scale=wts[:, 0:1]).then_inc(use_sb.sem, 1)

                def activate(u):
                    M, k = (DK if u < NQK else P), u % SLOTS
                    act.wait_ge(*tap.at(n, 3 * u + 3))
                    to = qk[:, u // 2, u % 2, :] if u < NQK else vt[:, u - NQK, :]
                    if u == 0:
                        for i in range(2):
                            act.wait_ge(*qs_ps[i].at(n, 0))
                            act.wait_ge(*vt_ps[i].at(n, 0))
                    act.activation(to, conv[0:M, k, :], ACT.Silu).then_inc(silu.sem, 1)

                for u in range(NQK + NV):
                    taps(u)
                    if u >= 1:
                        activate(u - 1)
                activate(NQK + NV - 1)
                for u in range(NQK + NV, USES):
                    act.wait_ge(*use_ps.at(n, u + 1))
                    if u == NQK + NV:
                        act.wait_ge(*og_sb.at(n, 0))
                    k = 2 * (u - NQK - NV)
                    act.activation(gate[:].rearrange("p t v -> p (t v)")[:, k * 512:(k + 2) * 512],
                                   ps[:, 2 * (u % SLOTS):2 * (u % SLOTS) + 2, :].rearrange("p a i -> p (a i)"),
                                   ACT.Silu).then_inc(use_sb.sem, 1)
                act.wait_ge(*za_step.at(n, 22))
                act.activation(ex[:, DEC, :, :], za[:, 0, :].rearrange("p (t h) -> p t h", h=H), ACT.Exp).then_inc(ex_sb.sem, 1)
                act.wait_ge(*cum_ps.at(n, 1))
                act.activation(ex[:, PI:PI + 3, :, :].rearrange("p k t h -> p (k t h)"), ps[:, 7, 0:3 * GT * H], ACT.Exp)\
                    .then_inc(ex_sb.sem, 1)

                def heads(i):
                    return [(j, HG * i + j) for j in range(HG)]

                def tokens_first(t, i):
                    B = 4 * i
                    act.wait_ge(*kt_ps[i].at(n, t + 1))
                    act.wait_ge(*coef.at(n, 4 * t + 4))
                    act.wait_ge(*up_ps[i].at(n, t))
                    for j, h in heads(i):
                        e = act.activation(kd[:, h, :], ps[:, B, j * DK:(j + 1) * DK], ACT.Copy, scale=cf[:, KDF, h:h + 1])
                    e.then_inc(kd_sb[i].sem, 1)
                    act.wait_ge(*lx_ps[i].at(n, LEVELS * t))
                    act.wait_ge(*tt_ps[i].at(n, LEVELS * t))
                    act.activation(tm[:, HG * i:HG * i + HG, :], ident4[:], ACT.Copy).then_inc(tm_one[i].sem, 1)
                    act.wait_ge(*vt_ps[i].at(n, t + 1))
                    act.wait_ge(*delta_ps[i].at(n, t))
                    act.wait_ge(*om.at(n, 4 * t))
                    for j, h in heads(i):
                        e = act.activation(vr[:, h, :], ps[:, B + 1 + j // 2, j % 2 * DV:(j % 2 + 1) * DV], ACT.Copy,
                                           scale=ex[:, BETA, t, h:h + 1])
                    e.then_inc(vb_sb[i].sem, 1)

                def level_tt(t, i, m):
                    act.wait_ge(*tt_ps[i].at(n, LEVELS * t + m + 1))
                    if m == 0:
                        act.wait_ge(*delta_ps[i].at(n, t))
                    act.activation(tt[:, HG * i:HG * i + HG, :], ps[:, 4 * i + 1, :].rearrange("p (h k) -> p h k", k=P),
                                   ACT.Copy).then_inc(tt_sb[i].sem, 1)

                def solve(t, i):
                    act.wait_ge(*delta_ps[i].at(n, t + 1))
                    act.wait_ge(*up_ps[i].at(n, t))
                    act.activation(delta[:, HG * i:HG * i + HG, :].rearrange("p (a h) v -> p a (h v)", a=2),
                                   ps[:, 4 * i + 1:4 * i + 3, 0:2 * DV], ACT.Copy).then_inc(delta_sb[i].sem, 1)
                    act.wait_ge(*qs_ps[i].at(n, t + 1))
                    act.wait_ge(*ot_ps.at(n, 3 * t))
                    for j, h in heads(i):
                        e = act.activation(o[:, h, :], ps[:, 4 * i + 3 * (j // 2), j % 2 * DV:(j % 2 + 1) * DV], ACT.Copy,
                                           scale=ex[:, PI, t, h:h + 1])
                    e.then_inc(qs_sb[i].sem, 1)

                for t in range(GT):
                    for i in range(2):
                        tokens_first(t, i)
                    for m in range(LEVELS):
                        for i in range(2):
                            level_tt(t, i, m)
                    for i in range(2):
                        solve(t, i)
                    for i in range(2):
                        act.wait_ge(*o_sb[i].at(n, t + 1))
                        act.wait_ge(*delta_ps[i].at(n, t + 1))
                    act.activation(vr[:], o[:], ACT.Square).then_inc(osq.sem, 1)
                    for k in range(3):
                        act.wait_ge(*ot_ps.at(n, 3 * t + k + 1))
                        act.wait_ge(*y_ps.at(n, t))
                        act.activation(ot[:, 4 * k:4 * k + 4, :], ps[:, (1, 2, 5)[k], :].rearrange("p (m i) -> p m i", i=P),
                                       ACT.Copy).then_inc(ot_sb.sem, 1)

        @block.vector
        def _(dve):
            ph.start(dve, "dve")
            dve.memset(cf[:], 0.0).then_inc(seen, 1)
            dve.wait_ge(wts_loaded, LOADED)
            dve.tensor_tensor(wo[:], wo[:], onorm[:].unsqueeze(2).to_broadcast([P, NV, D]), ALU.mult)
            for wt in (wq, wk, wv, wg):
                dve.tensor_scalar(wt[:], wt[:], norm1[:], None, ALU.mult)
            dve.tensor_scalar(wba[:], wba[:], norm1[:], None, ALU.mult).then_inc(prepared, 1)
            dve.wait_ge(prepared, 2)
            dve.tensor_scalar(decay_rate[:], decay_rate[:], -1.0, None, ALU.mult).then_inc(prepared, 1)
            dve.wait_ge(prepared, 3)
            with dve.Fori(0, NB) as b:
                n0 = dve.snap(b * NG + 1)
                for i in range(2):
                    dve.wait_ge(*state_sb[i].at(n0, 0))
                dve.memset(state[:], 0.0).then_inc(zeroed.sem, 1)
                dve.wait_ge(*ht_halo.at(n0, 0))
                dve.memset(ht[:, 0:3], 0.0).then_inc(zeroed.sem, 1)
                with dve.Fori(0, NG) as g:
                    n = dve.snap(b * NG + g + 1)
                    dve.wait_ge(*x_loaded.at(n, 16))
                    for t in range(GT):
                        dve.bn_stats(stats[:, t, :], x[:, t, :]).then_inc(stats_done.sem, 1)
                    dve.wait_ge(*stats_done.at(n, GT))
                    dve.sem_inc(seen, 1)
                    for t in range(GT):
                        dve.bn_aggr(mv[:, t, :], stats[:, t, :]).then_inc(moments.sem, 1)
                    dve.wait_ge(*moments.at(n, GT))
                    dve.tensor_scalar(ms[:, 0, :], mv[:, :, 1], 1e-5, None, ALU.add).then_inc(root1.sem, 1)
                    dve.wait_ge(*root1_done.at(n, 1))
                    dve.tensor_tensor(ms[:, 1, :], rstd[:, 0, :], rstd[:, 0, :], ALU.mult).then_inc(root2.sem, 1)
                    for t in range(GT):
                        ln = dve.tensor_scalar(y[:, t, :], x[:, t, :], mv[:, t, 0:1], rstd[:, 0, t:t + 1], ALU.subtract, ALU.mult)
                    ln.then_inc(y_sb.sem, 1)
                    dve.wait_ge(*root2.at(n, 1))
                    dve.tensor_tensor(ms[:, 1, :], ms[:, 1, :], mv[:, :, 1], ALU.mult).then_inc(root2.sem, 1)
                    dve.wait_ge(*root2.at(n, 2))
                    dve.tensor_scalar(ms[:, 1, :], ms[:, 1, :], 1e-6, None, ALU.add).then_inc(root2.sem, 2)
                    dve.wait_ge(*root2_done.at(n, 1))
                    dve.wait_ge(*y_sb.at(n, 1))
                    dve.tensor_tensor(hn[:], y[:], rstd[:, 1, :].unsqueeze(2).to_broadcast([P, GT, D]), ALU.mult)\
                        .then_inc(hn_sb.sem, 1)

                    step = [0]

                    def then(ins):
                        step[0] += 1
                        ins.then_inc(za_step.sem, 1)
                        dve.wait_ge(*za_step.at(n, step[0]))

                    ba = ps[:, 6, 0:GT * 2 * H].rearrange("p (t r h) -> p r t h", t=GT, r=2)

                    def row(k):
                        return za[:, k, :]

                    def row3(k):
                        return za[:, k, :].rearrange("p (t h) -> p t h", h=H)

                    dve.wait_ge(*ba_ps.at(n, 1))
                    then(dve.tensor_copy(row3(1), ba[:, 0]))
                    then(dve.tensor_tensor(row3(2), ba[:, 1], dt_bias[:].unsqueeze(1).to_broadcast([P, GT, H]), ALU.add))
                    then(dve.tensor_scalar(row(3), row(2), -1.0, None, ALU.mult))
                    then(dve.tensor_tensor(row(3), row(3), row(2), ALU.min))
                    dve.wait_ge(*za_exp.at(n, 2))
                    then(dve.tensor_scalar(row(6), row(4), 2.0, None, ALU.add))
                    then(dve.reciprocal(row(6), row(6)))
                    then(dve.tensor_tensor(row(6), row(6), row(4), ALU.mult))
                    then(dve.tensor_tensor(row(7), row(6), row(6), ALU.mult))
                    then(dve.tensor_scalar(row(8), row(7), 1.0 / 17, None, ALU.mult))
                    for k in (15, 13, 11, 9, 7, 5, 3):
                        then(dve.scalar_tensor_tensor(out=row(8), in0=row(8), scalar=1.0 / k, in1=row(7), op0=ALU.add, op1=ALU.mult))
                    then(dve.scalar_tensor_tensor(out=row(8), in0=row(8), scalar=1.0, in1=row(6), op0=ALU.add, op1=ALU.mult))
                    then(dve.tensor_scalar(row(9), row(2), 0.0, None, ALU.max))
                    then(dve.scalar_tensor_tensor(out=row(9), in0=row(8), scalar=2.0, in1=row(9), op0=ALU.mult, op1=ALU.add))
                    then(dve.tensor_tensor(row3(9), row3(9), decay_rate[:].unsqueeze(1).to_broadcast([P, GT, H]), ALU.mult))
                    then(dve.tensor_scalar(row(5), row(5), 1.0, None, ALU.add))
                    for i in range(2):
                        dve.wait_ge(*vb_sb[i].at(n, 0))
                        dve.wait_ge(*dec_ps[i].at(n, 0))
                    dve.wait_ge(*cum_ps.at(n, 0))
                    dve.tensor_scalar(row(0), row(9), -1e4, None, ALU.max)
                    dve.reciprocal(ex[:, BETA, :, :], row3(5)).then_inc(za_step.sem, 1)

                    for u in range(NQK + NV):
                        M, k = (DK if u < NQK else P), u % SLOTS
                        wts = conv_qk[:, u // 2, u % 2, :] if u < NQK else conv_v[:, u - NQK, :]
                        dve.wait_ge(*use_sb.at(n, u + 1))
                        for i in range(1, 4):
                            if i > 1:
                                dve.wait_ge(*tap.at(n, 3 * u + i - 1))
                            dve.scalar_tensor_tensor(out=conv[0:M, k, :], in0=raw[0:M, k, i:i + G], scalar=wts[:, i:i + 1],
                                                     in1=conv[0:M, k, :], op0=ALU.mult, op1=ALU.add).then_inc(tap.sem, 1)
                    dve.wait_ge(*use_ps.at(n, USES))
                    dve.tensor_copy(ht[:, 0:3], ht[:, G:G + 3]).then_inc(ht_halo.sem, 1)
                    dve.wait_ge(*ex_sb.at(n, 2))
                    dve.tensor_scalar(ex[:, DCUT, :, :], ex[:, DEC, :, :], not_first[:], None, ALU.mult).then_inc(decay_cut.sem, 1)

                    def heads(i):
                        return [(j, HG * i + j) for j in range(HG)]

                    def decays(t, i):
                        dve.wait_ge(*dec_ps[i].at(n, t + 1))
                        dve.tensor_tensor_scan(gd[:, HG * i:HG * i + HG, :].rearrange("p h k -> p (h k)"), ps[:, 4 * i, :],
                                               ident4[:].rearrange("p h k -> p (h k)"), 0.0, ALU.mult, ALU.add)\
                            .then_inc(gd_sb[i].sem, 1)

                    def norms(t):
                        dve.wait_ge(*n2_ps.at(n, t + 1))
                        dve.wait_ge(*rn_sb.at(n, t))
                        dve.tensor_scalar(cf[:, N2E, :], ps[:, 0, 0:2 * H], 1e-6, None, ALU.add).then_inc(n2_sb.sem, 1)
                        dve.wait_ge(*rn_sb.at(n, t + 1))
                        rk = cf[:, RN, :].rearrange("p (h r) -> p h r", r=2)[:, :, 1]
                        rq = cf[:, RN, :].rearrange("p (h r) -> p h r", r=2)[:, :, 0]
                        dve.tensor_tensor(cf[:, BRK, 0:H], rk, ex[:, BETA, t, :], ALU.mult).then_inc(coef.sem, 1)
                        dve.tensor_tensor(cf[:, KDF, 0:H], rk, ex[:, DLAST, t, :], ALU.mult)
                        dve.tensor_scalar(cf[:, RQS, 0:H], rq, DK ** -0.5, None, ALU.mult).then_inc(coef.sem, 1)
                        dve.wait_ge(*coef.at(n, 4 * t + 1))
                        dve.scalar_tensor_tensor(out=cf[:, NPB, 0:H], in0=cf[:, BRK, 0:H], scalar=-1.0, in1=ex[:, PI, t, :],
                                                 op0=ALU.mult, op1=ALU.mult).then_inc(coef.sem, 1)
                        dve.wait_ge(*coef.at(n, 4 * t + 2))
                        dve.tensor_tensor(cf[:, RQ2, 0:H], cf[:, RQS, 0:H], cf[:, RQS, 0:H], ALU.mult).then_inc(coef.sem, 1)
                        dve.wait_ge(*coef.at(n, 4 * t + 4))

                    def products(t, i):
                        dve.wait_ge(*kq_ps[i].at(n, t + 1))
                        dve.wait_ge(*gd_sb[i].at(n, t + 1))
                        for j, h in heads(i):
                            qk_ps = ps[:, 4 * i + 1 + j // 2, j % 2 * 2 * P:(j % 2 + 1) * 2 * P].rearrange("p (r k) -> p r k", r=2)
                            rk = cf[:, RN, 2 * h + 1:2 * h + 2]
                            e = dve.scalar_tensor_tensor(out=al[:, h, :, :], in0=qk_ps, scalar=rk,
                                                         in1=gd[:, h, :].unsqueeze(1).to_broadcast([P, 2, P]),
                                                         op0=ALU.mult, op1=ALU.mult)
                        e.then_inc(al_sb[i].sem, 1)

                    def level_am(t, i, m):
                        dve.wait_ge(*lx_ps[i].at(n, LEVELS * t + m + 1))
                        for j, h in heads(i):
                            if m == 0:
                                lx = left(ps[:, 4 * i + 3, j * P:(j + 1) * P], 0)
                                e = dve.scalar_tensor_tensor(out=am[:, h, :].unsqueeze(2), in0=lx, scalar=cf[:, BRK, h:h + 1],
                                                             in1=blocks[:, 0, :].unsqueeze(2), op0=ALU.mult, op1=ALU.mult)
                            else:
                                lx = ps[:, 4 * i + 3, j * 64:(j + 1) * 64]
                                e = dve.scalar_tensor_tensor(out=am[:, h, :], in0=lx, scalar=cf[:, BRK, h:h + 1],
                                                             in1=blocks[:, m, :], op0=ALU.mult, op1=ALU.mult)
                        e.then_inc(am_sb[i].sem, 1)

                    def level_tm(t, i, m):
                        half = left4(tm[:, HG * i:HG * i + HG, :], m)
                        if m == 0:
                            dve.wait_ge(*tm_one[i].at(n, t + 1))
                            dve.wait_ge(*am_sb[i].at(n, LEVELS * t + 1))
                            more = am[:, HG * i:HG * i + HG, :].rearrange("p h (n s) -> p h n s", s=1)
                        else:
                            dve.wait_ge(*ty_ps[i].at(n, (LEVELS - 1) * t + m))
                            dve.wait_ge(*tm_sb[i].at(n, LEVELS * t + m))
                            more = ps[:, 4 * i + 2, 0:HG * 64].rearrange("p (h n s) -> p h n s", h=HG, s=1 << m)
                        dve.tensor_tensor(half, half, more, ALU.add).then_inc(tm_sb[i].sem, 1)

                    def rest(t, i):
                        dve.wait_ge(*ks_ps[i].at(n, t + 1))
                        dve.wait_ge(*vb_sb[i].at(n, t + 1))
                        for j, h in heads(i):
                            e = dve.scalar_tensor_tensor(out=vr[:, h, :],
                                                         in0=ps[:, 4 * i + 3 * (j // 2), j % 2 * DV:(j % 2 + 1) * DV],
                                                         scalar=cf[:, NPB, h:h + 1], in1=vr[:, h, :], op0=ALU.mult, op1=ALU.add)
                        e.then_inc(r_sb[i].sem, 1)

                    def outputs(t, i):
                        dve.wait_ge(*ad_ps[i].at(n, t + 1))
                        dve.wait_ge(*qs_sb[i].at(n, t + 1))
                        mine = o[:, HG * i:HG * i + HG, :].rearrange("p (a h) v -> p a (h v)", a=2)
                        dve.tensor_tensor(mine, mine, ps[:, 4 * i + 1:4 * i + 3, 0:2 * DV], ALU.add).then_inc(o_sb[i].sem, 1)
                        dve.wait_ge(*up_ps[i].at(n, t + 1))
                        dve.wait_ge(*qs_ps[i].at(n, t + 1))
                        dve.wait_ge(*state_sb[i].at(n, t))
                        dve.wait_ge(*zeroed.at(b + 1, 2))
                        for j, h in heads(i):
                            e = dve.scalar_tensor_tensor(out=state[:, h, :], in0=state[:, h, :], scalar=ex[0:DK, PLAST, t, h:h + 1],
                                                         in1=ps[0:DK, 4 * i + 3 * (j // 2), j % 2 * DV:(j % 2 + 1) * DV],
                                                         op0=ALU.mult, op1=ALU.add)
                        e.then_inc(state_sb[i].sem, 1)

                    def gated_norm(t):
                        dve.wait_ge(*osq.at(n, t + 1))
                        dve.tensor_reduce(cf[:, OSUM, 0:H], vr[:], AX.X, ALU.add).then_inc(om.sem, 1)
                        dve.wait_ge(*om.at(n, 4 * t + 1))
                        dve.scalar_tensor_tensor(out=cf[:, OMS, 0:H], in0=cf[:, OSUM, 0:H], scalar=1.0 / DV,
                                                 in1=cf[:, RQ2, 0:H], op0=ALU.mult, op1=ALU.mult).then_inc(om.sem, 1)
                        dve.wait_ge(*om.at(n, 4 * t + 2))
                        dve.tensor_scalar(cf[:, OME, 0:H], cf[:, OMS, 0:H], 1e-6, None, ALU.add).then_inc(om.sem, 1)
                        dve.wait_ge(*orn.at(n, t + 1))
                        dve.tensor_tensor(cf[:, OF, 0:H], cf[:, ORN, 0:H], cf[:, RQS, 0:H], ALU.mult).then_inc(om.sem, 1)
                        dve.wait_ge(*om.at(n, 4 * t + 4))
                        for h in range(H):
                            e = dve.scalar_tensor_tensor(out=o[:, h, :], in0=o[:, h, :], scalar=cf[:, OF, h:h + 1],
                                                         in1=gate[:, t, h * DV:(h + 1) * DV], op0=ALU.mult, op1=ALU.mult)
                        e.then_inc(og_sb.sem, 1)

                    def add_out(t):
                        dve.wait_ge(*y_ps.at(n, t + 1))
                        if t == 0:
                            dve.wait_ge(*stored.at(n, 0))
                        dve.tensor_tensor(out[:, t, :], ps[:, 6, 0:D], y[:, t, :], ALU.add).then_inc(out_sb.sem, 1)

                    for t in range(GT):
                        for i in range(2):
                            decays(t, i)
                        norms(t)
                        for i in range(2):
                            products(t, i)
                        for m in range(LEVELS):
                            for i in range(2):
                                level_am(t, i, m)
                            for i in range(2):
                                level_tm(t, i, m)
                        for i in range(2):
                            rest(t, i)
                        for i in range(2):
                            outputs(t, i)
                        gated_norm(t)
                        add_out(t)
    ph.close()


def gated_mlp(nc, name, src, dst, c, hidden, func, layernorm, eps, w_up, w_gate, w_down, norm_w, norm_b=None,
              b_up=None, b_gate=None, b_down=None, shifted=False, skip=None):
    chunks = [(a, min(P, hidden - a)) for a in range(0, hidden, P)]
    NC = len(chunks)
    biased = b_up is not None
    extra = int(biased)
    assert not biased or chunks[-1][1] < P
    ph = Phase(nc, name)
    sb, signal = ph.sb, ph.counter
    ps = ph.banks()
    up_w = sb("up_w", [P, hidden])
    gate_w = sb("gate_w", [P, hidden])
    down_w = sb("down_w", [P, NC, D])
    scale = sb("scale", [P, 1])
    shift = sb("shift", [P, 1])
    up_b = sb("up_b", [P, NC])
    gate_b = sb("gate_b", [P, NC])
    ident = sb("ident", [P, P])
    minus_half = sb("minus_half", [P, GT])
    h = sb("h", [P, GT, D])
    x = sb("x", [P, GT, D])
    x2 = sb("x2", [P, GT, D])
    y = sb("y", [P, GT, D])
    stats = sb("stats", [P, GT, 6])
    mv = sb("mv", [P, GT, 2])
    ms = sb("ms", [P, 2, GT])
    rstd = sb("rstd", [P, GT])
    hn = sb("hn", [P, GT, D])
    ht = sb("ht", [P, G])
    gate = sb("gate", [P, 2, G])
    prod = sb("prod", [P, NC, G])

    loaded = ph.semaphore("loaded")
    prepared = ph.semaphore("prepared")
    NH = 2 if shifted else 1
    NX = 2 if skip is not None else 1
    h_loaded = signal("h_loaded", 16 * NH, "sp")
    x_loaded = signal("x_loaded", 16 * NX, "sp")
    stored = signal("stored", 16, "sp")
    stats_done = signal("stats_done", GT, "dve")
    seen = signal("seen", 1, "dve").sem
    moments = signal("moments", GT, "dve")
    under_root = signal("under_root", 3, "dve")
    root = signal("root", 1, "pool")
    normed = signal("normed", GT, "dve")
    ht_ps = signal("ht_ps", 1, "pe")
    ht_sb = signal("ht_sb", 1, "act")
    up_gate_ps = signal("up_gate_ps", NC, "pe")
    gated = signal("gated", NC, "act")
    prod_sb = signal("prod_sb", NC, "dve")
    y_ps = signal("y_ps", 1, "pe")
    y_sb = signal("y_sb", NX, "dve")

    loads = [(up_w[:], w_up), (gate_w[:], w_gate), (ident[:], c["ident"]), (minus_half[:], c["minus_half"][:, 0:GT]),
             (scale[:], norm_w)]
    for n, (a, m) in enumerate(chunks):
        loads.append((down_w[0:m, n, :], w_down(a, m)))
        if biased:
            loads += [(up_b[0:m, n:n + 1], b_up(a, m)), (gate_b[0:m, n:n + 1], b_gate(a, m))]
    if biased:
        loads += [(shift[:], norm_b), (down_w[chunks[-1][1]:chunks[-1][1] + 1, NC - 1, :], b_down)]

    with nc.Block() as block:

        @block.sync
        def _(sp):
            ph.start(sp, "sp")
            for out, in_ in loads:
                sp.dma_start(out, in_).then_inc(loaded, 16)
            with sp.Fori(0, NB) as b, sp.Fori(0, NG) as g:
                n = sp.snap(b * NG + g + 1)
                row = sp.snap(scratch_row(b, g))
                sp.wait_ge(*normed.at(n, 0))
                if shifted:
                    sp.dma_start(h[:, :, 0:D // 2], tiles(src[bass.ds(row, G), 0:D // 2])).then_inc(h_loaded.sem, 16)
                    sp.dma_start(h[:, :, D // 2:D], tiles(src[bass.ds(row - 1, G), D // 2:D])).then_inc(h_loaded.sem, 16)
                else:
                    sp.dma_start(h[:], tiles(src[bass.ds(row, G), :])).then_inc(h_loaded.sem, 16)
                sp.wait_ge(*y_sb.at(n, 0))
                sp.dma_start(x[:], tiles(src[bass.ds(row, G), :])).then_inc(x_loaded.sem, 16)
                if skip is not None:
                    sp.dma_start(x2[:], tiles(skip[bass.ds((b * NG + g) * G, G), :])).then_inc(x_loaded.sem, 16)
                sp.wait_ge(*y_sb.at(n, NX))
                sp.dma_start(tiles(dst[bass.ds(row, G), :]), y[:]).then_inc(stored.sem, 16)
            sp.wait_ge(*stored.at(TURNS + 1, 0))

        @block.gpsimd
        def _(pool):
            ph.start(pool, "pool")
            pool.memset(prod[:, NC - 1, :], 1.0).then_inc(prepared, 1)
            pool.wait_ge(loaded, 16 * len(loads))
            with pool.Fori(0, NB) as b, pool.Fori(0, NG) as g:
                n = pool.snap(b * NG + g + 1)
                pool.wait_ge(*under_root.at(n, 3))
                pool.wait_ge(*normed.at(n, 0))
                pool.tensor_tensor(rstd[:], ms[:, 1, :], minus_half[:], ALU.pow).then_inc(root.sem, 1)

        @block.tensor
        def _(pe):
            ph.start(pe, "pe")
            pe.wait_ge(loaded, 16 * len(loads))
            pe.wait_ge(prepared, 1)
            with pe.Fori(0, NB) as b, pe.Fori(0, NG) as g:
                n = pe.snap(b * NG + g + 1)
                for t in range(GT):
                    pe.wait_ge(*normed.at(n, t + 1))
                    mm = pe.transpose(ps[:, 0, t * P:(t + 1) * P], hn[:, t, :], ident[:])
                mm.then_inc(ht_ps.sem, 1)
                pe.wait_ge(*ht_sb.at(n, 1))
                for i, (a, m) in enumerate(chunks):
                    pe.wait_ge(*prod_sb.at(n, freed(i, 3, NC)))
                    pe.matmul(ps[0:m, 1 + 2 * (i % 3), :], gate_w[:, a:a + m], ht[:], start=True, stop=True)
                    pe.matmul(ps[0:m, 2 + 2 * (i % 3), :], up_w[:, a:a + m], ht[:], start=True, stop=True)\
                        .then_inc(up_gate_ps.sem, 1)
                pe.wait_ge(*prod_sb.at(n, NC))
                pe.wait_ge(*y_sb.at(n, 0))
                for t in range(GT):
                    for i, (a, m) in enumerate(chunks):
                        k = m + (extra if i == NC - 1 else 0)
                        mm = pe.matmul(ps[:, 7, t * P:(t + 1) * P], prod[0:k, i, t * P:(t + 1) * P], down_w[0:k, i, :],
                                       start=i == 0, stop=i == NC - 1)
                mm.then_inc(y_ps.sem, 1)

        @block.scalar
        def _(act):
            ph.start(act, "act")
            act.wait_ge(loaded, 16 * len(loads))
            with act.Fori(0, NB) as b, act.Fori(0, NG) as g:
                n = act.snap(b * NG + g + 1)
                act.wait_ge(*ht_ps.at(n, 1))
                act.wait_ge(*up_gate_ps.at(n, 0))
                act.activation(ht[:], ps[:, 0, :], ACT.Identity, scale=scale[:],
                               bias=shift[:] if biased else 0.0).then_inc(ht_sb.sem, 1)
                for i, (a, m) in enumerate(chunks):
                    act.wait_ge(*up_gate_ps.at(n, i + 1))
                    act.wait_ge(*prod_sb.at(n, freed(i, 2, NC)))
                    act.activation(gate[0:m, i % 2, :], ps[0:m, 1 + 2 * (i % 3), :], func,
                                   bias=gate_b[0:m, i:i + 1] if biased else 0.0).then_inc(gated.sem, 1)

        @block.vector
        def _(dve):
            ph.start(dve, "dve")
            dve.wait_ge(loaded, 16 * len(loads))
            dve.wait_ge(prepared, 1)
            with dve.Fori(0, NB) as b, dve.Fori(0, NG) as g:
                n = dve.snap(b * NG + g + 1)
                dve.wait_ge(*h_loaded.at(n, 16 * NH))
                for t in range(GT):
                    dve.bn_stats(stats[:, t, :], h[:, t, :]).then_inc(stats_done.sem, 1)
                dve.wait_ge(*stats_done.at(n, GT))
                dve.sem_inc(seen, 1)
                for t in range(GT):
                    dve.bn_aggr(mv[:, t, :], stats[:, t, :]).then_inc(moments.sem, 1)
                dve.wait_ge(*moments.at(n, GT))
                if layernorm:
                    dve.tensor_scalar(ms[:, 1, :], mv[:, :, 1], eps, None, ALU.add).then_inc(under_root.sem, 3)
                else:
                    dve.tensor_tensor(ms[:, 0, :], mv[:, :, 0], mv[:, :, 0], ALU.mult).then_inc(under_root.sem, 1)
                    dve.wait_ge(*under_root.at(n, 1))
                    dve.tensor_tensor(ms[:, 0, :], ms[:, 0, :], mv[:, :, 1], ALU.add).then_inc(under_root.sem, 1)
                    dve.wait_ge(*under_root.at(n, 2))
                    dve.tensor_scalar(ms[:, 1, :], ms[:, 0, :], eps, None, ALU.add).then_inc(under_root.sem, 1)
                dve.wait_ge(*root.at(n, 1))
                dve.wait_ge(*ht_ps.at(n, 0))
                for t in range(GT):
                    if layernorm:
                        dve.tensor_scalar(hn[:, t, :], h[:, t, :], mv[:, t, 0:1], rstd[:, t:t + 1], ALU.subtract, ALU.mult)\
                            .then_inc(normed.sem, 1)
                    else:
                        dve.tensor_scalar(hn[:, t, :], h[:, t, :], rstd[:, t:t + 1], None, ALU.mult)\
                            .then_inc(normed.sem, 1)
                for i, (a, m) in enumerate(chunks):
                    dve.wait_ge(*gated.at(n, i + 1))
                    if i == 0:
                        dve.wait_ge(*y_ps.at(n, 0))
                    up = ps[0:m, 2 + 2 * (i % 3), :]
                    if biased:
                        dve.scalar_tensor_tensor(out=prod[0:m, i, :], in0=up, scalar=up_b[0:m, i:i + 1],
                                                 in1=gate[0:m, i % 2, :], op0=ALU.add, op1=ALU.mult).then_inc(prod_sb.sem, 1)
                    else:
                        dve.tensor_tensor(prod[0:m, i, :], up, gate[0:m, i % 2, :], ALU.mult).then_inc(prod_sb.sem, 1)
                dve.wait_ge(*x_loaded.at(n, 16 * NX))
                dve.wait_ge(*stored.at(n, 0))
                dve.wait_ge(*y_ps.at(n, 1))
                dve.tensor_tensor(y[:], ps[:, 7, :].rearrange("p (t d) -> p t d", d=D), x[:], ALU.add).then_inc(y_sb.sem, 1)
                if skip is not None:
                    dve.wait_ge(*y_sb.at(n, 1))
                    dve.tensor_tensor(y[:], y[:], x2[:], ALU.add).then_inc(y_sb.sem, 1)
    ph.close()


def add_and_norm(nc, name, a, b_, x_out, y_out, c):
    ph = Phase(nc, name)
    sb, signal = ph.sb, ph.counter
    minus_half = sb("minus_half", [P, GT])
    x = sb("x", [P, GT, D])
    more = sb("more", [P, GT, D])
    total = sb("total", [P, GT, D])
    y = sb("y", [P, GT, D])
    stats = sb("stats", [P, GT, 6])
    mv = sb("mv", [P, GT, 2])
    var = sb("var", [P, GT])
    rstd = sb("rstd", [P, GT])
    const_loaded = ph.semaphore("const_loaded")
    N_IN = 1 + (b_ is not None)
    N_OUT = (x_out is not None) + (y_out is not None)
    loaded = signal("loaded", 16 * N_IN, "sp")
    stored = signal("stored", 16 * N_OUT, "sp")
    added = signal("added", 1, "dve")
    stats_done = signal("stats_done", GT, "dve")
    seen = signal("seen", 1, "dve").sem
    moments = signal("moments", GT, "dve")
    under_root = signal("under_root", 1, "dve")
    root = signal("root", 1, "pool")
    normed = signal("normed", GT, "dve")

    with nc.Block() as block:

        @block.sync
        def _(sp):
            ph.start(sp, "sp")
            sp.dma_start(minus_half[:], c["minus_half"][:, 0:GT]).then_inc(const_loaded, 16)
            with sp.Fori(0, NB) as b, sp.Fori(0, NG) as g:
                n = sp.snap(b * NG + g + 1)
                sp.wait_ge(*added.at(n, 0))
                sp.dma_start(x[:], tiles(a[0][bass.ds(a[1](b, g), G), :])).then_inc(loaded.sem, 16)
                if b_ is not None:
                    sp.dma_start(more[:], tiles(b_[0][bass.ds(b_[1](b, g), G), :])).then_inc(loaded.sem, 16)
                sp.wait_ge(*added.at(n, 1))
                if x_out is not None:
                    sp.dma_start(tiles(x_out[0][bass.ds(x_out[1](b, g), G), :]), total[:]).then_inc(stored.sem, 16)
                if y_out is not None:
                    sp.wait_ge(*normed.at(n, GT))
                    sp.dma_start(tiles(y_out[0][bass.ds(y_out[1](b, g), G), :]), y[:]).then_inc(stored.sem, 16)
            sp.wait_ge(*stored.at(TURNS + 1, 0))

        @block.gpsimd
        def _(pool):
            ph.start(pool, "pool")
            pool.wait_ge(const_loaded, 16)
            if y_out is not None:
                with pool.Fori(0, NB) as b, pool.Fori(0, NG) as g:
                    n = pool.snap(b * NG + g + 1)
                    pool.wait_ge(*under_root.at(n, 1))
                    pool.tensor_tensor(rstd[:], var[:], minus_half[:], ALU.pow).then_inc(root.sem, 1)

        @block.vector
        def _(dve):
            ph.start(dve, "dve")
            with dve.Fori(0, NB) as b, dve.Fori(0, NG) as g:
                n = dve.snap(b * NG + g + 1)
                dve.wait_ge(*loaded.at(n, 16 * N_IN))
                dve.wait_ge(*stored.at(n, 0))
                if b_ is not None:
                    dve.tensor_tensor(total[:], x[:], more[:], ALU.add).then_inc(added.sem, 1)
                else:
                    dve.tensor_copy(total[:], x[:]).then_inc(added.sem, 1)
                if y_out is not None:
                    dve.wait_ge(*added.at(n, 1))
                    for t in range(GT):
                        dve.bn_stats(stats[:, t, :], total[:, t, :]).then_inc(stats_done.sem, 1)
                    dve.wait_ge(*stats_done.at(n, GT))
                    dve.sem_inc(seen, 1)
                    for t in range(GT):
                        dve.bn_aggr(mv[:, t, :], stats[:, t, :]).then_inc(moments.sem, 1)
                    dve.wait_ge(*moments.at(n, GT))
                    dve.tensor_scalar(var[:], mv[:, :, 1], 1e-5, None, ALU.add).then_inc(under_root.sem, 1)
                    dve.wait_ge(*root.at(n, 1))
                    for t in range(GT):
                        dve.tensor_scalar(y[:, t, :], total[:, t, :], mv[:, t, 0:1], rstd[:, t:t + 1],
                                          ALU.subtract, ALU.mult).then_inc(normed.sem, 1)
    ph.close()


def token_row(b, g):
    return (b * NG + g) * G


def clear_padding(nc, arrays, c):
    ph = Phase(nc, "padding")
    cleared = ph.semaphore("cleared")
    with nc.Block() as block:
        @block.sync
        def _(sp):
            for a in arrays:
                sp.dma_start(a.rearrange("(b r) c -> b r c", b=NB)[:, PAD - 1, :], c["zero_rows"]).then_inc(cleared, 16)
            sp.wait_ge(cleared, 16 * len(arrays))
    ph.close()


def ffn_block(nc, name, y0, y1, w, c):
    HID = w["w2"].shape[0] // DEPTH
    with nc.Fori(0, DEPTH) as l:
        local_attention(nc, name + "a", y0, y1, l, w, c)
        gated_mlp(nc, name + "m", y1, y0, c, HID, ACT.Gelu, True, 1e-5,
                  w_up=w["w1"][bass.ds(l * D, D), 0:HID], w_gate=w["w1"][bass.ds(l * D, D), HID:2 * HID],
                  w_down=lambda a, m: w["w2"][bass.ds(l * HID + a, m), :],
                  norm_w=w["ln_g"][bass.ds(l * D, D), :], norm_b=w["ln_b"][bass.ds(l * D, D), :],
                  b_up=lambda a, m: w["b1"][bass.ds(l * 2 * HID + a, m), :],
                  b_gate=lambda a, m: w["b1"][bass.ds(l * 2 * HID + HID + a, m), :],
                  b_down=w["b2"][bass.ds(l, 1), :], shifted=True)


def hybrid_block(nc, x, a, b, f, c, out):
    def scratch(name):
        return nc.dram_tensor(name, (NB * ROWS, D), F32).ap()
    x1, x2, x3, y0, y1 = (scratch(n) for n in ("x1", "x2", "x3", "y0", "y1"))
    clear_padding(nc, (y0, y1), c)
    delta_attention(nc, "delta", x, y0, a, c)
    gated_mlp(nc, "mlp", y0, x1, c, a["Wup"].shape[1], ACT.Silu, False, 1e-6, w_up=a["Wup"], w_gate=a["Wgate"],
              w_down=lambda r, m: a["Wdown"][r:r + m, :], norm_w=a["norm2_w"], skip=x)
    add_and_norm(nc, "norm_a", (x1, scratch_row), None, None, (y0, scratch_row), c)
    ffn_block(nc, "f", y0, y1, f, c)
    add_and_norm(nc, "norm_b", (x1, scratch_row), (y0, scratch_row), (x2, scratch_row), (y1, scratch_row), c)
    window_attention(nc, "window", y1, x2, x3, b, c)
    add_and_norm(nc, "norm_c", (x3, scratch_row), None, None, (y0, scratch_row), c)
    ffn_block(nc, "g", y0, y1, f, c)
    add_and_norm(nc, "last", (x3, scratch_row), (y0, scratch_row), (out, token_row), None, c)



def shape_constants():
    import numpy as np

    T, P, W, DH = 1024, 128, 64, 64
    c = {"ident": np.eye(P, dtype=np.float32)}
    c["minus_half"] = np.full((P, 64), -0.5, np.float32)
    c["own_head"] = (np.arange(P)[:, None] // 8 % 4 == np.arange(4)[None, :]).astype(np.float32)
    i = np.arange(P)
    c["sums"] = np.concatenate([i[:, None] <= i, np.ones((P, P)), i[:, None] > i], 1).astype(np.float32)
    c["not_first"] = (i[:, None] > 0).astype(np.float32)
    levels = []
    for m in range(7):
        s = 1 << m
        cols = i[i // s % 2 == 0]
        levels.append(-((i[:, None] // s % 2 == 1) & (i[:, None] // (2 * s) == cols // (2 * s))).astype(np.float32))
    c["blocks"] = np.concatenate(levels, 1)
    c["zero_rows"] = np.zeros((4, 128), np.float32)
    q = np.arange(P)[:, None]
    k = np.arange(W + P)[None, :]
    for name, first in (("ffn_mask", q), ("attn_mask", q + 1)):
        seen = (k >= first) & (k <= q + W)
        edge = seen & (k >= W)
        m = np.where(np.stack([edge, edge, seen, seen], 1), 0.0, -1e30)
        c[name] = np.ascontiguousarray(m.reshape(P, 4 * (W + P)).astype(np.float32))
    half = np.arange(0, DH, 2, dtype=np.float32)
    inv_freq = (1.0 / 10000.0 ** (half / DH)).astype(np.float32)
    t = np.arange(T, dtype=np.float32)
    f = (t[:, None] * inv_freq[None, :]).astype(np.float32)
    f = np.concatenate([f, f], 1)
    base = ((half + 0.4 * DH) / (1.4 * DH)).astype(np.float32)
    s = (base[None, :] ** ((t - T // 2) / float(W // 2))[:, None]).astype(np.float32)
    s = np.concatenate([s, s], 1)
    sign = np.where(np.arange(DH) < DH // 2, -1.0, 1.0).astype(np.float32)
    cos, sin = np.cos(f), np.sin(f) * sign
    r = np.stack([cos * s * 8.0, sin * s * 8.0, cos / s, sin / s]).astype(np.float32)
    c["rotation"] = np.ascontiguousarray(r.reshape(4, T // P, P, DH).transpose(2, 0, 1, 3).reshape(P, 4 * (T // P) * DH))
    return c


def kernel(**inputs):
    import numpy as np
    import concourse.bacc as bacc
    from concourse import mybir as mb
    from concourse.bass_utils import run_bass_kernel_spmd

    nc = bacc.Bacc("TRN2", target_bir_lowering=False, num_devices=1)
    arrays = {}

    def give(name, array):
        arrays[name] = np.ascontiguousarray(array)
        return nc.dram_tensor(name, arrays[name].shape, mb.dt.from_np(arrays[name].dtype), kind="ExternalInput").ap()

    def group(prefix):
        given = {}
        for name, array in inputs.items():
            if name.startswith(prefix) and not name.endswith("_x"):
                key, array = name[len(prefix):], np.asarray(array)
                if prefix == "L0_attn_b_" and key.startswith("W"):
                    array = array.T
                elif key in ("A_log", "dt_bias", "bo"):
                    array = array.reshape(1, -1)
                elif array.ndim == 1 or key in ("ln_g", "ln_b", "b1"):
                    array = array.reshape(-1, 1)
                elif array.ndim == 3:
                    array = array.reshape(-1, array.shape[-1])
                given[key] = give(name, array)
        return given

    x = np.asarray(inputs["L0_attn_a_x"])
    shape = x.shape
    x = give("x", x.reshape(-1, shape[-1]))
    a, b, f = (group(p) for p in ("L0_attn_a_", "L0_attn_b_", "L0_ffn_"))
    c = {name: give("const_" + name, array) for name, array in shape_constants().items()}
    out = nc.dram_tensor("out", (shape[0] * shape[1], shape[2]), mb.dt.float32, kind="ExternalOutput").ap()
    hybrid_block(nc, x, a, b, f, c, out)
    r = run_bass_kernel_spmd(nc, [arrays], core_ids=[0])
    return r.results[0]["out"].reshape(shape)
```

```python
from contextlib import ExitStack, contextmanager

import concourse.bass as bass
from concourse import mybir

F32 = mybir.dt.float32
BF16 = mybir.dt.bfloat16
ALU = mybir.AluOpType
ACT = mybir.ActivationFunctionType
AX = mybir.AxisListType

P = 128
NB, T, D = 4, 1024, 128
GT = 4
G = GT * P
NG = T // G
TURNS = NB * NG
PAD = P
ROWS = PAD + T
DEPTH = 2


class Signal:

    def __init__(self, sem, per):
        self.sem = sem
        self.per = per

    def at(self, n, k):
        return self.sem, n * self.per + k


class Phase:

    def __init__(self, nc, name):
        self.nc, self.name, self.stack, self.counters, self.sems = nc, name, ExitStack(), [], []

    def sb(self, name, shape, dt=F32):
        return self.stack.enter_context(self.nc.sbuf_tensor(f"{self.name}_{name}", shape, dt))

    def banks(self):
        return self.stack.enter_context(self.nc.psum_tensor(f"{self.name}_ps", [P, 8, 512], F32))

    def semaphore(self, name):
        self.sems.append(self.stack.enter_context(self.nc.semaphore(f"{self.name}_{name}")))
        return self.sems[-1]

    def counter(self, name, per, owner):
        s = Signal(self.semaphore(name), per)
        self.counters.append((s, owner))
        return s

    def start(self, eng, owner):
        for s, o in self.counters:
            if o == owner:
                eng.sem_inc(s.sem, s.per)

    def close(self):
        for sem in self.sems:
            self.nc.gpsimd.sem_clear(sem)
        self.nc.all_engine_barrier()
        self.stack.close()


def freed(i, slots, total):
    if i >= slots:
        return i - slots + 1
    return max(j for j in range(total) if j % slots == i % slots) + 1 - total


def scratch_row(b, g):
    return b * ROWS + PAD + g * G


def tiles(rows):
    return rows.rearrange("(n p) c -> p n c", p=P)


def local_attention(nc, name, src, dst, l, w, c):
    H, DH, W = 8, 64, 64
    INNER = H * DH
    KEYS = W + P
    PAIRS = H // 2
    NT = T // P
    assert NG == 2 and GT % 2 == 0
    ph = Phase(nc, name)
    sb, signal = ph.sb, ph.counter
    ps = ph.banks()
    wqkv = sb("wqkv", [P, 3 * INNER])
    wo = sb("wo", [P, 4, D])
    ident = sb("ident", [P, P])
    identb = sb("identb", [P, P], BF16)
    mask = sb("mask", [P, 2, 2, KEYS])
    maskb = sb("maskb", [P, 2, 2, KEYS], BF16)
    scales = sb("scales", [P, 4, DH])
    table = sb("table", [P, 4, NT, DH])
    h = sb("h", [P, GT, D])
    x = sb("x", [P, GT, D])
    y = sb("y", [P, GT, D])
    ht = sb("ht", [P, G])
    raw = sb("raw", [P, 2, H, DH])
    sq = sb("sq", [P, 2, H, DH])
    ss = sb("ss", [P, 2, 2 * H])
    minus_half = sb("minus_half", [P, 2 * H])
    rn = sb("rn", [P, 2 * H])
    rot_c = sb("rot_c", [P, 2, H, DH])
    rot_s = sb("rot_s", [P, 2, H, DH])
    rot = sb("rot", [P, 2, H, DH])
    qk = sb("qk", [P, 2 * H, DH])
    qt = sb("qt", [P, 2, PAIRS, P])
    kt = sb("kt", [P, PAIRS, W + G])
    v = sb("v", [P, NT, H, DH])
    nmx = sb("nmx", [P, H])
    rowsum = sb("rowsum", [P, 2, H])
    pr = sb("pr", [P, H, 2 * P])
    pt = sb("pt", [P, H, 2, P])
    rs = sb("rs", [P, H])
    o = sb("o", [P, H, DH])
    ot = sb("ot", [P, 4, P])

    wts_loaded = ph.semaphore("wts_loaded")
    prepared = ph.semaphore("prepared")
    h_loaded = signal("h_loaded", 32, "sp")
    x_loaded = signal("x_loaded", 16, "sp")
    stored = signal("stored", 16, "sp")
    ht_ps = signal("ht_ps", 1, "pe")
    ht_sb = signal("ht_sb", 1, "act")
    qkv_ps = signal("qkv_ps", 2 * GT, "pe")
    raw_sb = signal("raw_sb", GT, "act")
    squared = signal("squared", GT, "act")
    v_sb = signal("v_sb", GT, "act")
    norm2 = signal("norm2", GT, "dve")
    clipped = signal("clipped", GT, "dve")
    rnorm = signal("rnorm", GT, "pool")
    rot_terms = signal("rot_terms", GT, "dve")
    rotated = signal("rotated", GT, "pool")
    qk_unit = signal("qk_unit", GT, "pool")
    qkt_ps = signal("qkt_ps", 2 * GT, "pe")
    qkt_sb = signal("qkt_sb", 2 * GT, "act")
    s_ps = signal("s_ps", PAIRS * GT, "pe")
    negmax = signal("negmax", PAIRS * GT, "dve")
    p_sb = signal("p_sb", PAIRS * GT, "act")
    pt_ps = signal("pt_ps", PAIRS * GT, "pe")
    EVAC = (0, 1, 1, 0)
    NEVAC = (EVAC.count(0), EVAC.count(1))
    pt_sb = [signal("pt_sb_dve", NEVAC[0] * GT, "dve"), signal("pt_sb_act", NEVAC[1] * GT, "act")]
    attended = signal("attended", PAIRS * GT, "pe")
    rsum = signal("rsum", GT, "dve")
    o_sb = signal("o_sb", GT, "dve")
    ot_ps = signal("ot_ps", GT, "pe")
    ot_sb = signal("ot_sb", GT, "act")
    y_ps = signal("y_ps", GT, "pe")
    y_sb = signal("y_sb", GT, "dve")
    halo = signal("halo", 1, "dve")

    WTS = 16 * 12
    OB, QKV, HTB, QKT, SP_ = 0, (1, 2, 3), 1, (1, 2), (4, 5, 6, 7)

    def out_bank(t):
        return 0 if t == GT - 1 else 3

    def head(i, s):
        return 4 * (i // 2) + i % 2 + 2 * s

    def pt_copied(n, t, i):
        return pt_sb[EVAC[i]].at(n, NEVAC[EVAC[i]] * t + 1 + EVAC[:i].count(EVAC[i]))

    def place(g, t):
        return g * GT + t if t < GT else g * -GT + t

    with nc.Block() as block:

        @block.sync
        def _(sp):
            ph.start(sp, "sp")
            sp.dma_start(wqkv[:], w["wqkv"][bass.ds(l * D, D), :]).then_inc(wts_loaded, 16)
            sp.dma_start(wo[:], tiles(w["wo"][bass.ds(l * INNER, INNER), :])).then_inc(wts_loaded, 16)
            sp.dma_start(ident[:], c["ident"]).then_inc(wts_loaded, 16)
            sp.dma_start(mask[:], c["ffn_mask"].rearrange("p (e h k) -> p e h k", e=2, h=2)).then_inc(wts_loaded, 16)
            sp.dma_start(table[:], c["rotation"].rearrange("p (r n i) -> p r n i", r=4, i=DH)).then_inc(wts_loaded, 16)
            sp.dma_start(minus_half[:], c["minus_half"][:, 0:2 * H]).then_inc(wts_loaded, 16)
            for n, scale in enumerate((w["q_scale"], w["k_scale"])):
                sp.dma_start(scales[:, 2 * n, :], scale[bass.ds(l, 1), :].to_broadcast([P, DH])).then_inc(wts_loaded, 16)
                for s in range(2):
                    sp.dma_start(scales[:, 2 * n + 1, 32 * s:32 * s + 32],
                                 scale[bass.ds(l, 1), 32 - 32 * s:64 - 32 * s].to_broadcast([P, 32]))\
                        .then_inc(wts_loaded, 16)

            def load_h(row):
                sp.dma_start(h[:, :, 0:D // 2], tiles(src[bass.ds(row, G), 0:D // 2])).then_inc(h_loaded.sem, 16)
                sp.dma_start(h[:, :, D // 2:D], tiles(src[bass.ds(row - 1, G), D // 2:D])).then_inc(h_loaded.sem, 16)

            load_h(scratch_row(0, 0))
            sp.wait_ge(*ht_ps.at(0, 2))
            load_h(scratch_row(0, 1))
            with sp.Fori(0, NB) as b, sp.Fori(0, NG) as g:
                n = sp.snap(b * NG + g + 1)
                row = sp.snap(scratch_row(b, g))
                ahead = sp.snap((n + 1) % TURNS)
                sp.wait_ge(*ht_ps.at(n, 2))
                load_h(sp.snap(ahead * G + ahead // NG * PAD + PAD))
                sp.wait_ge(*y_sb.at(n, 0))
                sp.dma_start(x[:], tiles(src[bass.ds(row, G), :])).then_inc(x_loaded.sem, 16)
                sp.wait_ge(*y_sb.at(n, GT))
                sp.dma_start(tiles(dst[bass.ds(row, G), :]), y[:]).then_inc(stored.sem, 16)
            sp.wait_ge(*stored.at(TURNS + 1, 0))
            sp.wait_ge(*h_loaded.at(TURNS + 1, 64))

        @block.gpsimd
        def _(pool):
            ph.start(pool, "pool")
            pool.memset(kt[:, :, 0:W], 0.0).then_inc(prepared, 1)
            pool.memset(v[:, NT - 1, :, :], 0.0).then_inc(prepared, 1)
            pool.memset(pr[:, :, 0:P - W], 0.0).then_inc(prepared, 1)
            pool.wait_ge(wts_loaded, WTS)

            def rotate(n, t):
                pool.wait_ge(*rot_terms.at(n, t + 1))
                pool.tensor_tensor(rot[:], rot_c[:], rot_s[:], ALU.add).then_inc(rotated.sem, 1)
                pool.wait_ge(*clipped.at(n, t + 1))
                pool.tensor_tensor(rn[:], ss[:, 1, :], minus_half[:], ALU.pow).then_inc(rnorm.sem, 1)
                pool.wait_ge(*rotated.at(n, t + 1))
                pool.wait_ge(*rnorm.at(n, t + 1))
                pool.wait_ge(*qkt_ps.at(n, 2 * t))
                pool.tensor_tensor(qk[:], rot[:].rearrange("p r h i -> p (r h) i"),
                                   rn[:].unsqueeze(2).to_broadcast([P, 2 * H, DH]), ALU.mult).then_inc(qk_unit.sem, 1)
                pool.wait_ge(*qk_unit.at(n, t + 1))

            for t in range(GT, 2 * GT - 1):
                rotate(0, t)
            with pool.Fori(0, NB) as b, pool.Fori(0, NG) as g:
                n = pool.snap(b * NG + g + 1)
                for t in range(GT):
                    rotate(n, t + GT - 1)

        @block.tensor
        def _(pe):
            ph.start(pe, "pe")
            pe.wait_ge(wts_loaded, WTS)
            pe.wait_ge(prepared, 6 + 3)

            def transpose_h(n):
                pe.wait_ge(*h_loaded.at(n, 64))
                pe.wait_ge(*qkt_sb.at(n, 2 * 1 + 1))
                for t in range(GT):
                    mm = pe.transpose(ps[:, HTB, t * P:(t + 1) * P], h[:, t, :], ident[:])
                mm.then_inc(ht_ps.sem, 1)

            def project(n, t, first=False):
                pe.wait_ge(*ht_sb.at(n, 2))
                pe.wait_ge(*raw_sb.at(n, t))
                pe.wait_ge(*v_sb.at(n, t))
                if not first:
                    pe.wait_ge(*qkt_sb.at(n, 2 * (t - GT + 2)))
                if t > GT and not first:
                    pe.wait_ge(*y_sb.at(n, t - GT))
                for j, bank in enumerate(QKV):
                    mm = pe.matmul(ps[:, bank, :], ht[:, t % GT * P:(t % GT + 1) * P], wqkv[:, j * INNER:(j + 1) * INNER],
                                   start=True, stop=True)
                    if j == 1:
                        mm.then_inc(qkv_ps.sem, 1)
                mm.then_inc(qkv_ps.sem, 1)

            def transpose_qk(n, t, projected):
                pe.wait_ge(*qk_unit.at(n, t + 1))
                pe.wait_ge(*raw_sb.at(n, projected))
                for j in range(2):
                    for i in range(4):
                        mm = pe.transpose(ps[:, QKT[j], i * P:(i + 1) * P],
                                          qk[:, 8 * j + 2 * i:8 * j + 2 * i + 2, :], ident[:])
                    mm.then_inc(qkt_ps.sem, 1)

            def scores(n, t, i, start_of_sequence):
                if i == 0:
                    pe.wait_ge(*qkt_sb.at(n, 2 * t + 2))
                    if t == GT:
                        pe.wait_ge(*halo.at(n, 1))
                pe.wait_ge(*pt_copied(n, t - 1, i))
                out = ps[:, SP_[i], 0:2 * KEYS]
                pe.matmul(out, identb[:], start_of_sequence, start=True, stop=False, skip_group_check=True)
                for s in range(2):
                    half, pair = 64 * (i % 2), head(i, s) // 2
                    mm = pe.matmul(ps[:, SP_[i], s * KEYS:(s + 1) * KEYS], qt[half:half + 64, t % 2, pair, :],
                                   kt[half:half + 64, pair, t % GT * P:t % GT * P + KEYS],
                                   start=False, stop=s == 1, skip_group_check=True)
                mm.then_inc(s_ps.sem, 1)

            first_mask = maskb[:, 0, :, :].rearrange("p h k -> p (h k)")
            other_mask = maskb[:, 1, :, :].rearrange("p h k -> p (h k)")

            transpose_h(0)
            for t in range(GT, 2 * GT):
                project(0, t, first=True)
            transpose_qk(0, GT, 2 * GT)
            scores(0, GT, 0, first_mask)
            scores(0, GT, 1, first_mask)
            with pe.Fori(0, NB) as b, pe.Fori(0, NG) as g:
                n = pe.snap(b * NG + g + 1)
                following = pe.snap(g * -1 + 1)
                slots = [pe.snap(g * -GT + (NT - 1))] + [pe.snap(g * GT + t) for t in range(GT)]

                def mask_of(t):
                    if t % GT:
                        return other_mask
                    return maskb[:, bass.ds(g if t == 0 else following, 1), :, :].rearrange("p e h k -> p (e h k)")

                def transpose_p(t, i):
                    pe.wait_ge(*p_sb.at(n, PAIRS * t + i + 1))
                    for s in range(2):
                        for k in range(2):
                            mm = pe.transpose(ps[:, SP_[i], (2 * s + k) * P:(2 * s + k + 1) * P],
                                              pr[:, 2 * i + s, k * P:(k + 1) * P], ident[:])
                    mm.then_inc(pt_ps.sem, 1)

                def attend(t, i):
                    if i == 0:
                        pe.wait_ge(*v_sb.at(n, t + 1))
                        pe.wait_ge(*o_sb.at(n, t))
                        if t == 0:
                            pe.wait_ge(*y_sb.at(n, 0))
                    pe.wait_ge(*pt_copied(n, t, i))
                    for s in range(2):
                        j = head(i, s)
                        for k in range(2):
                            mm = pe.matmul(ps[:, OB, j * DH:(j + 1) * DH], pt[:, 2 * i + s, k, :],
                                           v[:, bass.ds(slots[t + k], 1), j, :], start=k == 0, stop=k == 1)
                    mm.then_inc(attended.sem, 1)

                def transpose_o(t):
                    pe.wait_ge(*o_sb.at(n, t + 1))
                    pe.wait_ge(*v_sb.at(n, t + GT + 1))
                    for i in range(4):
                        mm = pe.transpose(ps[:, out_bank(t), i * P:(i + 1) * P], o[:, 2 * i:2 * i + 2, :], ident[:])
                    mm.then_inc(ot_ps.sem, 1)

                def project_out(t):
                    pe.wait_ge(*ot_sb.at(n, t + 1))
                    for i in range(4):
                        mm = pe.matmul(ps[:, out_bank(t), 0:D], ot[:, i, :], wo[:, i, :], start=i == 0, stop=i == 3)
                    mm.then_inc(y_ps.sem, 1)

                for t in range(GT):
                    scores(n, t, 2, mask_of(t))
                    transpose_p(t, 0)
                    if t > 0:
                        attend(t - 1, 3)
                    transpose_qk(n, t + 1, GT + t)

                    scores(n, t, 3, mask_of(t))
                    transpose_p(t, 1)
                    attend(t, 0)
                    if t > 0:
                        transpose_o(t - 1)

                    scores(n, t + 1, 0, mask_of(t + 1))
                    transpose_p(t, 2)
                    attend(t, 1)
                    if t > 0:
                        project_out(t - 1)
                    else:
                        transpose_h(n)

                    scores(n, t + 1, 1, mask_of(t + 1))
                    transpose_p(t, 3)
                    attend(t, 2)
                    project(n, t + GT)
                attend(GT - 1, 3)
                transpose_o(GT - 1)
                project_out(GT - 1)
            pe.wait_ge(*y_sb.at(TURNS + 1, 0))
            pe.sem_inc(qkt_ps.sem, 2 * (GT - 3))

        @block.scalar
        def _(act):
            ph.start(act, "act")

            def copy_ht(n):
                act.wait_ge(*ht_ps.at(n, 2))
                act.wait_ge(*qkv_ps.at(n, 2 * GT))
                act.activation(ht[:], ps[:, HTB, :], ACT.Copy).then_inc(ht_sb.sem, 1)

            def copy_qkv(n, t, slot, in_loop=True):
                act.wait_ge(*qkv_ps.at(n, 2 * t + 1))
                act.wait_ge(*rot_terms.at(n, t))
                act.wait_ge(*squared.at(n, t))
                act.activation(raw[:], ps[:, QKV[0]:QKV[1] + 1, :].rearrange("p r (h i) -> p r h i", i=DH), ACT.Copy)\
                    .then_inc(raw_sb.sem, 1)
                act.wait_ge(*qkv_ps.at(n, 2 * t + 2))
                if in_loop:
                    act.wait_ge(*attended.at(n, PAIRS * (t - GT - 2)))
                act.activation(v[:, slot, :, :], ps[:, QKV[2], :].rearrange("p (h i) -> p h i", i=DH), ACT.Copy)\
                    .then_inc(v_sb.sem, 1)

            def square(n, t):
                act.wait_ge(*raw_sb.at(n, t + 1))
                act.wait_ge(*norm2.at(n, t))
                act.activation(sq[:], raw[:], ACT.Square).then_inc(squared.sem, 1)

            def copy_qkt(n, t):
                act.wait_ge(*qkt_ps.at(n, 2 * t + 1))
                act.wait_ge(*s_ps.at(n, PAIRS * (t - 1)))
                act.activation(qt[:, t % 2], ps[:, QKT[0], :].rearrange("p (i k) -> p i k", k=P), ACT.Copy)\
                    .then_inc(qkt_sb.sem, 1)
                act.wait_ge(*qkt_ps.at(n, 2 * t + 2))
                if t % GT == GT - 1:
                    act.wait_ge(*halo.at(n, 0))
                act.activation(kt[:, :, W + t % GT * P:W + (t % GT + 1) * P],
                               ps[:, QKT[1], :].rearrange("p (i k) -> p i k", k=P), ACT.Copy).then_inc(qkt_sb.sem, 1)

            def softmax(n, t, i):
                act.wait_ge(*negmax.at(n, PAIRS * t + i + 1))
                act.wait_ge(*pt_ps.at(n, PAIRS * (t - 1) + i + 1))
                if i == 0:
                    act.wait_ge(*rsum.at(n, t - 1))
                for s in range(2):
                    e = act.activation(pr[:, 2 * i + s, P - W:2 * P], ps[:, SP_[i], s * KEYS:(s + 1) * KEYS], ACT.Exp,
                                       bias=nmx[:, 2 * i + s:2 * i + s + 1],
                                       accum_out=rowsum[:, t % 2, head(i, s):head(i, s) + 1])
                e.then_inc(p_sb.sem, 1)

            copy_ht(0)
            for t in range(GT, 2 * GT):
                if t > GT:
                    square(0, t - 1)
                copy_qkv(0, t, t - GT, in_loop=False)
            copy_qkt(0, GT)
            softmax(0, GT, 0)
            with act.Fori(0, NB) as b, act.Fori(0, NG) as g:
                n = act.snap(b * NG + g + 1)
                slots = [act.snap(place(g, GT + t)) for t in range(GT)]

                def copy_pt(t, i):
                    act.wait_ge(*pt_ps.at(n, PAIRS * t + i + 1))
                    act.wait_ge(*attended.at(n, PAIRS * (t - 1) + i + 1))
                    act.activation(pt[:, 2 * i:2 * i + 2, :, :],
                                   ps[:, SP_[i], :].rearrange("p (s k q) -> p s k q", s=2, k=2), ACT.Copy)\
                        .then_inc(pt_sb[1].sem, 1)

                def copy_ot(t):
                    act.wait_ge(*ot_ps.at(n, t + 1))
                    act.wait_ge(*y_ps.at(n, t))
                    act.activation(ot[:], ps[:, out_bank(t), :].rearrange("p (i k) -> p i k", k=P), ACT.Copy)\
                        .then_inc(ot_sb.sem, 1)

                for t in range(GT):
                    softmax(n, t, 1)
                    copy_qkt(n, t + 1)

                    softmax(n, t, 2)
                    copy_pt(t, 1)
                    if t > 0:
                        copy_ot(t - 1)

                    softmax(n, t, 3)
                    copy_pt(t, 2)
                    square(n, t + GT - 1)
                    if t == 0:
                        copy_ht(n)

                    softmax(n, t + 1, 0)
                    copy_qkv(n, t + GT, bass.ds(slots[t], 1))
                copy_ot(GT - 1)

        @block.vector
        def _(dve):
            ph.start(dve, "dve")
            dve.wait_ge(wts_loaded, WTS)
            dve.tensor_copy(identb[:], ident[:]).then_inc(prepared, 1)
            dve.tensor_copy(maskb[:], mask[:]).then_inc(prepared, 1)
            for r in range(4):
                dve.tensor_tensor(table[:, r], table[:, r], scales[:, r, :].unsqueeze(1).to_broadcast([P, NT, DH]),
                                  ALU.mult).then_inc(prepared, 1)
            dve.wait_ge(prepared, 6 + 3)

            def cosines(n, t, entry):
                dve.wait_ge(*raw_sb.at(n, t + 1))
                dve.wait_ge(*rotated.at(n, t))
                for r in range(2):
                    cos = table[:, 2 * r, entry, :].to_broadcast([P, H, DH])
                    dve.tensor_tensor(rot_c[:, r], raw[:, r], cos, ALU.mult)

            def sines(n, t, entry):
                for r in range(2):
                    swapped = raw[:, r].rearrange("p h (s i) -> p h s i", s=2)[:, :, ::-1, :]
                    sin = table[:, 2 * r + 1, entry, :].to_broadcast([P, H, DH]).rearrange("p h (s i) -> p h s i", s=2)
                    terms = dve.tensor_tensor(rot_s[:, r].rearrange("p h (s i) -> p h s i", s=2), swapped, sin, ALU.mult)
                terms.then_inc(rot_terms.sem, 1)

            def squared_norms(n, t):
                dve.wait_ge(*squared.at(n, t + 1))
                dve.wait_ge(*clipped.at(n, t))
                dve.tensor_reduce(ss[:, 0, :], sq[:].rearrange("p r h i -> p (r h) i"), AX.X, ALU.add).then_inc(norm2.sem, 1)
                dve.wait_ge(*norm2.at(n, t + 1))
                dve.wait_ge(*rnorm.at(n, t))
                dve.tensor_scalar(ss[:, 1, :], ss[:, 0, :], 1e-24, None, ALU.max).then_inc(clipped.sem, 1)

            def maximum(n, t, i):
                dve.wait_ge(*s_ps.at(n, PAIRS * t + i + 1))
                dve.wait_ge(*p_sb.at(n, PAIRS * (t - 1) + i + 1))
                dve.tensor_reduce(nmx[:, 2 * i:2 * i + 2], ps[:, SP_[i], 0:2 * KEYS].rearrange("p (s k) -> p s k", s=2),
                                  AX.X, ALU.max, negate=True).then_inc(negmax.sem, 1)

            for t in range(GT, 2 * GT - 1):
                cosines(0, t, slice(t - GT, t - GT + 1))
                sines(0, t, slice(t - GT, t - GT + 1))
                squared_norms(0, t)
            maximum(0, GT, 0)
            maximum(0, GT, 1)
            with dve.Fori(0, NB) as b, dve.Fori(0, NG) as g:
                n = dve.snap(b * NG + g + 1)
                entries = [dve.snap(place(g, GT - 1 + t)) for t in range(GT)]

                def copy_pt(t, i):
                    dve.wait_ge(*pt_ps.at(n, PAIRS * t + i + 1))
                    dve.wait_ge(*attended.at(n, PAIRS * (t - 1) + i + 1))
                    dve.tensor_copy(pt[:, 2 * i:2 * i + 2, :, :],
                                    ps[:, SP_[i], :].rearrange("p (s k q) -> p s k q", s=2, k=2)).then_inc(pt_sb[0].sem, 1)

                def normalize(t):
                    dve.wait_ge(*p_sb.at(n, PAIRS * t + PAIRS))
                    dve.wait_ge(*o_sb.at(n, t))
                    dve.reciprocal(rs[:], rowsum[:, t % 2, :]).then_inc(rsum.sem, 1)
                    dve.wait_ge(*rsum.at(n, t + 1))
                    dve.wait_ge(*attended.at(n, PAIRS * (t + 1)))
                    dve.wait_ge(*ot_ps.at(n, t))
                    dve.tensor_tensor(o[:], ps[:, OB, :].rearrange("p (h i) -> p h i", i=DH),
                                      rs[:].unsqueeze(2).to_broadcast([P, H, DH]), ALU.mult).then_inc(o_sb.sem, 1)

                def add(t):
                    dve.wait_ge(*y_ps.at(n, t + 1))
                    if t == 0:
                        dve.wait_ge(*x_loaded.at(n, 16))
                        dve.wait_ge(*stored.at(n, 0))
                    dve.tensor_tensor(y[:, t, :], ps[:, out_bank(t), 0:D], x[:, t, :], ALU.add).then_inc(y_sb.sem, 1)

                for t in range(GT):
                    entry = bass.ds(entries[t], 1)
                    maximum(n, t, 2)
                    copy_pt(t, 0)
                    if t > 0:
                        normalize(t - 1)
                    cosines(n, t + GT - 1, entry)

                    maximum(n, t, 3)
                    sines(n, t + GT - 1, entry)

                    maximum(n, t + 1, 0)
                    if t > 0:
                        add(t - 1)
                    if t == GT - 2:
                        dve.wait_ge(*qkt_sb.at(n, 2 * GT))
                        dve.wait_ge(*s_ps.at(n, PAIRS))
                        dve.tensor_copy(kt[:, :, 0:W], kt[:, :, G:G + W]).then_inc(halo.sem, 1)

                    maximum(n, t + 1, 1)
                    copy_pt(t, 3)
                    if t < GT - 1:
                        squared_norms(n, t + GT - 1)
                normalize(GT - 1)
                squared_norms(n, 2 * GT - 2)
                add(GT - 1)
    ph.close()


def window_attention(nc, name, src, x_in, dst, w, c):
    H, DH, W = 16, 8, 64
    KEYS = W + P
    PAIRS = H // 2
    RING = 4
    N = PAIRS * GT
    SCALE = float(DH) ** -0.5
    ph = Phase(nc, name)
    sb, signal = ph.sb, ph.counter
    ps = ph.banks()
    wq, wk, wv, wo = (sb(n, [P, D]) for n in ("wq", "wk", "wv", "wo"))
    bq, bk, bv, bqs = (sb(n, [P, 1]) for n in ("bq", "bk", "bv", "bqs"))
    bo = sb("bo", [P, D])
    ident = sb("ident", [P, P])
    identb = sb("identb", [P, P], BF16)
    mask = sb("mask", [P, 2, 2, KEYS])
    maskb = sb("maskb", [P, 2, 2, KEYS], BF16)
    own = sb("own", [P, 4])
    bk_own = sb("bk_own", [P, 4])
    h = sb("h", [P, GT, D])
    x = sb("x", [P, GT, D])
    xb = sb("xb", [P, GT, D])
    y = sb("y", [P, GT, D])
    ht = sb("ht", [P, G])
    qt = sb("qt", [P, G])
    kt = sb("kt", [P, 4, W + G])
    v = sb("v", [P, 1 + GT, H, DH + 1])
    nmx = sb("nmx", [P, H])
    pr = sb("pr", [P, H, 2 * P])
    pt = sb("pt", [P, H, 2, P])
    rs = sb("rs", [P, H])
    o = sb("o", [P, H, DH])
    ot = sb("ot", [P, P])

    wts_loaded = ph.semaphore("wts_loaded")
    prepared = ph.semaphore("prepared")
    h_loaded = signal("h_loaded", 16, "sp")
    x_loaded = signal("x_loaded", 16, "sp")
    stored = signal("stored", 16, "sp")
    xb_done = signal("xb_done", 1, "pool")
    ht_ps = signal("ht_ps", 1, "pe")
    ht_sb = signal("ht_sb", 1, "act")
    qkv_ps = signal("qkv_ps", 3, "pe")
    qkv_sb = signal("qkv_sb", 6, "act")
    s_ps = signal("s_ps", N, "pe")
    negmax = signal("negmax", N, "dve")
    p_sb = signal("p_sb", N, "act")
    pt_ps = signal("pt_ps", N, "pe")
    pt_sb = [signal("pt_sb_dve", N // 2, "dve"), signal("pt_sb_act", N // 2, "act")]
    attended = signal("attended", N, "pe")
    rsum = signal("rsum", GT, "dve")
    o_sb = signal("o_sb", GT, "dve")
    ot_ps = signal("ot_ps", GT, "pe")
    ot_sb = signal("ot_sb", GT, "act")
    y_ps = signal("y_ps", GT, "pe")
    y_sb = signal("y_sb", GT, "dve")
    halo = signal("halo", 2, "dve")

    loads = [(wq[:], w["Wq"]), (wk[:], w["Wk"]), (wv[:], w["Wv"]), (wo[:], w["Wo"]), (bq[:], w["bq"]), (bk[:], w["bk"]),
             (bv[:], w["bv"]), (bo[:], w["bo"].to_broadcast([P, D])), (ident[:], c["ident"]), (own[:], c["own_head"]),
             (mask[:], c["attn_mask"].rearrange("p (e h k) -> p e h k", e=2, h=2))]
    LOADED, PREPARED = 16 * len(loads), 3 + 4

    HTB, QB, KB, VB = 2, 3, 2, 0
    O_AT, OT_AT, Y_AT = 0, 256, 384

    def score_bank(j):
        return 4 + j % RING

    def pt_copied(n, j):
        return pt_sb[j % 2].at(n, j // 2 + 1)

    with nc.Block() as block:

        @block.sync
        def _(sp):
            ph.start(sp, "sp")
            for out, in_ in loads:
                sp.dma_start(out, in_).then_inc(wts_loaded, 16)
            sp.dma_start(h[:], tiles(src[bass.ds(scratch_row(0, 0), G), :])).then_inc(h_loaded.sem, 16)
            with sp.Fori(0, NB) as b, sp.Fori(0, NG) as g:
                n = sp.snap(b * NG + g + 1)
                row = sp.snap(scratch_row(b, g))
                ahead = sp.snap(n % TURNS)
                sp.wait_ge(*ht_ps.at(n, 1))
                sp.dma_start(h[:], tiles(src[bass.ds(sp.snap(ahead * G + ahead // NG * PAD + PAD), G), :]))\
                    .then_inc(h_loaded.sem, 16)
                sp.wait_ge(*xb_done.at(n, 0))
                sp.dma_start(x[:], tiles(x_in[bass.ds(row, G), :])).then_inc(x_loaded.sem, 16)
                sp.wait_ge(*y_sb.at(n, GT))
                sp.dma_start(tiles(dst[bass.ds(row, G), :]), y[:]).then_inc(stored.sem, 16)
            sp.wait_ge(*stored.at(TURNS + 1, 0))
            sp.wait_ge(*h_loaded.at(TURNS + 1, 16))

        @block.gpsimd
        def _(pool):
            ph.start(pool, "pool")
            pool.memset(kt[:, :, 0:W], 0.0).then_inc(prepared, 1)
            pool.memset(v[:, 0, :, :], 0.0).then_inc(prepared, 1)
            pool.memset(v[:, 1:, :, DH:], 1.0).then_inc(prepared, 1)
            pool.memset(pr[:, :, 0:P - W], 0.0).then_inc(prepared, 1)
            pool.wait_ge(wts_loaded, LOADED)
            with pool.Fori(0, NB) as b, pool.Fori(0, NG) as g:
                n = pool.snap(b * NG + g + 1)
                pool.wait_ge(*x_loaded.at(n, 16))
                pool.wait_ge(*y_sb.at(n, 0))
                pool.tensor_tensor(xb[:], x[:], bo[:].unsqueeze(1).to_broadcast([P, GT, D]), ALU.add).then_inc(xb_done.sem, 1)

        @block.tensor
        def _(pe):
            ph.start(pe, "pe")
            pe.wait_ge(wts_loaded, LOADED)
            pe.wait_ge(prepared, PREPARED)

            def transpose_h(n):
                pe.wait_ge(*h_loaded.at(n, 32))
                pe.wait_ge(*qkv_sb.at(n, 5))
                for t in range(GT):
                    mm = pe.transpose(ps[:, HTB, t * P:(t + 1) * P], h[:, t, :], ident[:])
                mm.then_inc(ht_ps.sem, 1)

            def project_qk(n):
                pe.wait_ge(*ht_sb.at(n, 2))
                pe.wait_ge(*qkv_sb.at(n, 1))
                pe.matmul(ps[:, QB, :], wq[:], ht[:], start=True, stop=True).then_inc(qkv_ps.sem, 1)
                pe.matmul(ps[:, KB, :], wk[:], ht[:], start=True, stop=True).then_inc(qkv_ps.sem, 1)

            def project_v(n):
                pe.wait_ge(*y_sb.at(n, GT - 1))
                for t in range(GT):
                    mm = pe.matmul(ps[:, VB, t * P:(t + 1) * P], ht[:, t * P:(t + 1) * P], wv[:], start=True, stop=True)
                mm.then_inc(qkv_ps.sem, 1)

            def scores(n, j, m):
                t, i = j // PAIRS % GT, j % PAIRS
                if j >= N:
                    pe.wait_ge(*qkv_sb.at(n, 6 + (3 if j == N else 5)))
                    pe.wait_ge(*halo.at(n, 1))
                pe.wait_ge(*pt_copied(n, j - RING))
                bank, at = score_bank(j), 32 * (i // 2)
                pe.matmul(ps[:, bank, 0:2 * KEYS], identb[:], m, start=True, stop=False, skip_group_check=True)
                for s in range(2):
                    mm = pe.matmul(ps[:, bank, s * KEYS:(s + 1) * KEYS], qt[at:at + 32, t * P:(t + 1) * P],
                                   kt[at:at + 32, (2 * i + s) % 4, t * P:t * P + KEYS],
                                   start=False, stop=s == 1, skip_group_check=True, tile_position=(at, 0))
                mm.then_inc(s_ps.sem, 1)

            first_mask = maskb[:, 0, :, :].rearrange("p h k -> p (h k)")
            other_mask = maskb[:, 1, :, :].rearrange("p h k -> p (h k)")

            transpose_h(0)
            project_qk(0)
            project_v(0)
            scores(0, N, first_mask)
            scores(0, N + 1, first_mask)
            with pe.Fori(0, NB) as b, pe.Fori(0, NG) as g:
                n = pe.snap(b * NG + g + 1)
                following = pe.snap(g * -1 + 1)

                def mask_of(j):
                    if j // PAIRS % GT:
                        return other_mask
                    return maskb[:, bass.ds(g if j < N else following, 1), :, :].rearrange("p e h k -> p (e h k)")

                def transpose_p(j):
                    pe.wait_ge(*p_sb.at(n, j + 1))
                    for s in range(2):
                        for k in range(2):
                            mm = pe.transpose(ps[:, score_bank(j), (2 * s + k) * P:(2 * s + k + 1) * P],
                                              pr[:, 2 * (j % PAIRS) + s, k * P:(k + 1) * P], ident[:])
                    mm.then_inc(pt_ps.sem, 1)

                def attend(j):
                    t = j // PAIRS
                    if j % PAIRS == 0:
                        pe.wait_ge(*y_sb.at(n, t - 1))
                        if t == 0:
                            pe.wait_ge(*qkv_sb.at(n, 6))
                    pe.wait_ge(*pt_copied(n, j))
                    for s in range(2):
                        head = 2 * (j % PAIRS) + s
                        for k in range(2):
                            mm = pe.matmul(ps[:, t % 2, O_AT + head * (DH + 1):O_AT + (head + 1) * (DH + 1)],
                                           pt[:, head, k, :], v[:, t + k, head, :], start=k == 0, stop=k == 1)
                    mm.then_inc(attended.sem, 1)

                def transpose_o(t):
                    pe.wait_ge(*o_sb.at(n, t + 1))
                    pe.transpose(ps[:, t % 2, OT_AT:OT_AT + P], o[:].rearrange("p h i -> p (h i)"), ident[:])\
                        .then_inc(ot_ps.sem, 1)

                def project_out(t):
                    pe.wait_ge(*ot_sb.at(n, t + 1))
                    pe.matmul(ps[:, t % 2, Y_AT:Y_AT + D], ot[:], wo[:], start=True, stop=True).then_inc(y_ps.sem, 1)

                for j in range(N):
                    t, i = j // PAIRS, j % PAIRS
                    if j + 2 < N:
                        scores(n, j + 2, mask_of(j + 2))
                    transpose_p(j)
                    if j > 0:
                        attend(j - 1)
                    if t > 0 and i == 2:
                        transpose_o(t - 1)
                    if t > 0 and i == 4:
                        project_out(t - 1)
                    if t == GT - 1 and i == 1:
                        transpose_h(n)
                    if t == GT - 1 and i == 5:
                        project_qk(n)
                    if t == GT - 1 and i == 7:
                        project_v(n)
                attend(N - 1)
                transpose_o(GT - 1)
                scores(n, N, mask_of(N))
                project_out(GT - 1)
                scores(n, N + 1, mask_of(N + 1))

        @block.scalar
        def _(act):
            ph.start(act, "act")
            act.wait_ge(wts_loaded, LOADED)
            act.wait_ge(prepared, PREPARED)

            def copy_ht(n):
                act.wait_ge(*ht_ps.at(n, 2))
                act.wait_ge(*qkv_ps.at(n, 3))
                act.activation(ht[:], ps[:, HTB, :], ACT.Copy).then_inc(ht_sb.sem, 1)

            def copy_q(n):
                act.wait_ge(*qkv_ps.at(n, 3 + 1))
                act.wait_ge(*s_ps.at(n, N))
                act.activation(qt[:], ps[:, QB, :], ACT.Identity, scale=SCALE, bias=bqs[:]).then_inc(qkv_sb.sem, 1)

            def copy_k(n, parts):
                act.wait_ge(*qkv_ps.at(n, 3 + 2))
                act.wait_ge(*halo.at(n, 1))
                for m in parts:
                    act.activation(kt[:, m, W:W + G], ps[:, KB, :], ACT.Identity, scale=own[:, m:m + 1],
                                   bias=bk_own[:, m:m + 1]).then_inc(qkv_sb.sem, 1)

            def copy_v(n):
                act.wait_ge(*qkv_ps.at(n, 3 + 3))
                act.wait_ge(*attended.at(n, N))
                act.wait_ge(*halo.at(n, 2))
                act.activation(v[:, 1:, :, 0:DH], ps[:, VB, :].rearrange("p (t h i) -> p t h i", t=GT, i=DH), ACT.Copy)\
                    .then_inc(qkv_sb.sem, 1)

            def exponentials(n, j):
                act.wait_ge(*negmax.at(n, j + 1))
                act.wait_ge(*pt_ps.at(n, j + 1 - PAIRS))
                i = j % PAIRS
                for s in range(2):
                    e = act.activation(pr[:, 2 * i + s, P - W:2 * P], ps[:, score_bank(j), s * KEYS:(s + 1) * KEYS],
                                       ACT.Exp, bias=nmx[:, 2 * i + s:2 * i + s + 1])
                e.then_inc(p_sb.sem, 1)

            copy_ht(0)
            copy_q(0)
            copy_k(0, range(4))
            exponentials(0, N)
            copy_v(0)
            with act.Fori(0, NB) as b, act.Fori(0, NG) as g:
                n = act.snap(b * NG + g + 1)

                def copy_pt(j):
                    act.wait_ge(*pt_ps.at(n, j + 1))
                    act.wait_ge(*attended.at(n, j + 1 - PAIRS))
                    i = j % PAIRS
                    act.activation(pt[:, 2 * i:2 * i + 2, :, :],
                                   ps[:, score_bank(j), :].rearrange("p (s k q) -> p s k q", s=2, k=2), ACT.Copy)\
                        .then_inc(pt_sb[1].sem, 1)

                def copy_ot(t):
                    act.wait_ge(*ot_ps.at(n, t + 1))
                    act.wait_ge(*y_ps.at(n, t))
                    act.activation(ot[:], ps[:, t % 2, OT_AT:OT_AT + P], ACT.Identity, bias=bv[:]).then_inc(ot_sb.sem, 1)

                for j in range(N):
                    t, i = j // PAIRS, j % PAIRS
                    if j + 1 < N:
                        exponentials(n, j + 1)
                    if j % 2 == 1:
                        copy_pt(j)
                    if t > 0 and i == 3:
                        copy_ot(t - 1)
                    if t == GT - 1 and i == 2:
                        copy_ht(n)
                copy_q(n)
                copy_k(n, (0, 1))
                copy_ot(GT - 1)
                copy_k(n, (2, 3))
                exponentials(n, N)
                copy_v(n)

        @block.vector
        def _(dve):
            ph.start(dve, "dve")
            dve.wait_ge(wts_loaded, LOADED)
            dve.tensor_copy(identb[:], ident[:])
            dve.tensor_copy(maskb[:], mask[:])
            dve.tensor_scalar(bqs[:], bq[:], SCALE, None, ALU.mult)
            dve.tensor_scalar(bk_own[:], own[:], bk[:], None, ALU.mult).then_inc(prepared, 3)

            def maximum(n, j):
                dve.wait_ge(*s_ps.at(n, j + 1))
                dve.wait_ge(*p_sb.at(n, j + 1 - PAIRS))
                i = j % PAIRS
                dve.tensor_reduce(nmx[:, 2 * i:2 * i + 2], ps[:, score_bank(j), 0:2 * KEYS].rearrange("p (s k) -> p s k", s=2),
                                  AX.X, ALU.max, negate=True).then_inc(negmax.sem, 1)

            maximum(0, N)
            maximum(0, N + 1)
            with dve.Fori(0, NB) as b, dve.Fori(0, NG) as g:
                n = dve.snap(b * NG + g + 1)

                def copy_pt(j):
                    dve.wait_ge(*pt_ps.at(n, j + 1))
                    dve.wait_ge(*attended.at(n, j + 1 - PAIRS))
                    i = j % PAIRS
                    dve.tensor_copy(pt[:, 2 * i:2 * i + 2, :, :],
                                    ps[:, score_bank(j), :].rearrange("p (s k q) -> p s k q", s=2, k=2)).then_inc(pt_sb[0].sem, 1)

                def normalize(t):
                    dve.wait_ge(*attended.at(n, PAIRS * (t + 1)))
                    dve.wait_ge(*o_sb.at(n, t))
                    oh = ps[:, t % 2, O_AT:O_AT + H * (DH + 1)].rearrange("p (h i) -> p h i", i=DH + 1)
                    dve.reciprocal(rs[:], oh[:, :, DH]).then_inc(rsum.sem, 1)
                    dve.wait_ge(*rsum.at(n, t + 1))
                    dve.wait_ge(*ot_ps.at(n, t))
                    dve.tensor_tensor(o[:], oh[:, :, 0:DH], rs[:].unsqueeze(2).to_broadcast([P, H, DH]), ALU.mult)\
                        .then_inc(o_sb.sem, 1)

                def add(t):
                    dve.wait_ge(*y_ps.at(n, t + 1))
                    if t == 0:
                        dve.wait_ge(*xb_done.at(n, 1))
                        dve.wait_ge(*stored.at(n, 0))
                    dve.tensor_tensor(y[:, t, :], ps[:, t % 2, Y_AT:Y_AT + D], xb[:, t, :], ALU.add).then_inc(y_sb.sem, 1)

                for j in range(N):
                    t, i = j // PAIRS, j % PAIRS
                    if j + 2 < N:
                        maximum(n, j + 2)
                    if j % 2 == 0:
                        copy_pt(j)
                    if t > 0 and i == 0:
                        normalize(t - 1)
                    if t > 0 and i == 5:
                        add(t - 1)
                    if t == 1 and i == 6:
                        dve.tensor_copy(kt[:, :, 0:W], kt[:, :, G:G + W]).then_inc(halo.sem, 1)
                    if t == 2 and i == 6:
                        dve.tensor_copy(v[:, 0, :, :], v[:, GT, :, :]).then_inc(halo.sem, 1)
                normalize(GT - 1)
                maximum(n, N)
                maximum(n, N + 1)
                add(GT - 1)
    ph.close()


def delta_attention(nc, name, x_in, dst, w, c):
    H, DK, DV = 8, 96, 192
    HG = 4
    VD = H * DV
    LEVELS = 7
    NQK, NV = 2 * H, VD // P
    NG3 = GT * 3 // 2
    SLOTS = 3
    USES = NQK + NV + NG3
    ph = Phase(nc, name)
    sb, signal = ph.sb, ph.counter
    ps = ph.banks()
    wq = sb("wq", [P, H * DK])
    wk = sb("wk", [P, H * DK])
    wv = sb("wv", [P, VD])
    wg = sb("wg", [P, VD])
    wo = sb("wo", [P, NV, D])
    onorm = sb("onorm", [P, NV])
    wba = sb("wba", [P, 2 * H])
    conv_qk = sb("conv_qk", [DK, H, 2, 4])
    conv_v = sb("conv_v", [P, NV, 4])
    norm1 = sb("norm1", [P, 1])
    decay_rate = sb("decay_rate", [P, H])
    dt_bias = sb("dt_bias", [P, H])
    ident = sb("ident", [P, P])
    ident4 = sb("ident4", [P, HG, P])
    sums = sb("sums", [P, 3, P])
    not_first = sb("not_first", [P, 1])
    blocks = sb("blocks", [P, LEVELS, P // 2])
    minus_half = sb("minus_half", [P, 4 * H])
    x = sb("x", [P, GT, D])
    y = sb("y", [P, GT, D])
    hn = sb("hn", [P, GT, D])
    out = sb("out", [P, GT, D])
    stats = sb("stats", [P, GT, 6])
    mv = sb("mv", [P, GT, 2])
    ms = sb("ms", [P, 2, GT])
    rstd = sb("rstd", [P, 2, GT])
    ht = sb("ht", [P, 3 + G])
    raw = sb("raw", [P, SLOTS, 3 + G])
    conv = sb("conv", [P, SLOTS, G])
    qk = sb("qk", [DK, H, 2, G])
    vt = sb("vt", [P, NV, G])
    gate = sb("gate", [P, GT, VD])
    za = sb("za", [P, 12, GT * H])
    ex = sb("ex", [P, 6, GT, H])
    sq = sb("sq", [DK, H, 2, P])
    cf = sb("cf", [P, 2, 14, 2 * H])
    gd = sb("gd", [P, H, P])
    al = sb("al", [P, H, 2, P])
    tm = sb("tm", [P, H, P])
    tt = sb("tt", [P, H, P])
    am = sb("am", [P, H, P // 2])
    kd = sb("kd", [P, H, DK])
    vr = sb("vr", [P, H, DV])
    delta = sb("delta", [P, H, DV])
    o = sb("o", [P, H, DV])
    ot = sb("ot", [P, NV, P])
    state = sb("state", [DK, H, DV])

    wts_loaded = ph.semaphore("wts_loaded")
    prepared = ph.semaphore("prepared")
    x_loaded = signal("x_loaded", 16, "sp")
    stored = signal("stored", 16, "sp")
    stats_done = signal("stats_done", GT, "dve")
    seen = signal("seen", 1, "dve").sem
    moments = signal("moments", GT, "dve")
    root1 = signal("root1", 1, "dve")
    root1_done = signal("root1_done", 1, "pool")
    root2 = signal("root2", 4, "dve")
    root2_done = signal("root2_done", 1, "pool")
    y_sb = signal("y_sb", 1, "dve")
    hn_sb = signal("hn_sb", 1, "dve")
    ht_ps = signal("ht_ps", 1, "pe")
    ht_sb = signal("ht_sb", 1, "act")
    ht_halo = signal("ht_halo", 1, "dve")
    ba_ps = signal("ba_ps", 1, "pe")
    za_step = signal("za_step", 22, "dve")
    za_exp = signal("za_exp", 2, "act")
    cum_ps = signal("cum_ps", 1, "pe")
    ex_sb = signal("ex_sb", 2, "act")
    decay_cut = signal("decay_cut", 1, "dve")
    use_ps = signal("use_ps", USES, "pe")
    use_sb = signal("use_sb", USES, "act")
    tap = signal("tap", 3 * (NQK + NV), "dve")
    silu = signal("silu", NQK + NV, "act")
    zeroed = signal("zeroed", 2, "dve")
    sq_sb = signal("sq_sb", GT, "pool")
    n2_ps = signal("n2_ps", GT, "pe")
    n2_sb = signal("n2_sb", GT, "dve")
    rn_sb = signal("rn_sb", GT, "pool")
    coef = signal("coef", 4 * GT, "dve")

    def both(n, per, owner):
        return [signal(f"{n}{i}", per, owner) for i in range(2)]
    dec_ps = both("dec_ps", GT, "pe")
    gd_sb = both("gd_sb", GT, "dve")
    kq_ps = both("kq_ps", GT, "pe")
    al_sb = both("al_sb", GT, "dve")
    kt_ps = both("kt_ps", GT, "pe")
    kd_sb = both("kd_sb", GT, "act")
    vt_ps = both("vt_ps", GT, "pe")
    vb_sb = both("vb_sb", GT, "act")
    tm_one = both("tm_one", GT, "act")
    lx_ps = both("lx_ps", LEVELS * GT, "pe")
    am_sb = both("am_sb", LEVELS * GT, "dve")
    ty_ps = both("ty_ps", (LEVELS - 1) * GT, "pe")
    tm_sb = both("tm_sb", LEVELS * GT, "dve")
    tt_ps = both("tt_ps", LEVELS * GT, "pe")
    tt_sb = both("tt_sb", LEVELS * GT, "act")
    ks_ps = both("ks_ps", GT, "pe")
    r_sb = both("r_sb", GT, "dve")
    delta_ps = both("delta_ps", GT, "pe")
    delta_sb = both("delta_sb", GT, "act")
    qs_ps = both("qs_ps", GT, "pe")
    qs_sb = both("qs_sb", GT, "act")
    ad_ps = both("ad_ps", GT, "pe")
    o_sb = both("o_sb", GT, "dve")
    up_ps = both("up_ps", GT, "pe")
    state_sb = both("state_sb", GT, "dve")
    osq = signal("osq", GT, "act")
    o_gated = signal("o_gated", GT, "pool")
    om = signal("om", 4 * GT, "dve")
    orn = signal("orn", GT, "pool")
    og_sb = signal("og_sb", GT, "pool")
    ot_ps = signal("ot_ps", 3 * GT, "pe")
    ot_sb = signal("ot_sb", 3 * GT, "act")
    y_ps = signal("y_ps", GT, "pe")
    out_sb = signal("out_sb", GT, "dve")

    loads = [(wq[:], w["Wq"]), (wk[:], w["Wk"]), (wv[:], w["Wv"]), (wg[:], w["Wg"]), (wo[:], tiles(w["Wo"])),
             (wba[:, 0:H], w["Wb"]), (wba[:, H:2 * H], w["Wa"]),
             (conv_qk[:, :, 0, :], w["conv_q_w"].rearrange("(h d) i -> d h i", d=DK)),
             (conv_qk[:, :, 1, :], w["conv_k_w"].rearrange("(h d) i -> d h i", d=DK)),
             (conv_v[:], tiles(w["conv_v_w"])), (norm1[:], w["norm1_w"]),
             (decay_rate[:], w["A_log"].to_broadcast([P, H])), (dt_bias[:], w["dt_bias"].to_broadcast([P, H])),
             (ident[:], c["ident"]), (sums[:], c["sums"].rearrange("p (k i) -> p k i", k=3)),
             (not_first[:], c["not_first"]), (blocks[:], c["blocks"].rearrange("p (m i) -> p m i", m=LEVELS)),
             (minus_half[:], c["minus_half"][:, 0:4 * H])]
    ow = w["onorm_w"]
    for m, (p0, p1, a) in ((0, (0, P, 0)), (1, (0, DV - P, P)), (1, (DV - P, P, 0)), (2, (0, P, DV - P))):
        for n in range(m, NV, 3):
            loads.append((onorm[p0:p1, n:n + 1], ow[a:a + p1 - p0, :]))
    for i in range(HG):
        loads.append((ident4[:, i, :], c["ident"]))
    LOADED = 16 * len(loads)

    N2, N2E, RN, BRK, NPB, KDF, OSUM, OMS, OME, ORN, OF, RQ2, PBK, RQS = range(14)
    BETA, DEC, DCUT, PI, PLAST, DLAST = range(6)

    def left(t, m):
        s = 1 << m
        return t.rearrange("p (n two s) -> p n two s", two=2, s=s)[:, :, 0, :]

    def left4(t, m):
        s = 1 << m
        return t.rearrange("p h (n two s) -> p h n two s", two=2, s=s)[:, :, :, 0, :]

    with nc.Block() as block:

        @block.sync
        def _(sp):
            ph.start(sp, "sp")
            for dst_, src_ in loads:
                sp.dma_start(dst_, src_).then_inc(wts_loaded, 16)
            sp.dma_start(x[:], tiles(x_in[0:G, :])).then_inc(x_loaded.sem, 16)
            with sp.Fori(0, NB) as b, sp.Fori(0, NG) as g:
                n = sp.snap(b * NG + g + 1)
                ahead = sp.snap(n % TURNS * G)
                sp.wait_ge(*y_sb.at(n, 1))
                sp.dma_start(x[:], tiles(x_in[bass.ds(ahead, G), :])).then_inc(x_loaded.sem, 16)
                sp.wait_ge(*out_sb.at(n, GT))
                sp.dma_start(tiles(dst[bass.ds(scratch_row(b, g), G), :]), out[:]).then_inc(stored.sem, 16)
            sp.wait_ge(*stored.at(TURNS + 1, 0))
            sp.wait_ge(*x_loaded.at(TURNS + 1, 16))

        @block.gpsimd
        def _(pool):
            ph.start(pool, "pool")
            pool.wait_ge(wts_loaded, LOADED)

            def token_roots(n):
                pool.wait_ge(*root1.at(n, 2))
                pool.wait_ge(*y_sb.at(n, 1))
                pool.tensor_tensor(rstd[:, 0, :], ms[:, 0, :], minus_half[:, 0:GT], ALU.pow).then_inc(root1_done.sem, 1)
                pool.wait_ge(*root2.at(n, 8))
                pool.tensor_tensor(rstd[:, 1, :], ms[:, 1, :], minus_half[:, 0:GT], ALU.pow).then_inc(root2_done.sem, 1)

            token_roots(0)
            with pool.Fori(0, NB) as b, pool.Fori(0, NG) as g:
                n = pool.snap(b * NG + g + 1)

                def squares(t):
                    if t == 0:
                        pool.wait_ge(*silu.at(n, NQK))
                    pool.wait_ge(*n2_ps.at(n, t))
                    now = qk[:, :, :, t * P:(t + 1) * P].rearrange("p h r i -> p (h r) i")
                    pool.tensor_tensor(sq[:].rearrange("p h r i -> p (h r) i"), now, now, ALU.mult).then_inc(sq_sb.sem, 1)

                def roots(t):
                    pool.wait_ge(*n2_sb.at(n, t + 1))
                    pool.tensor_tensor(cf[:, t % 2, RN, :], cf[:, t % 2, N2E, :], minus_half[:, 0:2 * H], ALU.pow)\
                        .then_inc(rn_sb.sem, 1)

                def apply_gate(t):
                    pool.wait_ge(*osq.at(n, t + 1))
                    of = o[:].rearrange("p h v -> p (h v)")
                    pool.tensor_tensor(of, of, gate[:, t, :], ALU.mult).then_inc(o_gated.sem, 1)

                def apply_norm(t):
                    pool.wait_ge(*om.at(n, 4 * t + 3))
                    pool.tensor_tensor(cf[:, t % 2, ORN, 0:H], cf[:, t % 2, OME, 0:H], minus_half[:, 0:H], ALU.pow)\
                        .then_inc(orn.sem, 1)
                    pool.wait_ge(*o_gated.at(n, t + 1))
                    pool.wait_ge(*om.at(n, 4 * t + 4))
                    pool.tensor_tensor(o[:], o[:], cf[:, t % 2, OF, 0:H].unsqueeze(2).to_broadcast([P, H, DV]), ALU.mult)\
                        .then_inc(og_sb.sem, 1)

                squares(0)
                roots(0)
                for t in range(GT):
                    if t > 0:
                        apply_gate(t - 1)
                    if t < GT - 1:
                        squares(t + 1)
                    if t > 0:
                        apply_norm(t - 1)
                    if t < GT - 1:
                        roots(t + 1)
                token_roots(n)
                apply_gate(GT - 1)
                apply_norm(GT - 1)

        @block.tensor
        def _(pe):
            ph.start(pe, "pe")
            pe.wait_ge(wts_loaded, LOADED)
            pe.wait_ge(prepared, 3)
            with pe.Fori(0, NB) as b, pe.Fori(0, NG) as g:
                n = pe.snap(b * NG + g + 1)
                pe.wait_ge(*hn_sb.at(n, 1))
                pe.wait_ge(*out_sb.at(n, 0))
                for i in range(2):
                    pe.wait_ge(*state_sb[i].at(n, 0))
                for t in range(GT):
                    mm = pe.transpose(ps[:, 6, t * P:(t + 1) * P], hn[:, t, :], ident[:])
                mm.then_inc(ht_ps.sem, 1)
                pe.wait_ge(*ht_sb.at(n, 1))
                for t in range(GT):
                    mm = pe.matmul(ps[:, 6, t * 2 * H:(t + 1) * 2 * H], ht[:, 3 + t * P:3 + (t + 1) * P], wba[:],
                                   start=True, stop=True)
                mm.then_inc(ba_ps.sem, 1)
                pe.wait_ge(*zeroed.at(b + 1, 2))
                pe.wait_ge(*ht_halo.at(n, 0))
                for u in range(NQK + NV):
                    pe.wait_ge(*use_sb.at(n, freed(u, SLOTS, USES)))
                    if u < NQK:
                        M, lhs = DK, (wq, wk)[u % 2][:, u // 2 * DK:(u // 2 + 1) * DK]
                    else:
                        M, lhs = P, wv[:, (u - NQK) * P:(u - NQK + 1) * P]
                    slot = 2 * (u % SLOTS)
                    pe.matmul(ps[0:M, slot, :], lhs, ht[:, 0:G], start=True, stop=True)
                    pe.matmul(ps[0:M, slot + 1, 0:3], lhs, ht[:, G:G + 3], start=True, stop=True).then_inc(use_ps.sem, 1)
                for u in range(NQK + NV, USES):
                    pe.wait_ge(*use_sb.at(n, freed(u, SLOTS, USES)))
                    for i in range(2):
                        k = 2 * (u - NQK - NV) + i
                        mm = pe.matmul(ps[:, 2 * (u % SLOTS) + i, :], ht[:, 3 + k // 3 * P:3 + (k // 3 + 1) * P],
                                       wg[:, k % 3 * 512:(k % 3 + 1) * 512], start=True, stop=True)
                    mm.then_inc(use_ps.sem, 1)
                pe.wait_ge(*za_step.at(n, 22))
                for i in range(3):
                    mm = pe.matmul(ps[:, 7, i * GT * H:(i + 1) * GT * H], sums[:, i, :], za[:, 0, :], start=True, stop=True)
                mm.then_inc(cum_ps.sem, 1)

                def heads(i):
                    return [(j, HG * i + j) for j in range(HG)]

                def decays(t, i):
                    if t == 0:
                        pe.wait_ge(*decay_cut.at(n, 1))
                        pe.wait_ge(*use_sb.at(n, USES))
                        pe.wait_ge(*silu.at(n, NQK + NV))
                    else:
                        pe.wait_ge(*kd_sb[i].at(n, t))
                    for j, h in heads(i):
                        mm = pe.matmul(ps[:, 4 * i, j * P:(j + 1) * P], ex[:, DCUT, t, h:h + 1].to_broadcast([P, P]), ident[:],
                                       start=True, stop=True)
                    mm.then_inc(dec_ps[i].sem, 1)

                def norms(t):
                    pe.wait_ge(*sq_sb.at(n, t + 1))
                    pe.wait_ge(*gd_sb[0].at(n, t + 1))
                    for k in range(2 * H):
                        mm = pe.matmul(ps[:, 0, k:k + 1], sq[:, k // 2, k % 2, :], sums[0:DK, 1, 0:1], start=True, stop=True)
                    mm.then_inc(n2_ps.sem, 1)

                def products(t, i):
                    pe.wait_ge(*o_sb[i].at(n, t))
                    for j, h in heads(i):
                        mm = pe.matmul(ps[:, 4 * i + 1 + j // 2, j % 2 * 2 * P:(j % 2 + 1) * 2 * P],
                                       qk[:, h, 1, t * P:(t + 1) * P], qk[:, h, :, t * P:(t + 1) * P], start=True, stop=True)
                    mm.then_inc(kq_ps[i].sem, 1)

                def tokens_first(t, i):
                    B = 4 * i
                    pe.wait_ge(*state_sb[i].at(n, t))
                    pe.wait_ge(*(n2_sb.at(n, t + 1) if i == 0 else gd_sb[i].at(n, t + 1)))
                    for j, h in heads(i):
                        mm = pe.transpose(ps[:, B, j * DK:(j + 1) * DK], qk[:, h, 1, t * P:(t + 1) * P], ident[0:DK, 0:DK])
                    mm.then_inc(kt_ps[i].sem, 1)
                    pe.wait_ge(*al_sb[i].at(n, t + 1))
                    for j, h in heads(i):
                        mm = pe.transpose(ps[:, B + 3, j * P:(j + 1) * P], al[:, h, 1, :], ident[:])
                    mm.then_inc(lx_ps[i].sem, 1)
                    for k in range(6):
                        mm = pe.transpose(ps[:, B + 1 + k // 3, k % 3 * P:(k % 3 + 1) * P],
                                          vt[:, 6 * i + k, t * P:(t + 1) * P], ident[:])
                    mm.then_inc(vt_ps[i].sem, 1)

                def level_lx(t, i, m):
                    pe.wait_ge(*tm_sb[i].at(n, LEVELS * t + m))
                    pe.wait_ge(*am_sb[i].at(n, LEVELS * t + m))
                    for j, h in heads(i):
                        mm = pe.matmul(ps[:, 4 * i + 3, j * 64:(j + 1) * 64], al[:, h, 1, :], left(tm[:, h, :], m),
                                       start=True, stop=True)
                    mm.then_inc(lx_ps[i].sem, 1)

                def level_ty(t, i, m):
                    pe.wait_ge(*am_sb[i].at(n, LEVELS * t + m + 1))
                    pe.wait_ge(*tt_sb[i].at(n, LEVELS * t + m))
                    pe.wait_ge(*vb_sb[i].at(n, t + 1))
                    for j, h in heads(i):
                        mm = pe.matmul(ps[:, 4 * i + 2, j * 64:(j + 1) * 64], tt[:, h, :], am[:, h, :], start=True, stop=True)
                    mm.then_inc(ty_ps[i].sem, 1)

                def level_tt(t, i, m):
                    pe.wait_ge(*tm_sb[i].at(n, LEVELS * t + m + 1))
                    pe.wait_ge(*(vb_sb[i].at(n, t + 1) if m == 0 else tt_sb[i].at(n, LEVELS * t + m)))
                    for j, h in heads(i):
                        mm = pe.transpose(ps[:, 4 * i + 1, j * P:(j + 1) * P], tm[:, h, :], ident[:])
                    mm.then_inc(tt_ps[i].sem, 1)

                def pairs(i, banks, M, lhs, rhs, done):
                    for j, h in heads(i):
                        mm = pe.matmul(ps[0:M, 4 * i + banks[j // 2], j % 2 * DV:(j % 2 + 1) * DV], lhs(h), rhs(h),
                                       start=True, stop=True)
                    mm.then_inc(done.sem, 1)

                def from_state(t, i):
                    pe.wait_ge(*(ot_sb.at(n, 3 * t) if i == 0 else out_sb.at(n, t)))
                    if t < GT - 1:
                        pe.wait_ge(*(n2_sb.at(n, t + 2) if i == 0 else gd_sb[i].at(n, t + 2)))
                    pe.wait_ge(*state_sb[i].at(n, t))
                    pe.wait_ge(*zeroed.at(b + 1, 2))
                    pe.wait_ge(*kd_sb[i].at(n, t + 1))
                    pe.wait_ge(*am_sb[i].at(n, LEVELS * t + LEVELS))
                    pairs(i, (0, 3), P, lambda h: qk[:, h, 1, t * P:(t + 1) * P], lambda h: state[:, h, :], ks_ps[i])

                def solve(t, i):
                    pe.wait_ge(*r_sb[i].at(n, t + 1))
                    pe.wait_ge(*tt_sb[i].at(n, LEVELS * t + LEVELS))
                    pairs(i, (1, 2), P, lambda h: tt[:, h, :], lambda h: vr[:, h, :], delta_ps[i])
                    pairs(i, (0, 3), P, lambda h: qk[:, h, 0, t * P:(t + 1) * P], lambda h: state[:, h, :], qs_ps[i])

                def outputs(t, i):
                    pe.wait_ge(*delta_sb[i].at(n, t + 1))
                    pairs(i, (1, 2), P, lambda h: al[:, h, 0, :], lambda h: delta[:, h, :], ad_ps[i])
                    pe.wait_ge(*qs_sb[i].at(n, t + 1))
                    pairs(i, (0, 3), DK, lambda h: kd[:, h, :], lambda h: delta[:, h, :], up_ps[i])

                def transpose_out(t, k):
                    if k == 0:
                        pe.wait_ge(*og_sb.at(n, t + 1))
                    if k == 2:
                        pe.wait_ge(*ot_sb.at(n, 3 * t + 1))
                    elif t == GT - 1:
                        pe.wait_ge(*state_sb[k].at(n, GT))
                    elif t == GT - 2:
                        pe.wait_ge(*kd_sb[k].at(n, GT))
                    else:
                        pe.wait_ge(*(n2_sb.at(n, t + 3) if k == 0 else gd_sb[1].at(n, t + 3)))
                    for i in range(4):
                        m = 4 * k + i
                        mm = pe.transpose(ps[:, (0, 4, 0)[k], i * P:(i + 1) * P],
                                          o[:].rearrange("p h v -> p (h v)")[:, m * P:(m + 1) * P], ident[:])
                    mm.then_inc(ot_ps.sem, 1)

                def project_out(t):
                    pe.wait_ge(*ot_sb.at(n, 3 * t + 3))
                    for m in range(NV):
                        mm = pe.matmul(ps[:, 4, 0:D], ot[:, m, :], wo[:, m, :], start=m == 0, stop=m == NV - 1)
                    mm.then_inc(y_ps.sem, 1)

                for i in range(2):
                    decays(0, i)
                norms(0)
                for t in range(GT):
                    for i in range(2):
                        products(t, i)
                    for i in range(2):
                        tokens_first(t, i)
                    for i in range(2):
                        level_tt(t, i, 0)
                    for m in range(1, LEVELS):
                        for i in range(2):
                            level_lx(t, i, m)
                        for i in range(2):
                            level_ty(t, i, m)
                        for i in range(2):
                            level_tt(t, i, m)
                        if m == 1 and t < GT - 1:
                            for i in range(2):
                                decays(t + 1, i)
                        if m == 2 and t < GT - 1:
                            norms(t + 1)
                        if m == 3 and t > 0:
                            transpose_out(t - 1, 0)
                            transpose_out(t - 1, 1)
                        if m == 4 and t > 0:
                            transpose_out(t - 1, 2)
                        if m == 5 and t > 0:
                            project_out(t - 1)
                    for i in range(2):
                        from_state(t, i)
                    for i in range(2):
                        solve(t, i)
                    for i in range(2):
                        outputs(t, i)
                for k in range(3):
                    transpose_out(GT - 1, k)
                project_out(GT - 1)

        @block.scalar
        def _(act):
            ph.start(act, "act")
            act.wait_ge(wts_loaded, LOADED)
            act.activation(decay_rate[:], decay_rate[:], ACT.Exp).then_inc(prepared, 1)
            with act.Fori(0, NB) as b, act.Fori(0, NG) as g:
                n = act.snap(b * NG + g + 1)
                act.wait_ge(*ht_ps.at(n, 1))
                act.wait_ge(*use_ps.at(n, 0))
                act.wait_ge(*ht_halo.at(n, 0))
                act.activation(ht[:, 3:], ps[:, 6, :], ACT.Copy).then_inc(ht_sb.sem, 1)
                act.wait_ge(*za_step.at(n, 4))
                act.activation(za[:, 4, :], za[:, 3, :], ACT.Exp).then_inc(za_exp.sem, 1)
                act.activation(za[:, 5, :], za[:, 1, :], ACT.Exp, scale=-1.0).then_inc(za_exp.sem, 1)

                def taps(u):
                    M = DK if u < NQK else P
                    slot, k = 2 * (u % SLOTS), u % SLOTS
                    wts = conv_qk[:, u // 2, u % 2, :] if u < NQK else conv_v[:, u - NQK, :]
                    act.wait_ge(*use_ps.at(n, u + 1))
                    act.wait_ge(*tap.at(n, 3 * freed(u, SLOTS, NQK + NV)))
                    act.wait_ge(*silu.at(n, freed(u, SLOTS, NQK + NV)))
                    both_banks = ps[0:M, slot:slot + 2, :].rearrange("p a i -> p (a i)")
                    act.activation(raw[0:M, k, :], both_banks[:, 0:3 + G], ACT.Copy)
                    act.activation(conv[0:M, k, :], both_banks[:, 0:G], ACT.Copy, scale=wts[:, 0:1]).then_inc(use_sb.sem, 1)

                def activate(u):
                    M, k = (DK if u < NQK else P), u % SLOTS
                    act.wait_ge(*tap.at(n, 3 * u + 3))
                    to = qk[:, u // 2, u % 2, :] if u < NQK else vt[:, u - NQK, :]
                    if u == 0:
                        for i in range(2):
                            act.wait_ge(*qs_ps[i].at(n, 0))
                            act.wait_ge(*vt_ps[i].at(n, 0))
                    act.activation(to, conv[0:M, k, :], ACT.Silu).then_inc(silu.sem, 1)

                for u in range(NQK + NV):
                    taps(u)
                    if u >= 1:
                        activate(u - 1)
                activate(NQK + NV - 1)
                for u in range(NQK + NV, USES):
                    act.wait_ge(*use_ps.at(n, u + 1))
                    if u == NQK + NV:
                        act.wait_ge(*og_sb.at(n, 0))
                    k = 2 * (u - NQK - NV)
                    act.activation(gate[:].rearrange("p t v -> p (t v)")[:, k * 512:(k + 2) * 512],
                                   ps[:, 2 * (u % SLOTS):2 * (u % SLOTS) + 2, :].rearrange("p a i -> p (a i)"),
                                   ACT.Silu).then_inc(use_sb.sem, 1)
                act.wait_ge(*za_step.at(n, 22))
                act.activation(ex[:, DEC, :, :], za[:, 0, :].rearrange("p (t h) -> p t h", h=H), ACT.Exp).then_inc(ex_sb.sem, 1)
                act.wait_ge(*cum_ps.at(n, 1))
                act.activation(ex[:, PI:PI + 3, :, :].rearrange("p k t h -> p (k t h)"), ps[:, 7, 0:3 * GT * H], ACT.Exp)\
                    .then_inc(ex_sb.sem, 1)

                def heads(i):
                    return [(j, HG * i + j) for j in range(HG)]

                def tokens_first(t, i):
                    B = 4 * i
                    act.wait_ge(*kt_ps[i].at(n, t + 1))
                    act.wait_ge(*coef.at(n, 4 * t + 4))
                    act.wait_ge(*up_ps[i].at(n, t))
                    for j, h in heads(i):
                        e = act.activation(kd[:, h, :], ps[:, B, j * DK:(j + 1) * DK], ACT.Copy, scale=cf[:, t % 2, KDF, h:h + 1])
                    e.then_inc(kd_sb[i].sem, 1)
                    act.wait_ge(*lx_ps[i].at(n, LEVELS * t))
                    act.wait_ge(*tt_ps[i].at(n, LEVELS * t))
                    act.activation(tm[:, HG * i:HG * i + HG, :], ident4[:], ACT.Copy).then_inc(tm_one[i].sem, 1)
                    act.wait_ge(*vt_ps[i].at(n, t + 1))
                    act.wait_ge(*delta_ps[i].at(n, t))
                    for j, h in heads(i):
                        e = act.activation(vr[:, h, :], ps[:, B + 1 + j // 2, j % 2 * DV:(j % 2 + 1) * DV], ACT.Copy,
                                           scale=ex[:, BETA, t, h:h + 1])
                    e.then_inc(vb_sb[i].sem, 1)

                def level_tt(t, i, m):
                    act.wait_ge(*tt_ps[i].at(n, LEVELS * t + m + 1))
                    if m == 0:
                        act.wait_ge(*delta_ps[i].at(n, t))
                    act.activation(tt[:, HG * i:HG * i + HG, :], ps[:, 4 * i + 1, :].rearrange("p (h k) -> p h k", k=P),
                                   ACT.Copy).then_inc(tt_sb[i].sem, 1)

                def solve(t, i):
                    act.wait_ge(*delta_ps[i].at(n, t + 1))
                    act.wait_ge(*up_ps[i].at(n, t))
                    act.wait_ge(*om.at(n, 4 * t - 3))
                    act.activation(delta[:, HG * i:HG * i + HG, :].rearrange("p (a h) v -> p a (h v)", a=2),
                                   ps[:, 4 * i + 1:4 * i + 3, 0:2 * DV], ACT.Copy).then_inc(delta_sb[i].sem, 1)
                    act.wait_ge(*qs_ps[i].at(n, t + 1))
                    act.wait_ge(*ot_ps.at(n, 3 * t))
                    for j, h in heads(i):
                        e = act.activation(o[:, h, :], ps[:, 4 * i + 3 * (j // 2), j % 2 * DV:(j % 2 + 1) * DV], ACT.Copy,
                                           scale=ex[:, PI, t, h:h + 1])
                    e.then_inc(qs_sb[i].sem, 1)

                def square_out(t):
                    for i in range(2):
                        act.wait_ge(*o_sb[i].at(n, t + 1))
                        act.wait_ge(*up_ps[i].at(n, t + 1))
                    act.activation(delta[:], o[:], ACT.Square).then_inc(osq.sem, 1)

                def copy_ot(t, k):
                    act.wait_ge(*ot_ps.at(n, 3 * t + k + 1))
                    act.wait_ge(*y_ps.at(n, t))
                    act.activation(ot[:, 4 * k:4 * k + 4, :], ps[:, (0, 4, 0)[k], :].rearrange("p (m i) -> p m i", i=P),
                                   ACT.Copy).then_inc(ot_sb.sem, 1)

                for t in range(GT):
                    for i in range(2):
                        tokens_first(t, i)
                    for m in range(LEVELS):
                        for i in range(2):
                            level_tt(t, i, m)
                        if m == 3 and t > 0:
                            copy_ot(t - 1, 0)
                            copy_ot(t - 1, 1)
                        if m == 4 and t > 0:
                            copy_ot(t - 1, 2)
                    for i in range(2):
                        solve(t, i)
                    square_out(t)
                for k in range(3):
                    copy_ot(GT - 1, k)

        @block.vector
        def _(dve):
            ph.start(dve, "dve")
            dve.memset(cf[:], 0.0).then_inc(seen, 1)
            dve.wait_ge(wts_loaded, LOADED)
            dve.tensor_tensor(wo[:], wo[:], onorm[:].unsqueeze(2).to_broadcast([P, NV, D]), ALU.mult)
            for wt in (wq, wk, wv, wg):
                dve.tensor_scalar(wt[:], wt[:], norm1[:], None, ALU.mult)
            dve.tensor_scalar(wba[:], wba[:], norm1[:], None, ALU.mult).then_inc(prepared, 1)
            dve.wait_ge(prepared, 2)
            dve.tensor_scalar(decay_rate[:], decay_rate[:], -1.0, None, ALU.mult).then_inc(prepared, 1)
            dve.wait_ge(prepared, 3)

            def token_moments(n):
                dve.wait_ge(*x_loaded.at(n, 32))
                for t in range(GT):
                    dve.bn_stats(stats[:, t, :], x[:, t, :]).then_inc(stats_done.sem, 1)
                dve.wait_ge(*stats_done.at(n, 2 * GT))
                dve.sem_inc(seen, 1)
                for t in range(GT):
                    dve.bn_aggr(mv[:, t, :], stats[:, t, :]).then_inc(moments.sem, 1)
                dve.wait_ge(*moments.at(n, 2 * GT))
                dve.tensor_scalar(ms[:, 0, :], mv[:, :, 1], 1e-5, None, ALU.add).then_inc(root1.sem, 1)

            def token_mean_squares(n):
                dve.wait_ge(*root1_done.at(n, 2))
                dve.tensor_tensor(ms[:, 1, :], rstd[:, 0, :], rstd[:, 0, :], ALU.mult).then_inc(root2.sem, 1)
                dve.wait_ge(*ht_ps.at(n, 1))
                for t in range(GT):
                    ln = dve.tensor_scalar(hn[:, t, :], x[:, t, :], mv[:, t, 0:1], rstd[:, 0, t:t + 1], ALU.subtract, ALU.mult)
                ln.then_inc(root2.sem, 1)
                dve.wait_ge(*root2.at(n, 4 + 1))
                dve.tensor_tensor(ms[:, 1, :], ms[:, 1, :], mv[:, :, 1], ALU.mult).then_inc(root2.sem, 1)
                dve.wait_ge(*root2.at(n, 4 + 3))
                dve.tensor_scalar(ms[:, 1, :], ms[:, 1, :], 1e-6, None, ALU.add).then_inc(root2.sem, 1)

            def norm_tokens(n):
                dve.wait_ge(*root2_done.at(n, 2))
                dve.tensor_tensor(hn[:], hn[:], rstd[:, 1, :].unsqueeze(2).to_broadcast([P, GT, D]), ALU.mult)\
                    .then_inc(hn_sb.sem, 1)

            token_moments(0)
            token_mean_squares(0)
            norm_tokens(0)
            with dve.Fori(0, NB) as b:
                n0 = dve.snap(b * NG + 1)
                for i in range(2):
                    dve.wait_ge(*state_sb[i].at(n0, 0))
                dve.memset(state[:], 0.0).then_inc(zeroed.sem, 1)
                dve.wait_ge(*ht_halo.at(n0, 0))
                dve.memset(ht[:, 0:3], 0.0).then_inc(zeroed.sem, 1)
                with dve.Fori(0, NG) as g:
                    n = dve.snap(b * NG + g + 1)
                    dve.wait_ge(*out_sb.at(n, 0))
                    for t in range(GT):
                        ln = dve.tensor_scalar(y[:, t, :], x[:, t, :], mv[:, t, 0:1], rstd[:, 0, t:t + 1], ALU.subtract, ALU.mult)
                    ln.then_inc(y_sb.sem, 1)

                    step = [0]

                    def then(ins):
                        step[0] += 1
                        ins.then_inc(za_step.sem, 1)
                        dve.wait_ge(*za_step.at(n, step[0]))

                    ba = ps[:, 6, 0:GT * 2 * H].rearrange("p (t r h) -> p r t h", t=GT, r=2)

                    def row(k):
                        return za[:, k, :]

                    def row3(k):
                        return za[:, k, :].rearrange("p (t h) -> p t h", h=H)

                    dve.wait_ge(*ba_ps.at(n, 1))
                    then(dve.tensor_copy(row3(1), ba[:, 0]))
                    then(dve.tensor_tensor(row3(2), ba[:, 1], dt_bias[:].unsqueeze(1).to_broadcast([P, GT, H]), ALU.add))
                    then(dve.tensor_scalar(row(3), row(2), -1.0, None, ALU.mult))
                    then(dve.tensor_tensor(row(3), row(3), row(2), ALU.min))
                    dve.wait_ge(*za_exp.at(n, 2))
                    then(dve.tensor_scalar(row(6), row(4), 2.0, None, ALU.add))
                    then(dve.reciprocal(row(6), row(6)))
                    then(dve.tensor_tensor(row(6), row(6), row(4), ALU.mult))
                    then(dve.tensor_tensor(row(7), row(6), row(6), ALU.mult))
                    then(dve.tensor_scalar(row(8), row(7), 1.0 / 17, None, ALU.mult))
                    for k in (15, 13, 11, 9, 7, 5, 3):
                        then(dve.scalar_tensor_tensor(out=row(8), in0=row(8), scalar=1.0 / k, in1=row(7), op0=ALU.add, op1=ALU.mult))
                    then(dve.scalar_tensor_tensor(out=row(8), in0=row(8), scalar=1.0, in1=row(6), op0=ALU.add, op1=ALU.mult))
                    then(dve.tensor_scalar(row(9), row(2), 0.0, None, ALU.max))
                    then(dve.scalar_tensor_tensor(out=row(9), in0=row(8), scalar=2.0, in1=row(9), op0=ALU.mult, op1=ALU.add))
                    then(dve.tensor_tensor(row3(9), row3(9), decay_rate[:].unsqueeze(1).to_broadcast([P, GT, H]), ALU.mult))
                    then(dve.tensor_scalar(row(5), row(5), 1.0, None, ALU.add))
                    for i in range(2):
                        dve.wait_ge(*vb_sb[i].at(n, 0))
                        dve.wait_ge(*dec_ps[i].at(n, 0))
                    dve.wait_ge(*cum_ps.at(n, 0))
                    dve.tensor_scalar(row(0), row(9), -1e4, None, ALU.max)
                    dve.reciprocal(ex[:, BETA, :, :], row3(5)).then_inc(za_step.sem, 1)

                    for u in range(NQK + NV):
                        M, k = (DK if u < NQK else P), u % SLOTS
                        wts = conv_qk[:, u // 2, u % 2, :] if u < NQK else conv_v[:, u - NQK, :]
                        dve.wait_ge(*use_sb.at(n, u + 1))
                        for i in range(1, 4):
                            if i > 1:
                                dve.wait_ge(*tap.at(n, 3 * u + i - 1))
                            dve.scalar_tensor_tensor(out=conv[0:M, k, :], in0=raw[0:M, k, i:i + G], scalar=wts[:, i:i + 1],
                                                     in1=conv[0:M, k, :], op0=ALU.mult, op1=ALU.add).then_inc(tap.sem, 1)
                    dve.wait_ge(*use_ps.at(n, USES))
                    dve.tensor_copy(ht[:, 0:3], ht[:, G:G + 3]).then_inc(ht_halo.sem, 1)
                    dve.wait_ge(*ex_sb.at(n, 2))
                    dve.tensor_scalar(ex[:, DCUT, :, :], ex[:, DEC, :, :], not_first[:], None, ALU.mult).then_inc(decay_cut.sem, 1)

                    def heads(i):
                        return [(j, HG * i + j) for j in range(HG)]

                    def decays(t, i):
                        dve.wait_ge(*dec_ps[i].at(n, t + 1))
                        dve.wait_ge(*al_sb[i].at(n, t))
                        dve.tensor_tensor_scan(gd[:, HG * i:HG * i + HG, :].rearrange("p h k -> p (h k)"), ps[:, 4 * i, :],
                                               ident4[:].rearrange("p h k -> p (h k)"), 0.0, ALU.mult, ALU.add)\
                            .then_inc(gd_sb[i].sem, 1)

                    def norms(t):
                        dve.wait_ge(*n2_ps.at(n, t + 1))
                        dve.wait_ge(*rn_sb.at(n, t))
                        dve.tensor_scalar(cf[:, t % 2, N2E, :], ps[:, 0, 0:2 * H], 1e-6, None, ALU.add).then_inc(n2_sb.sem, 1)

                    def coefficients(t):
                        f = cf[:, t % 2]
                        dve.wait_ge(*rn_sb.at(n, t + 1))
                        rk = f[:, RN, :].rearrange("p (h r) -> p h r", r=2)[:, :, 1]
                        rq = f[:, RN, :].rearrange("p (h r) -> p h r", r=2)[:, :, 0]
                        dve.tensor_tensor(f[:, BRK, 0:H], rk, ex[:, BETA, t, :], ALU.mult).then_inc(coef.sem, 1)
                        dve.tensor_tensor(f[:, KDF, 0:H], rk, ex[:, DLAST, t, :], ALU.mult)
                        dve.tensor_scalar(f[:, RQS, 0:H], rq, DK ** -0.5, None, ALU.mult).then_inc(coef.sem, 1)
                        dve.wait_ge(*coef.at(n, 4 * t + 1))
                        dve.scalar_tensor_tensor(out=f[:, NPB, 0:H], in0=f[:, BRK, 0:H], scalar=-1.0, in1=ex[:, PI, t, :],
                                                 op0=ALU.mult, op1=ALU.mult).then_inc(coef.sem, 1)
                        dve.wait_ge(*coef.at(n, 4 * t + 2))
                        dve.tensor_tensor(f[:, RQ2, 0:H], f[:, RQS, 0:H], f[:, RQS, 0:H], ALU.mult).then_inc(coef.sem, 1)
                        dve.wait_ge(*coef.at(n, 4 * t + 4))

                    def products(t, i):
                        dve.wait_ge(*kq_ps[i].at(n, t + 1))
                        dve.wait_ge(*gd_sb[i].at(n, t + 1))
                        for j, h in heads(i):
                            qk_ps = ps[:, 4 * i + 1 + j // 2, j % 2 * 2 * P:(j % 2 + 1) * 2 * P].rearrange("p (r k) -> p r k", r=2)
                            rk = cf[:, t % 2, RN, 2 * h + 1:2 * h + 2]
                            e = dve.scalar_tensor_tensor(out=al[:, h, :, :], in0=qk_ps, scalar=rk,
                                                         in1=gd[:, h, :].unsqueeze(1).to_broadcast([P, 2, P]),
                                                         op0=ALU.mult, op1=ALU.mult)
                        e.then_inc(al_sb[i].sem, 1)

                    def level_am(t, i, m):
                        dve.wait_ge(*lx_ps[i].at(n, LEVELS * t + m + 1))
                        for j, h in heads(i):
                            if m == 0:
                                lx = left(ps[:, 4 * i + 3, j * P:(j + 1) * P], 0)
                                e = dve.scalar_tensor_tensor(out=am[:, h, :].unsqueeze(2), in0=lx, scalar=cf[:, t % 2, BRK, h:h + 1],
                                                             in1=blocks[:, 0, :].unsqueeze(2), op0=ALU.mult, op1=ALU.mult)
                            else:
                                lx = ps[:, 4 * i + 3, j * 64:(j + 1) * 64]
                                e = dve.scalar_tensor_tensor(out=am[:, h, :], in0=lx, scalar=cf[:, t % 2, BRK, h:h + 1],
                                                             in1=blocks[:, m, :], op0=ALU.mult, op1=ALU.mult)
                        e.then_inc(am_sb[i].sem, 1)

                    def level_tm(t, i, m):
                        half = left4(tm[:, HG * i:HG * i + HG, :], m)
                        if m == 0:
                            dve.wait_ge(*tm_one[i].at(n, t + 1))
                            dve.wait_ge(*am_sb[i].at(n, LEVELS * t + 1))
                            more = am[:, HG * i:HG * i + HG, :].rearrange("p h (n s) -> p h n s", s=1)
                        else:
                            dve.wait_ge(*ty_ps[i].at(n, (LEVELS - 1) * t + m))
                            dve.wait_ge(*tm_sb[i].at(n, LEVELS * t + m))
                            more = ps[:, 4 * i + 2, 0:HG * 64].rearrange("p (h n s) -> p h n s", h=HG, s=1 << m)
                        dve.tensor_tensor(half, half, more, ALU.add).then_inc(tm_sb[i].sem, 1)

                    def rest(t, i):
                        dve.wait_ge(*ks_ps[i].at(n, t + 1))
                        dve.wait_ge(*vb_sb[i].at(n, t + 1))
                        for j, h in heads(i):
                            e = dve.scalar_tensor_tensor(out=vr[:, h, :],
                                                         in0=ps[:, 4 * i + 3 * (j // 2), j % 2 * DV:(j % 2 + 1) * DV],
                                                         scalar=cf[:, t % 2, NPB, h:h + 1], in1=vr[:, h, :], op0=ALU.mult, op1=ALU.add)
                        e.then_inc(r_sb[i].sem, 1)

                    def outputs(t, i):
                        dve.wait_ge(*ad_ps[i].at(n, t + 1))
                        dve.wait_ge(*qs_sb[i].at(n, t + 1))
                        mine = o[:, HG * i:HG * i + HG, :].rearrange("p (a h) v -> p a (h v)", a=2)
                        dve.tensor_tensor(mine, mine, ps[:, 4 * i + 1:4 * i + 3, 0:2 * DV], ALU.add).then_inc(o_sb[i].sem, 1)
                        dve.wait_ge(*up_ps[i].at(n, t + 1))
                        dve.wait_ge(*qs_ps[i].at(n, t + 1))
                        dve.wait_ge(*state_sb[i].at(n, t))
                        dve.wait_ge(*zeroed.at(b + 1, 2))
                        for j, h in heads(i):
                            e = dve.scalar_tensor_tensor(out=state[:, h, :], in0=state[:, h, :], scalar=ex[0:DK, PLAST, t, h:h + 1],
                                                         in1=ps[0:DK, 4 * i + 3 * (j // 2), j % 2 * DV:(j % 2 + 1) * DV],
                                                         op0=ALU.mult, op1=ALU.add)
                        e.then_inc(state_sb[i].sem, 1)

                    def mean_squares(t):
                        f = cf[:, t % 2]
                        dve.wait_ge(*osq.at(n, t + 1))
                        dve.tensor_reduce(f[:, OSUM, 0:H], delta[:], AX.X, ALU.add).then_inc(om.sem, 1)
                        dve.wait_ge(*om.at(n, 4 * t + 1))
                        dve.scalar_tensor_tensor(out=f[:, OMS, 0:H], in0=f[:, OSUM, 0:H], scalar=1.0 / DV,
                                                 in1=f[:, RQ2, 0:H], op0=ALU.mult, op1=ALU.mult).then_inc(om.sem, 1)
                        dve.wait_ge(*om.at(n, 4 * t + 2))
                        dve.tensor_scalar(f[:, OME, 0:H], f[:, OMS, 0:H], 1e-6, None, ALU.add).then_inc(om.sem, 1)

                    def norm_factors(t):
                        f = cf[:, t % 2]
                        dve.wait_ge(*orn.at(n, t + 1))
                        dve.tensor_tensor(f[:, OF, 0:H], f[:, ORN, 0:H], f[:, RQS, 0:H], ALU.mult).then_inc(om.sem, 1)

                    def add_out(t):
                        dve.wait_ge(*y_ps.at(n, t + 1))
                        if t == 0:
                            dve.wait_ge(*stored.at(n, 0))
                        dve.tensor_tensor(out[:, t, :], ps[:, 4, 0:D], y[:, t, :], ALU.add).then_inc(out_sb.sem, 1)

                    for i in range(2):
                        decays(0, i)
                    norms(0)
                    coefficients(0)
                    for t in range(GT):
                        for i in range(2):
                            products(t, i)
                        if t > 0:
                            mean_squares(t - 1)
                        for m in range(LEVELS):
                            for i in range(2):
                                level_am(t, i, m)
                            for i in range(2):
                                level_tm(t, i, m)
                            if m == 0 and t > 0:
                                norm_factors(t - 1)
                            if m == 1 and t < GT - 1:
                                for i in range(2):
                                    decays(t + 1, i)
                            if m == 2 and t < GT - 1:
                                norms(t + 1)
                            if m == 3 and t < GT - 1:
                                coefficients(t + 1)
                            if m == 5 and t > 0:
                                add_out(t - 1)
                            if m == 3 and t == GT - 1:
                                token_moments(n)
                            if m == 4 and t == GT - 1:
                                token_mean_squares(n)
                            if m == 6 and t == GT - 1:
                                norm_tokens(n)
                        for i in range(2):
                            rest(t, i)
                        for i in range(2):
                            outputs(t, i)
                    mean_squares(GT - 1)
                    norm_factors(GT - 1)
                    add_out(GT - 1)
    ph.close()


def gated_mlp(nc, name, src, dst, c, hidden, func, layernorm, eps, w_up, w_gate, w_down, norm_w, norm_b=None,
              b_up=None, b_gate=None, b_down=None, shifted=False, skip=None):
    chunks = [(a, min(P, hidden - a)) for a in range(0, hidden, P)]
    NC = len(chunks)
    biased = b_up is not None
    extra = int(biased)
    assert not biased or chunks[-1][1] < P
    ph = Phase(nc, name)
    sb, signal = ph.sb, ph.counter
    ps = ph.banks()
    up_w = sb("up_w", [P, hidden])
    gate_w = sb("gate_w", [P, hidden])
    down_w = sb("down_w", [P, NC, D])
    scale = sb("scale", [P, 1])
    shift = sb("shift", [P, 1])
    up_b = sb("up_b", [P, NC])
    gate_b = sb("gate_b", [P, NC])
    ident = sb("ident", [P, P])
    minus_half = sb("minus_half", [P, GT])
    h = sb("h", [P, GT, D])
    x = sb("x", [P, GT, D])
    x2 = sb("x2", [P, GT, D])
    y = sb("y", [P, GT, D])
    stats = sb("stats", [P, GT, 6])
    mv = sb("mv", [P, GT, 2])
    ms = sb("ms", [P, 2, GT])
    rstd = sb("rstd", [P, GT])
    hn = sb("hn", [P, GT, D])
    ht = sb("ht", [P, G])
    gate = sb("gate", [P, 2, G])
    prod = sb("prod", [P, NC, G])

    loaded = ph.semaphore("loaded")
    prepared = ph.semaphore("prepared")
    NH = 2 if shifted else 1
    NX = 2 if skip is not None else 1
    h_loaded = signal("h_loaded", 16 * NH, "sp")
    x_loaded = signal("x_loaded", 16 * NX, "sp")
    stored = signal("stored", 16, "sp")
    stats_done = signal("stats_done", GT, "dve")
    seen = signal("seen", 1, "dve").sem
    moments = signal("moments", GT, "dve")
    under_root = signal("under_root", 3, "dve")
    root = signal("root", 1, "pool")
    normed = signal("normed", GT, "dve")
    ht_ps = signal("ht_ps", 1, "pe")
    ht_sb = signal("ht_sb", 1, "act")
    up_gate_ps = signal("up_gate_ps", NC, "pe")
    gated = signal("gated", NC, "act")
    prod_sb = signal("prod_sb", NC, "dve")
    y_ps = signal("y_ps", 1, "pe")
    y_sb = signal("y_sb", NX, "dve")

    loads = [(up_w[:], w_up), (gate_w[:], w_gate), (ident[:], c["ident"]), (minus_half[:], c["minus_half"][:, 0:GT]),
             (scale[:], norm_w)]
    for n, (a, m) in enumerate(chunks):
        loads.append((down_w[0:m, n, :], w_down(a, m)))
        if biased:
            loads += [(up_b[0:m, n:n + 1], b_up(a, m)), (gate_b[0:m, n:n + 1], b_gate(a, m))]
    if biased:
        loads += [(shift[:], norm_b), (down_w[chunks[-1][1]:chunks[-1][1] + 1, NC - 1, :], b_down)]

    with nc.Block() as block:

        @block.sync
        def _(sp):
            ph.start(sp, "sp")
            for out, in_ in loads:
                sp.dma_start(out, in_).then_inc(loaded, 16)

            def load_h(row):
                if shifted:
                    sp.dma_start(h[:, :, 0:D // 2], tiles(src[bass.ds(row, G), 0:D // 2])).then_inc(h_loaded.sem, 16)
                    sp.dma_start(h[:, :, D // 2:D], tiles(src[bass.ds(row - 1, G), D // 2:D])).then_inc(h_loaded.sem, 16)
                else:
                    sp.dma_start(h[:], tiles(src[bass.ds(row, G), :])).then_inc(h_loaded.sem, 16)

            load_h(scratch_row(0, 0))
            with sp.Fori(0, NB) as b, sp.Fori(0, NG) as g:
                n = sp.snap(b * NG + g + 1)
                row = sp.snap(scratch_row(b, g))
                ahead = sp.snap(n % TURNS)
                sp.wait_ge(*normed.at(n, GT))
                load_h(sp.snap(ahead * G + ahead // NG * PAD + PAD))
                sp.wait_ge(*y_sb.at(n, 0))
                sp.dma_start(x[:], tiles(src[bass.ds(row, G), :])).then_inc(x_loaded.sem, 16)
                if skip is not None:
                    sp.dma_start(x2[:], tiles(skip[bass.ds((b * NG + g) * G, G), :])).then_inc(x_loaded.sem, 16)
                sp.wait_ge(*y_sb.at(n, NX))
                sp.dma_start(tiles(dst[bass.ds(row, G), :]), y[:]).then_inc(stored.sem, 16)
            sp.wait_ge(*stored.at(TURNS + 1, 0))
            sp.wait_ge(*h_loaded.at(TURNS + 1, 16 * NH))

        @block.gpsimd
        def _(pool):
            ph.start(pool, "pool")
            pool.memset(prod[:, NC - 1, :], 1.0).then_inc(prepared, 1)
            pool.wait_ge(loaded, 16 * len(loads))

            def roots(n):
                pool.wait_ge(*under_root.at(n, 6))
                pool.wait_ge(*normed.at(n, GT))
                pool.tensor_tensor(rstd[:], ms[:, 1, :], minus_half[:], ALU.pow).then_inc(root.sem, 1)

            roots(0)
            with pool.Fori(0, NB) as b, pool.Fori(0, NG) as g:
                n = pool.snap(b * NG + g + 1)
                roots(n)

        @block.tensor
        def _(pe):
            ph.start(pe, "pe")
            pe.wait_ge(loaded, 16 * len(loads))
            pe.wait_ge(prepared, 1)

            def transpose_next(n):
                pe.wait_ge(*ht_sb.at(n, 1))
                for t in range(GT):
                    pe.wait_ge(*normed.at(n, GT + t + 1))
                    mm = pe.transpose(ps[:, 0, t * P:(t + 1) * P], hn[:, t, :], ident[:])
                mm.then_inc(ht_ps.sem, 1)

            transpose_next(0)
            with pe.Fori(0, NB) as b, pe.Fori(0, NG) as g:
                n = pe.snap(b * NG + g + 1)
                pe.wait_ge(*ht_sb.at(n, 1))
                for i, (a, m) in enumerate(chunks):
                    pe.wait_ge(*prod_sb.at(n, freed(i, 3, NC)))
                    pe.matmul(ps[0:m, 1 + 2 * (i % 3), :], gate_w[:, a:a + m], ht[:], start=True, stop=True)
                    pe.matmul(ps[0:m, 2 + 2 * (i % 3), :], up_w[:, a:a + m], ht[:], start=True, stop=True)\
                        .then_inc(up_gate_ps.sem, 1)
                transpose_next(n)
                pe.wait_ge(*prod_sb.at(n, NC))
                pe.wait_ge(*y_sb.at(n, 0))
                for t in range(GT):
                    for i, (a, m) in enumerate(chunks):
                        k = m + (extra if i == NC - 1 else 0)
                        mm = pe.matmul(ps[:, 7, t * P:(t + 1) * P], prod[0:k, i, t * P:(t + 1) * P], down_w[0:k, i, :],
                                       start=i == 0, stop=i == NC - 1)
                mm.then_inc(y_ps.sem, 1)

        @block.scalar
        def _(act):
            ph.start(act, "act")
            act.wait_ge(loaded, 16 * len(loads))

            def copy_next(n):
                act.wait_ge(*ht_ps.at(n, 2))
                act.wait_ge(*up_gate_ps.at(n, NC))
                act.activation(ht[:], ps[:, 0, :], ACT.Identity, scale=scale[:],
                               bias=shift[:] if biased else 0.0).then_inc(ht_sb.sem, 1)

            copy_next(0)
            with act.Fori(0, NB) as b, act.Fori(0, NG) as g:
                n = act.snap(b * NG + g + 1)
                for i, (a, m) in enumerate(chunks):
                    act.wait_ge(*up_gate_ps.at(n, i + 1))
                    act.wait_ge(*prod_sb.at(n, freed(i, 2, NC)))
                    act.activation(gate[0:m, i % 2, :], ps[0:m, 1 + 2 * (i % 3), :], func,
                                   bias=gate_b[0:m, i:i + 1] if biased else 0.0).then_inc(gated.sem, 1)
                copy_next(n)

        @block.vector
        def _(dve):
            ph.start(dve, "dve")
            dve.wait_ge(loaded, 16 * len(loads))
            dve.wait_ge(prepared, 1)

            def moments_of(n):
                dve.wait_ge(*h_loaded.at(n, 32 * NH))
                for t in range(GT):
                    dve.bn_stats(stats[:, t, :], h[:, t, :]).then_inc(stats_done.sem, 1)
                dve.wait_ge(*stats_done.at(n, 2 * GT))
                dve.sem_inc(seen, 1)
                for t in range(GT):
                    dve.bn_aggr(mv[:, t, :], stats[:, t, :]).then_inc(moments.sem, 1)
                dve.wait_ge(*moments.at(n, 2 * GT))
                if layernorm:
                    dve.tensor_scalar(ms[:, 1, :], mv[:, :, 1], eps, None, ALU.add).then_inc(under_root.sem, 3)
                else:
                    dve.tensor_tensor(ms[:, 0, :], mv[:, :, 0], mv[:, :, 0], ALU.mult).then_inc(under_root.sem, 1)
                    dve.wait_ge(*under_root.at(n, 4))
                    dve.tensor_tensor(ms[:, 0, :], ms[:, 0, :], mv[:, :, 1], ALU.add).then_inc(under_root.sem, 1)
                    dve.wait_ge(*under_root.at(n, 5))
                    dve.tensor_scalar(ms[:, 1, :], ms[:, 0, :], eps, None, ALU.add).then_inc(under_root.sem, 1)

            def norm(n):
                dve.wait_ge(*root.at(n, 2))
                dve.wait_ge(*ht_ps.at(n, 1))
                for t in range(GT):
                    if layernorm:
                        dve.tensor_scalar(hn[:, t, :], h[:, t, :], mv[:, t, 0:1], rstd[:, t:t + 1], ALU.subtract, ALU.mult)\
                            .then_inc(normed.sem, 1)
                    else:
                        dve.tensor_scalar(hn[:, t, :], h[:, t, :], rstd[:, t:t + 1], None, ALU.mult)\
                            .then_inc(normed.sem, 1)

            moments_of(0)
            norm(0)
            with dve.Fori(0, NB) as b, dve.Fori(0, NG) as g:
                n = dve.snap(b * NG + g + 1)
                for i, (a, m) in enumerate(chunks):
                    dve.wait_ge(*gated.at(n, i + 1))
                    if i == 0:
                        dve.wait_ge(*y_ps.at(n, 0))
                    up = ps[0:m, 2 + 2 * (i % 3), :]
                    if biased:
                        dve.scalar_tensor_tensor(out=prod[0:m, i, :], in0=up, scalar=up_b[0:m, i:i + 1],
                                                 in1=gate[0:m, i % 2, :], op0=ALU.add, op1=ALU.mult).then_inc(prod_sb.sem, 1)
                    else:
                        dve.tensor_tensor(prod[0:m, i, :], up, gate[0:m, i % 2, :], ALU.mult).then_inc(prod_sb.sem, 1)
                    if i == 0:
                        moments_of(n)
                    if i == NC - 2:
                        norm(n)
                dve.wait_ge(*x_loaded.at(n, 16 * NX))
                dve.wait_ge(*stored.at(n, 0))
                dve.wait_ge(*y_ps.at(n, 1))
                dve.tensor_tensor(y[:], ps[:, 7, :].rearrange("p (t d) -> p t d", d=D), x[:], ALU.add).then_inc(y_sb.sem, 1)
                if skip is not None:
                    dve.wait_ge(*y_sb.at(n, 1))
                    dve.tensor_tensor(y[:], y[:], x2[:], ALU.add).then_inc(y_sb.sem, 1)
    ph.close()


def add_and_norm(nc, name, a, b_, x_out, y_out, c):
    ph = Phase(nc, name)
    sb, signal = ph.sb, ph.counter
    minus_half = sb("minus_half", [P, GT])
    x = sb("x", [P, NG, GT, D])
    more = sb("more", [P, NG, GT, D])
    total = sb("total", [P, NG, GT, D])
    y = sb("y", [P, NG, GT, D])
    stats = sb("stats", [P, NG, GT, 6])
    mv = sb("mv", [P, NG, GT, 2])
    var = sb("var", [P, NG, GT])
    rstd = sb("rstd", [P, NG, GT])
    const_loaded = ph.semaphore("const_loaded")
    N_IN = 1 + (b_ is not None)
    N_OUT = (x_out is not None) + (y_out is not None)
    loaded = [signal(f"loaded{g}", 16 * N_IN, "sp") for g in range(NG)]
    stored = [signal(f"stored{g}", 16 * N_OUT, "sp") for g in range(NG)]
    added = signal("added", NG, "dve")
    stats_done = signal("stats_done", NG * GT, "dve")
    seen = signal("seen", 1, "dve").sem
    moments = signal("moments", NG * GT, "dve")
    under_root = signal("under_root", NG, "dve")
    root = signal("root", NG, "pool")
    normed = signal("normed", NG * GT, "dve")

    with nc.Block() as block:

        @block.sync
        def _(sp):
            ph.start(sp, "sp")
            sp.dma_start(minus_half[:], c["minus_half"][:, 0:GT]).then_inc(const_loaded, 16)

            def load(b, g):
                sp.dma_start(x[:, g], tiles(a[0][bass.ds(a[1](b, g), G), :])).then_inc(loaded[g].sem, 16)
                if b_ is not None:
                    sp.dma_start(more[:, g], tiles(b_[0][bass.ds(b_[1](b, g), G), :])).then_inc(loaded[g].sem, 16)

            for g in range(NG):
                load(0, g)
            with sp.Fori(0, NB) as b:
                n = sp.snap(b + 1)
                following = sp.snap(n % NB)
                for g in range(NG):
                    sp.wait_ge(*added.at(n, g + 1))
                    if x_out is not None:
                        sp.dma_start(tiles(x_out[0][bass.ds(x_out[1](b, g), G), :]), total[:, g]).then_inc(stored[g].sem, 16)
                    load(following, g)
                    if y_out is not None:
                        sp.wait_ge(*normed.at(n, (g + 1) * GT))
                        sp.dma_start(tiles(y_out[0][bass.ds(y_out[1](b, g), G), :]), y[:, g]).then_inc(stored[g].sem, 16)
            for g in range(NG):
                sp.wait_ge(*stored[g].at(NB + 1, 0))
                sp.wait_ge(*loaded[g].at(NB + 1, 16 * N_IN))

        @block.gpsimd
        def _(pool):
            ph.start(pool, "pool")
            pool.wait_ge(const_loaded, 16)
            if y_out is not None:
                with pool.Fori(0, NB) as b:
                    n = pool.snap(b + 1)
                    for g in range(NG):
                        pool.wait_ge(*under_root.at(n, g + 1))
                        pool.tensor_tensor(rstd[:, g], var[:, g], minus_half[:], ALU.pow).then_inc(root.sem, 1)

        @block.vector
        def _(dve):
            ph.start(dve, "dve")
            with dve.Fori(0, NB) as b:
                n = dve.snap(b + 1)
                for g in range(NG):
                    dve.wait_ge(*loaded[g].at(n, 16 * N_IN))
                    dve.wait_ge(*stored[g].at(n, 0))
                    if b_ is not None:
                        dve.tensor_tensor(total[:, g], x[:, g], more[:, g], ALU.add).then_inc(added.sem, 1)
                    else:
                        dve.tensor_copy(total[:, g], x[:, g]).then_inc(added.sem, 1)
                    if y_out is not None:
                        dve.wait_ge(*added.at(n, g + 1))
                        for t in range(GT):
                            dve.bn_stats(stats[:, g, t, :], total[:, g, t, :]).then_inc(stats_done.sem, 1)
                        dve.wait_ge(*stats_done.at(n, (g + 1) * GT))
                        dve.sem_inc(seen, 1)
                        for t in range(GT):
                            dve.bn_aggr(mv[:, g, t, :], stats[:, g, t, :]).then_inc(moments.sem, 1)
                        dve.wait_ge(*moments.at(n, (g + 1) * GT))
                        dve.tensor_scalar(var[:, g], mv[:, g, :, 1], 1e-5, None, ALU.add).then_inc(under_root.sem, 1)
                if y_out is not None:
                    for g in range(NG):
                        dve.wait_ge(*root.at(n, g + 1))
                        for t in range(GT):
                            dve.tensor_scalar(y[:, g, t, :], total[:, g, t, :], mv[:, g, t, 0:1], rstd[:, g, t:t + 1],
                                              ALU.subtract, ALU.mult).then_inc(normed.sem, 1)
    ph.close()


def token_row(b, g):
    return (b * NG + g) * G


def clear_padding(nc, arrays, c):
    ph = Phase(nc, "padding")
    cleared = ph.semaphore("cleared")
    with nc.Block() as block:
        @block.sync
        def _(sp):
            for a in arrays:
                sp.dma_start(a.rearrange("(b r) c -> b r c", b=NB)[:, PAD - 1, :], c["zero_rows"]).then_inc(cleared, 16)
            sp.wait_ge(cleared, 16 * len(arrays))
    ph.close()


def ffn_block(nc, name, y0, y1, w, c):
    HID = w["w2"].shape[0] // DEPTH
    with nc.Fori(0, DEPTH) as l:
        local_attention(nc, name + "a", y0, y1, l, w, c)
        gated_mlp(nc, name + "m", y1, y0, c, HID, ACT.Gelu, True, 1e-5,
                  w_up=w["w1"][bass.ds(l * D, D), 0:HID], w_gate=w["w1"][bass.ds(l * D, D), HID:2 * HID],
                  w_down=lambda a, m: w["w2"][bass.ds(l * HID + a, m), :],
                  norm_w=w["ln_g"][bass.ds(l * D, D), :], norm_b=w["ln_b"][bass.ds(l * D, D), :],
                  b_up=lambda a, m: w["b1"][bass.ds(l * 2 * HID + a, m), :],
                  b_gate=lambda a, m: w["b1"][bass.ds(l * 2 * HID + HID + a, m), :],
                  b_down=w["b2"][bass.ds(l, 1), :], shifted=True)


def hybrid_block(nc, x, a, b, f, c, out):
    def scratch(name):
        return nc.dram_tensor(name, (NB * ROWS, D), F32).ap()
    x1, x2, x3, y0, y1 = (scratch(n) for n in ("x1", "x2", "x3", "y0", "y1"))
    clear_padding(nc, (y0, y1), c)
    delta_attention(nc, "delta", x, y0, a, c)
    gated_mlp(nc, "mlp", y0, x1, c, a["Wup"].shape[1], ACT.Silu, False, 1e-6, w_up=a["Wup"], w_gate=a["Wgate"],
              w_down=lambda r, m: a["Wdown"][r:r + m, :], norm_w=a["norm2_w"], skip=x)
    add_and_norm(nc, "norm_a", (x1, scratch_row), None, None, (y0, scratch_row), c)
    ffn_block(nc, "f", y0, y1, f, c)
    add_and_norm(nc, "norm_b", (x1, scratch_row), (y0, scratch_row), (x2, scratch_row), (y1, scratch_row), c)
    window_attention(nc, "window", y1, x2, x3, b, c)
    add_and_norm(nc, "norm_c", (x3, scratch_row), None, None, (y0, scratch_row), c)
    ffn_block(nc, "g", y0, y1, f, c)
    add_and_norm(nc, "last", (x3, scratch_row), (y0, scratch_row), (out, token_row), None, c)



def shape_constants():
    import numpy as np

    T, P, W, DH = 1024, 128, 64, 64
    c = {"ident": np.eye(P, dtype=np.float32)}
    c["minus_half"] = np.full((P, 64), -0.5, np.float32)
    c["own_head"] = (np.arange(P)[:, None] // 8 % 4 == np.arange(4)[None, :]).astype(np.float32)
    i = np.arange(P)
    c["sums"] = np.concatenate([i[:, None] <= i, np.ones((P, P)), i[:, None] > i], 1).astype(np.float32)
    c["not_first"] = (i[:, None] > 0).astype(np.float32)
    levels = []
    for m in range(7):
        s = 1 << m
        cols = i[i // s % 2 == 0]
        levels.append(-((i[:, None] // s % 2 == 1) & (i[:, None] // (2 * s) == cols // (2 * s))).astype(np.float32))
    c["blocks"] = np.concatenate(levels, 1)
    c["zero_rows"] = np.zeros((4, 128), np.float32)
    q = np.arange(P)[:, None]
    k = np.arange(W + P)[None, :]
    for name, first in (("ffn_mask", q), ("attn_mask", q + 1)):
        seen = (k >= first) & (k <= q + W)
        edge = seen & (k >= W)
        m = np.where(np.stack([edge, edge, seen, seen], 1), 0.0, -1e30)
        c[name] = np.ascontiguousarray(m.reshape(P, 4 * (W + P)).astype(np.float32))
    half = np.arange(0, DH, 2, dtype=np.float32)
    inv_freq = (1.0 / 10000.0 ** (half / DH)).astype(np.float32)
    t = np.arange(T, dtype=np.float32)
    f = (t[:, None] * inv_freq[None, :]).astype(np.float32)
    f = np.concatenate([f, f], 1)
    base = ((half + 0.4 * DH) / (1.4 * DH)).astype(np.float32)
    s = (base[None, :] ** ((t - T // 2) / float(W // 2))[:, None]).astype(np.float32)
    s = np.concatenate([s, s], 1)
    sign = np.where(np.arange(DH) < DH // 2, -1.0, 1.0).astype(np.float32)
    cos, sin = np.cos(f), np.sin(f) * sign
    r = np.stack([cos * s * 8.0, sin * s * 8.0, cos / s, sin / s]).astype(np.float32)
    c["rotation"] = np.ascontiguousarray(r.reshape(4, T // P, P, DH).transpose(2, 0, 1, 3).reshape(P, 4 * (T // P) * DH))
    return c


def kernel(**inputs):
    import numpy as np
    import concourse.bacc as bacc
    from concourse import mybir as mb
    from concourse.bass_utils import run_bass_kernel_spmd

    nc = bacc.Bacc("TRN2", target_bir_lowering=False, num_devices=1)
    arrays = {}

    def give(name, array):
        arrays[name] = np.ascontiguousarray(array)
        return nc.dram_tensor(name, arrays[name].shape, mb.dt.from_np(arrays[name].dtype), kind="ExternalInput").ap()

    def group(prefix):
        given = {}
        for name, array in inputs.items():
            if name.startswith(prefix) and not name.endswith("_x"):
                key, array = name[len(prefix):], np.asarray(array)
                if prefix == "L0_attn_b_" and key.startswith("W"):
                    array = array.T
                elif key in ("A_log", "dt_bias", "bo"):
                    array = array.reshape(1, -1)
                elif array.ndim == 1 or key in ("ln_g", "ln_b", "b1"):
                    array = array.reshape(-1, 1)
                elif array.ndim == 3:
                    array = array.reshape(-1, array.shape[-1])
                given[key] = give(name, array)
        return given

    x = np.asarray(inputs["L0_attn_a_x"])
    shape = x.shape
    x = give("x", x.reshape(-1, shape[-1]))
    a, b, f = (group(p) for p in ("L0_attn_a_", "L0_attn_b_", "L0_ffn_"))
    c = {name: give("const_" + name, array) for name, array in shape_constants().items()}
    out = nc.dram_tensor("out", (shape[0] * shape[1], shape[2]), mb.dt.float32, kind="ExternalOutput").ap()
    hybrid_block(nc, x, a, b, f, c, out)
    r = run_bass_kernel_spmd(nc, [arrays], core_ids=[0])
    return r.results[0]["out"].reshape(shape)
```
